# Optimizing a Trainium2 kernel written in Bass

```python
import numpy as np
import jax
import jax.numpy as jnp

def _softmax(x, axis=-1):
    return jax.nn.softmax(x, axis=axis)

def _gelu(x):
    return jax.nn.gelu(x, approximate=True)

def _silu(x):
    return jax.nn.silu(x)

def _sigmoid(x):
    return jax.nn.sigmoid(x)

def _layernorm(x, axis=-1, eps=1e-05):
    m = jnp.mean(x, axis=axis, keepdims=True)
    v = jnp.var(x, axis=axis, keepdims=True)
    return (x - m) / jnp.sqrt(v + eps)

def _scatter_add(tgt, idx, src, axis=0):
    return tgt.at[idx].add(src)

def _segment_sum(src, seg, n):
    return jax.ops.segment_sum(src, seg, n)
kernel_name = 'mk_prb_d2_jaxref_r4_dbab8c'

def setup_inputs(seed: int=0):
    np.random.seed(seed)
    _w = jnp.asarray

    def _L0_attn_setup():
        import jax, jax.numpy as jnp
        import numpy as np
        D_MODEL = 256
        STATE_DIM = 16
        BATCH = 32
        SEQ = 512

        def _selective_scan(delta, A, B, C):

            def step(state, inp):
                delta_t, B_t, C_t = inp
                state = jnp.exp(A * delta_t) * state + B_t
                y = jnp.sum(state * C_t, axis=-1)
                return (state, y)
            b = delta.shape[0]
            init = jnp.zeros((b, A.shape[0]), dtype=delta.dtype)
            xs = (jnp.swapaxes(delta, 0, 1), jnp.swapaxes(B, 0, 1), jnp.swapaxes(C, 0, 1))
            _, ys = jax.lax.scan(step, init, xs)
            return jnp.swapaxes(ys, 0, 1)
        key = jax.random.key(seed)
        k_x, k_win, k_bin, k_wout, k_bout = jax.random.split(key, 5)
        proj_dim = 2 * D_MODEL + 3 * STATE_DIM
        x = jax.random.normal(k_x, (BATCH, SEQ, D_MODEL), dtype=jnp.float32)
        W_in = jax.random.normal(k_win, (D_MODEL, proj_dim), dtype=jnp.float32) * 0.02
        b_in = jnp.zeros((proj_dim,), dtype=jnp.float32)
        W_out = jax.random.normal(k_wout, (D_MODEL, D_MODEL), dtype=jnp.float32) * 0.02
        b_out = jnp.zeros((D_MODEL,), dtype=jnp.float32)
        A_log = -jnp.log(jnp.arange(1, STATE_DIM + 1, dtype=jnp.float32))
        return {'x': x, 'W_in': W_in, 'b_in': b_in, 'A_log': A_log, 'W_out': W_out, 'b_out': b_out}
    _L0_attn_in = _L0_attn_setup()

    def _L0_ffn_setup():
        import jax, jax.numpy as jnp
        import numpy as np
        B, S, H, I, E_ROUTED, TOP_K = (8, 512, 256, 512, 8, 2)

        def _expert(x, Wg, Wu, Wd):
            return jax.nn.silu(x @ Wg.T) * (x @ Wu.T) @ Wd.T
        key = jax.random.key(seed)
        ks = jax.random.split(key, 9)
        s = 0.02
        return {'x': jax.random.normal(ks[0], (B, S, H), dtype=jnp.float32), 'Wg_s': jax.random.normal(ks[1], (I, H), dtype=jnp.float32) * s, 'Wu_s': jax.random.normal(ks[2], (I, H), dtype=jnp.float32) * s, 'Wd_s': jax.random.normal(ks[3], (H, I), dtype=jnp.float32) * s, 'Wg': jax.random.normal(ks[4], (E_ROUTED, I, H), dtype=jnp.float32) * s, 'Wu': jax.random.normal(ks[5], (E_ROUTED, I, H), dtype=jnp.float32) * s, 'Wd': jax.random.normal(ks[6], (E_ROUTED, H, I), dtype=jnp.float32) * s, 'Wr': jax.random.normal(ks[7], (E_ROUTED, H), dtype=jnp.float32) * s, 'rb': jnp.zeros((E_ROUTED,), dtype=jnp.float32)}
    _L0_ffn_in = _L0_ffn_setup()

    def _L1_attn_setup():
        import jax, jax.numpy as jnp
        import numpy as np
        import math

        def _alibi_slopes(n_heads):

            def pow2(n):
                start = 2 ** (-2 ** (-(math.log2(n) - 3)))
                return [start ** i for i in range(n)]
            if math.log2(n_heads).is_integer():
                slopes = pow2(n_heads)
            else:
                closest = 2 ** math.floor(math.log2(n_heads))
                slopes = pow2(closest) + _alibi_slopes(2 * closest).tolist()[0::2][:n_heads - closest]
            return np.asarray(slopes, dtype=np.float32)
        key = jax.random.key(seed)
        ks = jax.random.split(key, 4)
        B, L, D = (2, 512, 256)
        s = 1.0 / math.sqrt(D)
        return {'x': jax.random.normal(ks[0], (B, L, D), jnp.float32), 'Wqkv': jax.random.normal(ks[1], (D, 3 * D), jnp.float32) * s, 'bqkv': jnp.zeros((3 * D,), jnp.float32), 'Wout': jax.random.normal(ks[2], (D, D), jnp.float32) * s, 'bout': jnp.zeros((D,), jnp.float32)}
    _L1_attn_in = _L1_attn_setup()

    def _L1_ffn_setup():
        import jax, jax.numpy as jnp
        import numpy as np
        NUM_GROUPS = 2
        EXPERT_CAPACITY = 160
        NUM_SELECTED = 2
        key = jax.random.key(seed)
        k1, k2, k3, k4 = jax.random.split(key, 4)
        B, S, H, E, F = (4, 512, 256, 8, 1024)
        return {'input_emb': jax.random.normal(k1, (B, S, H), dtype=jnp.float32), 'w_router': jax.random.normal(k2, (H, E), dtype=jnp.float32) * 0.02, 'wi': jax.random.normal(k3, (E, H, F), dtype=jnp.float32) * 0.02, 'wo': jax.random.normal(k4, (E, F, H), dtype=jnp.float32) * 0.02}
    _L1_ffn_in = _L1_ffn_setup()
    _d = {'L0_attn_x': _L0_attn_in['x'], 'L0_attn_W_in': _L0_attn_in['W_in'], 'L0_attn_b_in': _L0_attn_in['b_in'], 'L0_attn_A_log': _L0_attn_in['A_log'], 'L0_attn_W_out': _L0_attn_in['W_out'], 'L0_attn_b_out': _L0_attn_in['b_out'], 'L0_ffn_Wg_s': _L0_ffn_in['Wg_s'], 'L0_ffn_Wu_s': _L0_ffn_in['Wu_s'], 'L0_ffn_Wd_s': _L0_ffn_in['Wd_s'], 'L0_ffn_Wg': _L0_ffn_in['Wg'], 'L0_ffn_Wu': _L0_ffn_in['Wu'], 'L0_ffn_Wd': _L0_ffn_in['Wd'], 'L0_ffn_Wr': _L0_ffn_in['Wr'], 'L0_ffn_rb': _L0_ffn_in['rb'], 'L1_attn_Wqkv': _L1_attn_in['Wqkv'], 'L1_attn_bqkv': _L1_attn_in['bqkv'], 'L1_attn_Wout': _L1_attn_in['Wout'], 'L1_attn_bout': _L1_attn_in['bout'], 'L1_ffn_w_router': _L1_ffn_in['w_router'], 'L1_ffn_wi': _L1_ffn_in['wi'], 'L1_ffn_wo': _L1_ffn_in['wo']}
    _x0 = _d['L0_attn_x']
    _d['L0_attn_x'] = jax.random.normal(jax.random.fold_in(jax.random.key(seed), 1), (4, 1024, 256), dtype=_x0.dtype)
    del _x0
    return _d

def reference(L0_attn_x, L0_attn_W_in, L0_attn_b_in, L0_attn_A_log, L0_attn_W_out, L0_attn_b_out, L0_ffn_Wg_s, L0_ffn_Wu_s, L0_ffn_Wd_s, L0_ffn_Wg, L0_ffn_Wu, L0_ffn_Wd, L0_ffn_Wr, L0_ffn_rb, L1_attn_Wqkv, L1_attn_bqkv, L1_attn_Wout, L1_attn_bout, L1_ffn_w_router, L1_ffn_wi, L1_ffn_wo):

    def _L0_attn_ref(x, W_in, b_in, A_log, W_out, b_out):
        import jax, jax.numpy as jnp
        import numpy as np
        D_MODEL = 256
        STATE_DIM = 16
        BATCH = 32
        SEQ = 512

        def _selective_scan(delta, A, B, C):

            def step(state, inp):
                delta_t, B_t, C_t = inp
                state = jnp.exp(A * delta_t) * state + B_t
                y = jnp.sum(state * C_t, axis=-1)
                return (state, y)
            b = delta.shape[0]
            init = jnp.zeros((b, A.shape[0]), dtype=delta.dtype)
            xs = (jnp.swapaxes(delta, 0, 1), jnp.swapaxes(B, 0, 1), jnp.swapaxes(C, 0, 1))
            _, ys = jax.lax.scan(step, init, xs)
            return jnp.swapaxes(ys, 0, 1)
        xz = jnp.einsum('bsd,dp->bsp', x, W_in) + b_in
        d, n = (D_MODEL, STATE_DIM)
        xm = xz[..., :d]
        z = xz[..., d:2 * d]
        Bm = xz[..., 2 * d:2 * d + n]
        Cm = xz[..., 2 * d + n:2 * d + 2 * n]
        delta = jax.nn.softplus(xz[..., 2 * d + 2 * n:])
        A = -jnp.exp(A_log)
        y = _selective_scan(delta, A, Bm, Cm)
        y = y[..., None] * jax.nn.gelu(z, approximate=False)
        return jnp.einsum('bsd,de->bse', y, W_out) + b_out

    def _L0_ffn_ref(x, Wg_s, Wu_s, Wd_s, Wg, Wu, Wd, Wr, rb):
        import jax, jax.numpy as jnp
        import numpy as np
        B, S, H, I, E_ROUTED, TOP_K = (8, 512, 256, 512, 8, 2)

        def _expert(x, Wg, Wu, Wd):
            return jax.nn.silu(x @ Wg.T) * (x @ Wu.T) @ Wd.T
        shared = _expert(x, Wg_s, Wu_s, Wd_s)
        logits = jnp.einsum('bsh,eh->bse', x, Wr) + rb
        probs = jax.nn.sigmoid(logits)
        scores, idx = jax.lax.top_k(probs, TOP_K)
        cw = (jax.nn.one_hot(idx, E_ROUTED, dtype=x.dtype) * scores[..., None]).sum(-2)
        out = shared
        for e in range(E_ROUTED):
            out = out + cw[..., e:e + 1] * _expert(x, Wg[e], Wu[e], Wd[e])
        return out

    def _L1_attn_ref(x, Wqkv, bqkv, Wout, bout):
        import jax, jax.numpy as jnp
        import numpy as np
        import math

        def _alibi_slopes(n_heads):

            def pow2(n):
                start = 2 ** (-2 ** (-(math.log2(n) - 3)))
                return [start ** i for i in range(n)]
            if math.log2(n_heads).is_integer():
                slopes = pow2(n_heads)
            else:
                closest = 2 ** math.floor(math.log2(n_heads))
                slopes = pow2(closest) + _alibi_slopes(2 * closest).tolist()[0::2][:n_heads - closest]
            return np.asarray(slopes, dtype=np.float32)
        n_heads = 16
        B, L, D = x.shape
        head_dim = D // n_heads
        qkv = (x @ Wqkv + bqkv).reshape(B, L, 3, n_heads, head_dim)
        q, k, v = (qkv[:, :, 0], qkv[:, :, 1], qkv[:, :, 2])
        scores = jnp.einsum('bqhd,bkhd->bhqk', q, k) / math.sqrt(head_dim)
        pos = jnp.arange(L)
        bias = -jnp.abs(pos[None, :] - pos[:, None]).astype(jnp.float32)
        slopes = jnp.asarray(_alibi_slopes(n_heads))
        scores = scores + slopes[None, :, None, None] * bias[None, None]
        probs = jax.nn.softmax(scores, axis=-1)
        out = jnp.einsum('bhqk,bkhd->bqhd', probs, v).reshape(B, L, D)
        return out @ Wout + bout

    def _L1_ffn_ref(input_emb, w_router, wi, wo):
        import jax, jax.numpy as jnp
        import numpy as np
        NUM_GROUPS = 2
        EXPERT_CAPACITY = 160
        NUM_SELECTED = 2
        B, S, H = input_emb.shape
        E = w_router.shape[1]
        G = NUM_GROUPS
        T = B * S // G
        C = EXPERT_CAPACITY
        K = NUM_SELECTED
        x = input_emb.reshape(G, T, H)
        router_logits = jnp.einsum('gth,he->gte', x.astype(jnp.float32), w_router.astype(jnp.float32))
        router_probs = jax.nn.softmax(router_logits, axis=-1)
        gate, idx = jax.lax.top_k(router_probs, K)
        mask = jax.nn.one_hot(idx, E, dtype=jnp.float32)
        mask_kt = jnp.swapaxes(mask, 1, 2).reshape(G, K * T, E)
        pos = jnp.cumsum(mask_kt, axis=1) * mask_kt - 1.0
        pos = jnp.swapaxes(pos.reshape(G, K, T, E), 1, 2)
        disp_k = jax.nn.one_hot(pos, C, dtype=jnp.float32) * mask[..., None]
        dispatch = disp_k.sum(axis=2)
        combine = jnp.einsum('gtk,gtkec->gtec', gate, disp_k)
        expert_in = jnp.einsum('gtec,gth->egch', dispatch, x)
        h = jax.nn.relu(jnp.einsum('egch,ehf->egcf', expert_in, wi))
        expert_out = jnp.einsum('egcf,efh->egch', h, wo)
        y = jnp.einsum('gtec,egch->gth', combine, expert_out)
        return y.reshape(B, S, H)
    x = L0_attn_x
    xn = _layernorm(x, axis=-1)
    x = x + _L0_attn_ref(xn, L0_attn_W_in, L0_attn_b_in, L0_attn_A_log, L0_attn_W_out, L0_attn_b_out) + _L0_ffn_ref(xn, L0_ffn_Wg_s, L0_ffn_Wu_s, L0_ffn_Wd_s, L0_ffn_Wg, L0_ffn_Wu, L0_ffn_Wd, L0_ffn_Wr, L0_ffn_rb)
    xn = _layernorm(x, axis=-1)
    x = x + _L1_attn_ref(xn, L1_attn_Wqkv, L1_attn_bqkv, L1_attn_Wout, L1_attn_bout) + _L1_ffn_ref(xn, L1_ffn_w_router, L1_ffn_wi, L1_ffn_wo)
    return x

_drawn_inputs = setup_inputs


def setup_inputs(seed=0):
    import zlib

    import numpy as np

    out = dict(_drawn_inputs(seed))
    spreads = {'L0_attn_b_in': (0.0, 0.1),
     'L0_attn_b_out': (0.0, 0.1),
     'L0_ffn_rb': (0.0, 0.737),
     'L1_attn_bqkv': (0.0, 0.1),
     'L1_attn_bout': (0.0, 0.1)}
    factors = {'L0_ffn_Wg': 2.769,
     'L0_ffn_Wu': 2.746,
     'L0_ffn_Wd': 2.74,
     'L0_ffn_Wr': 3.223,
     'L1_ffn_w_router': 2.911,
     'L1_ffn_wi': 3.265,
     'L1_ffn_wo': 2.717}
    for name, (base, spread) in spreads.items():
        noise = np.random.default_rng([zlib.crc32(name.encode()), seed]).standard_normal(out[name].shape)
        drawn = base * np.exp(spread * noise) if base else spread * noise
        out[name] = jnp.asarray(drawn.astype(out[name].dtype))
    for name, factor in factors.items():
        out[name] = (out[name] * factor).astype(out[name].dtype)
    return out
```

```python
import concourse.bass as bass
from concourse import mybir
from concourse.alu_op_type import AluOpType as ALU
from contextlib import ExitStack

F32 = mybir.dt.float32
BF16 = mybir.dt.bfloat16
I32 = mybir.dt.int32
ACT = mybir.ActivationFunctionType
AX = mybir.AxisListType

P = 128
BATCH, SEQ, D = 4, 1024, 256
TOK = BATCH * SEQ
NT = TOK // P
HC = D // P
N_STATE = 16
E = 8
I0 = 512
F1 = 1024
BLOCKS0 = 2 * NT + E
G1, CAP = 2, 160
SLOTS1 = G1 * CAP
BLOCKS1 = E * SLOTS1 // P
HEADS, HD = 16, 16
EPS = 1e-5


class Chain:

    def __init__(self, engine, sem):
        self.engine, self.sem, self.n = engine, sem, 0

    def __call__(self, instruction):
        self.n += 1
        instruction.then_inc(self.sem, 1)
        self.engine.wait_ge(self.sem, self.n)


class Memory:

    def __init__(self, nc, stack):
        self.nc, self.stack, self.semaphores = nc, stack, []

    def sb(self, name, shape, dt=F32):
        return self.stack.enter_context(self.nc.sbuf_tensor(name, shape, dt))

    def sem(self, name):
        self.semaphores.append(self.stack.enter_context(self.nc.semaphore(name)))
        return self.semaphores[-1]

    def sems(self, name, n):
        return [self.sem(f"{name}{i}") for i in range(n)]


def phase(nc):
    return _Phase(nc)


class _Phase(ExitStack):
    def __init__(self, nc):
        super().__init__()
        self.nc, self.memory, self.block = nc, Memory(nc, self), ExitStack()

    def __exit__(self, *error):
        self.block.close()
        if error[0] is None:
            with self.nc.Block() as block:
                @block.sync
                def _(sp):
                    for s in self.memory.semaphores:
                        sp.sem_clear(s)
        return super().__exit__(*error)


def software_pipelined(engine, count, produce, consume):
    produce(0, 0, 0)
    with engine.Fori(0, count // 2 - 1) as j:
        produce(j * 2 + 1, 1, j)
        consume(j * 2, 0, j)
        produce(j * 2 + 2, 0, j + 1)
        consume(j * 2 + 1, 1, j)
    produce(count - 1, 1, count // 2 - 1)
    consume(count - 2, 0, count // 2 - 1)
    consume(count - 1, 1, count // 2 - 1)


def by_twos(engine, count, step):
    with engine.Fori(0, count // 2) as j:
        step(j * 2, 0, j)
        step(j * 2 + 1, 1, j)


def made(i):
    return i + 3


def reusable(i):
    return i + 1


def stored(turn):
    return turn * 16 + 32


def storable(turn):
    return turn * 16 + 16


def spread(ap, axis, shape):
    return ap.unsqueeze(axis).to_broadcast(shape)


def norm_and_route(nc, L, x_src, X, xnT, xn_dram, wr_src, bias, const, route, v_out=None):
    G = 1 if L == 0 else G1
    TG = NT // G
    NC = 2 * NT
    NCE = E * NC
    NB = BLOCKS0 if L == 0 else BLOCKS1
    with phase(nc) as stack:
        m = stack.memory
        st = m.sb(f"stats{L}", [P, NT, 6])
        sd = m.sb(f"mean_diff{L}", [P, NT])
        mean = m.sb(f"mean{L}", [P, NT])
        var = m.sb(f"var{L}", [P, NT])
        root = m.sb(f"root{L}", [P, NT])
        quot = m.sb(f"quot{L}", [P, NT])
        rstd = m.sb(f"rstd{L}", [P, NT])
        xn = [m.sb(f"xn_stage{L}_{s}", [P, D]) for s in range(2)]
        xt = [m.sb(f"xt_stage{L}_{s}", [P, HC, P]) for s in range(2)]
        wr = m.sb(f"w_router{L}", [P, HC, E])
        LG = m.sb(f"logits{L}", [P, NT, E])
        PR = m.sb(f"scores{L}", [P, NT, E])
        A1 = m.sb(f"work_a{L}", [P, NT, E])
        A2 = m.sb(f"work_b{L}", [P, NT, E])
        pick = m.sb(f"pick{L}", [P, NT])
        OH = m.sb(f"onehot{L}", [P, G, E, 2, TG])
        OHb = m.sb(f"onehot_bf{L}", [P, NCE], BF16)
        T = m.sb(f"totals{L}", [P, NCE])
        S = m.sb(f"totals_up_to{L}", [P, NCE])
        R = m.sb(f"rank{L}", [P, NCE])
        over = m.sb(f"count_over{L}", [P, E, NT])
        nblk = m.sb(f"expert_blocks{L}", [P, E])
        ends = m.sb(f"expert_end{L}", [P, E])
        base = m.sb(f"expert_base{L}", [P, E])
        after = m.sb(f"block_after{L}", [P, BLOCKS0, E])
        blk_e = m.sb(f"block_expert_f{L}", [P, BLOCKS0])
        dest = m.sb(f"dest{L}", [P, NC])
        keep = m.sb(f"keep{L}", [P, NC])
        row_i = m.sb(f"row_i{L}", [P, NC], I32)
        lo_i = m.sb(f"row_in_block_i{L}", [P, NC], I32)
        hi_i = m.sb(f"row_block_i{L}", [P, NC], I32)
        lo = m.sb(f"row_in_block{L}", [P, NC])
        hi = m.sb(f"row_block{L}", [P, NC])
        hot_row = [m.sb(f"hot_row{L}_{s}", [P, P], BF16) for s in range(2)]
        hot_block = [m.sb(f"hot_block{L}_{s}", [P, 2, NB], BF16) for s in range(2)]
        zeros = m.sb(f"zeros_bf{L}", [P, 2 * NB], BF16)
        table = m.sb(f"table{L}", [P, 2, NB])
        x_loaded = m.sems(f"x_loaded{L}_", 4)
        wr_loaded, chain = m.sem(f"wr_loaded{L}"), m.sem(f"dve_chain{L}")
        stats_made = m.sem(f"stats_made{L}")
        var_ready, root_ready = m.sem(f"var_ready{L}"), m.sem(f"root_ready{L}")
        xn_ready, xn_stored = m.sem(f"xn_ready{L}"), m.sems(f"xn_stored{L}_", 2)
        xt_done, xt_ready, xt_copied = m.sem(f"xt_done{L}"), m.sem(f"xt_ready{L}"), m.sem(f"xt_copied{L}")
        lg_done, lg_read = m.sem(f"lg_done{L}"), m.sem(f"lg_read{L}")
        exp_wanted, exp_ready = m.sem(f"exp_wanted{L}"), m.sem(f"exp_ready{L}")
        oh_ready, rank_done = m.sem(f"oh_ready{L}"), m.sem(f"rank_done{L}")
        zeros_ready, hot_ready, hot_used, table_done = (
            m.sem(f"zeros_ready{L}"), m.sem(f"hot_ready{L}"), m.sem(f"hot_used{L}"), m.sem(f"table_done{L}"))
        ps = stack.enter_context(nc.psum_tensor(f"ps_route{L}", [P, 8, 512], F32))
        ps_xt = [ps[:, s, 0:D].rearrange("p (c t) -> p c t", c=HC) for s in range(2)]
        ps_lg = [ps[:, 2 + s, 0:E] for s in range(2)]
        ps_v = [ps[:, 4 + s, 0:D] for s in range(2)]
        ps_rank, ps_total = ps[:, 6, :], ps[:, 7, :]
        ps_table = ps[:, 2, 0:2 * NB]
        block = stack.block.enter_context(nc.Block())

        @block.sync
        def _(sp):
            if x_src is not None:
                n = NT // 4
                for c in range(4):
                    sp.dma_start(X[:, c * n:(c + 1) * n, :], x_src[:, c * n:(c + 1) * n, :]).then_inc(x_loaded[c], 16)
            sp.dma_start(wr[:], wr_src).then_inc(wr_loaded, 16)
            for s in range(2):
                sp.sem_inc(xn_stored[s], 16)

            def store(i, s, turn):
                sp.wait_ge(xn_ready, i + 1)
                sp.dma_start(xn_dram[bass.ts(i, P), :], xn[s][:]).then_inc(xn_stored[s], 16)

            by_twos(sp, NT, store)
            for s in range(2):
                sp.wait_ge(xn_stored[s], stored(NT // 2 - 1))

        @block.tensor
        def _(pe):
            pe.wait_ge(wr_loaded, 16)
            pe.sem_inc(xt_done, 2)
            pe.sem_inc(lg_done, 2)

            def transpose(i, s, turn):
                pe.wait_ge(xn_ready, i + 1)
                pe.wait_ge(xt_ready, reusable(i))
                for c in range(HC):
                    last = nc.tensor.transpose(ps_xt[s][:, c, :], xn[s][:, c * P:(c + 1) * P], const["ident"])
                last.then_inc(xt_done, 1)

            def logits(i, s, turn):
                pe.wait_ge(xt_ready, made(i))
                pe.wait_ge(lg_read, reusable(i))
                if v_out is not None:
                    for c in range(HC):
                        nc.tensor.matmul(ps_v[s], xt[s][:, c, :], v_out["w"][:, c, :], start=(c == 0), stop=(c == HC - 1))
                for c in range(HC):
                    last = nc.tensor.matmul(ps_lg[s], xt[s][:, c, :], wr[:, c, :], start=(c == 0), stop=(c == HC - 1))
                last.then_inc(lg_done, 1)

            software_pipelined(pe, NT, transpose, logits)
            pe.wait_ge(oh_ready, 1)
            nc.tensor.matmul(ps_rank, const["tri"], OHb[:], start=True, stop=True)
            nc.tensor.matmul(ps_total, const["ones"], OHb[:], start=True, stop=True).then_inc(rank_done, 1)
            pe.wait_ge(zeros_ready, 1)
            pe.wait_ge(lg_read, NT + 2)
            nc.tensor.matmul(ps_table, const["ones"], zeros[:], start=True, stop=False)
            pe.sem_inc(hot_used, 2)

            def place(i, s, turn):
                pe.wait_ge(hot_ready, i + 1)
                nc.tensor.matmul(ps_table, hot_row[s][:], hot_block[s][:].rearrange("p a b -> p (a b)"),
                                 start=False, stop=False).then_inc(hot_used, 1)

            by_twos(pe, NC, place)
            nc.tensor.matmul(ps_table, const["ones"], zeros[:], start=False, stop=True).then_inc(table_done, 1)

        @block.scalar
        def _(act):
            act.wait_ge(var_ready, 1)
            nc.scalar.activation(root[:], var[:], ACT.Sqrt).then_inc(root_ready, 1)
            act.sem_inc(xt_ready, 2)

            def copy(i, s, turn):
                act.wait_ge(xt_done, made(i))
                act.wait_ge(lg_done, reusable(i))
                act.wait_ge(xt_copied, reusable(i))
                nc.scalar.copy(xt[s][:], ps_xt[s]).then_inc(xt_ready, 1)

            by_twos(act, NT, copy)
            act.wait_ge(exp_wanted, 1)
            nc.scalar.activation(A2[:], LG[:] if L == 0 else A1[:], ACT.Exp, scale=(-1.0 if L == 0 else 1.0)).then_inc(exp_ready, 1)

        @block.gpsimd
        def _(pool):
            pool.sem_inc(xt_copied, 2)

            def copy(i, s, turn):
                pool.wait_ge(xt_ready, made(i))
                nc.gpsimd.tensor_copy(xnT[:, :, bass.ts(i, P)], xt[s][:]).then_inc(xt_copied, 1)

            by_twos(pool, NT, copy)

        @block.vector
        def _(dve):
            V = nc.vector
            step = Chain(dve, chain)
            V.memset(zeros[:], 0.0).then_inc(zeros_ready, 1)
            for c in range(4):
                if x_src is not None:
                    dve.wait_ge(x_loaded[c], 16)
                with dve.Fori(c * NT // 4, (c + 1) * NT // 4) as i:
                    V.bn_stats(st[:, i, :], X[:, i, :]).then_inc(stats_made, 1)
            dve.wait_ge(stats_made, NT)
            step(V.tensor_tensor(sd[:], st[:, :, 1], st[:, :, 4], ALU.subtract))
            step(V.tensor_tensor(mean[:], st[:, :, 1], st[:, :, 4], ALU.add))
            step(V.tensor_scalar(mean[:], mean[:], 0.5, None, ALU.mult))
            step(V.tensor_tensor(sd[:], sd[:], sd[:], ALU.mult))
            step(V.tensor_tensor(var[:], st[:, :, 2], st[:, :, 5], ALU.add))
            step(V.tensor_scalar(var[:], var[:], 1.0 / D, EPS, ALU.mult, ALU.add))
            V.scalar_tensor_tensor(var[:], sd[:], 0.25, var[:], ALU.mult, ALU.add).then_inc(var_ready, 1)
            dve.wait_ge(var_ready, 1)
            dve.wait_ge(root_ready, 1)
            step(V.reciprocal(quot[:], root[:]))
            step(V.tensor_tensor(quot[:], quot[:], var[:], ALU.mult))
            step(V.tensor_tensor(root[:], root[:], quot[:], ALU.add))
            step(V.tensor_scalar(root[:], root[:], 0.5, None, ALU.mult))
            step(V.reciprocal(rstd[:], root[:]))
            dve.sem_inc(lg_read, 2)

            def normalise(i, s, turn):
                dve.wait_ge(xt_done, reusable(i))
                dve.wait_ge(xn_stored[s], storable(turn))
                V.tensor_scalar(xn[s][:], X[:, i, :], mean[:, bass.ds(i, 1)], rstd[:, bass.ds(i, 1)],
                                ALU.subtract, ALU.mult).then_inc(xn_ready, 1)

            def keep_logits(i, s, turn):
                dve.wait_ge(lg_done, made(i))
                if v_out is not None:
                    V.tensor_tensor(v_out["v"][:, i, :], ps_v[s], v_out["b"][:], ALU.add)
                if bias is not None:
                    V.tensor_tensor(LG[:, i, :], ps_lg[s], bias, ALU.add).then_inc(lg_read, 1)
                else:
                    V.tensor_copy(LG[:, i, :], ps_lg[s]).then_inc(lg_read, 1)

            software_pipelined(dve, NT, normalise, keep_logits)
            dve.wait_ge(lg_read, NT + 2)
            full = [P, NT, E]
            if L == 0:
                V.memset(pick[:], 0.0).then_inc(exp_wanted, 1)
                dve.wait_ge(exp_ready, 1)
                step(V.tensor_scalar(A1[:], A2[:], 1.0, None, ALU.add))
                step(V.reciprocal(PR[:], A1[:]))
            else:
                step(V.reduce_max(pick[:], LG[:], AX.X))
                V.tensor_tensor(A1[:], LG[:], spread(pick[:], 2, full), ALU.subtract).then_inc(exp_wanted, 1)
                dve.wait_ge(exp_ready, 1)
                step(V.reduce_sum(pick[:], A2[:], AX.X))
                step(V.reciprocal(pick[:], pick[:]))
                step(V.tensor_tensor(PR[:], A2[:], spread(pick[:], 2, full), ALU.mult))
            gate = route["gate"][:].rearrange("p (g k t) -> p g k t", g=G, k=2)
            for k in range(2):
                src = PR if k == 0 else A1
                step(V.reduce_max(pick[:], src[:], AX.X))
                step(V.tensor_copy(gate[:, :, k, :], pick[:].rearrange("p (g t) -> p g t", g=G)))
                step(V.tensor_tensor(A2[:], src[:], spread(pick[:], 2, full), ALU.is_equal))
                step(V.scalar_tensor_tensor(A2[:], A2[:], -64.0, const["expert_no"], ALU.mult, ALU.add))
                step(V.tensor_reduce(pick[:], A2[:], AX.X, ALU.min))
                step(V.tensor_tensor(A2[:], A2[:], spread(pick[:], 2, full), ALU.is_equal))
                for g in range(G):
                    step(V.tensor_copy(OH[:, g, :, k, :], A2[:, g * TG:(g + 1) * TG, :].rearrange("p t e -> p e t")))
                if k == 0:
                    step(V.scalar_tensor_tensor(A1[:], A2[:], -4.0, PR[:], ALU.mult, ALU.add))
            oh = OH[:].rearrange("p g e k t -> p (g e k t)")
            V.tensor_copy(OHb[:], oh).then_inc(oh_ready, 1)
            dve.wait_ge(rank_done, 1)
            step(V.tensor_copy(T[:], ps_total))
            step(V.tensor_tensor_scan(S[:], const[f"go_on{L}"], T[:], 0.0, ALU.mult, ALU.add))
            step(V.tensor_tensor(R[:], S[:], T[:], ALU.subtract))
            step(V.tensor_tensor(R[:], R[:], ps_rank, ALU.add))
            if L == 0:
                counts = S[:].rearrange("p (e c) -> p e c", e=E)[:, :, NC - 1]
                step(V.tensor_tensor(over[:], spread(counts, 2, [P, E, NT]), spread(const["rows_before"], 1, [P, E, NT]), ALU.is_gt))
                step(V.reduce_sum(nblk[:], over[:], AX.X))
                step(V.tensor_tensor_scan(ends[:], const["one8"], nblk[:], 0.0, ALU.mult, ALU.add))
                step(V.tensor_tensor(base[:], ends[:], nblk[:], ALU.subtract))
                step(V.tensor_scalar(base[:], base[:], float(P), None, ALU.mult))
                view = R[:].rearrange("p (e c) -> p e c", e=E)
                step(V.tensor_tensor(view, view, spread(base[:], 2, [P, E, NC]), ALU.add))
                sh = [P, BLOCKS0, E]
                step(V.tensor_tensor(after[:], spread(const["count_up"][:, 0:BLOCKS0], 2, sh), spread(ends[:], 1, sh), ALU.is_ge))
                step(V.reduce_sum(blk_e[:], after[:], AX.X))
                step(V.tensor_scalar(route["expert"][:], blk_e[:], float(E - 1), None, ALU.min))
            else:
                step(V.tensor_tensor(T[:], oh, R[:], ALU.mult))
                for g in range(G):
                    step(V.reduce_sum(keep[:, g * 2 * TG:(g + 1) * 2 * TG],
                                      T[:, g * E * 2 * TG:(g + 1) * E * 2 * TG].rearrange("p (e c) -> p c e", e=E), AX.X))
                step(V.tensor_scalar(keep[:], keep[:], float(CAP), None, ALU.is_lt))
                step(V.tensor_tensor(R[:], R[:], const["slot_base"], ALU.add))
            step(V.tensor_tensor(T[:], oh, R[:], ALU.mult))
            for g in range(G):
                step(V.reduce_sum(dest[:, g * 2 * TG:(g + 1) * 2 * TG],
                                  T[:, g * E * 2 * TG:(g + 1) * E * 2 * TG].rearrange("p (e c) -> p c e", e=E), AX.X))
            if L == 1:
                step(V.tensor_tensor(dest[:], dest[:], keep[:], ALU.mult))
                step(V.tensor_tensor(route["gate"][:], route["gate"][:], keep[:], ALU.mult))
            step(V.tensor_copy(route["dest"][:], dest[:]))
            if L == 1:
                step(V.tensor_scalar(keep[:], keep[:], -8192.0, 8192.0, ALU.mult, ALU.add))
                step(V.tensor_tensor(dest[:], dest[:], keep[:], ALU.add))
            step(V.tensor_copy(row_i[:], dest[:]))
            step(V.tensor_scalar(lo_i[:], row_i[:], P - 1, None, ALU.bitwise_and))
            step(V.tensor_scalar(hi_i[:], row_i[:], 7, None, ALU.logical_shift_right))
            step(V.tensor_copy(lo[:], lo_i[:]))
            step(V.tensor_copy(hi[:], hi_i[:]))

            def one_hots(i, s, turn):
                dve.wait_ge(hot_used, reusable(i))
                V.tensor_scalar(hot_row[s][:], const["count_up"], lo[:, bass.ds(i, 1)], None, ALU.is_equal)
                V.tensor_scalar(hot_block[s][:, 0, :], const["count_up"][:, 0:NB], hi[:, bass.ds(i, 1)], const["part_no"],
                                ALU.is_equal, ALU.mult)
                V.tensor_scalar(hot_block[s][:, 1, :], const["count_up"][:, 0:NB], hi[:, bass.ds(i, 1)],
                                const[f"tile_no{L}"][:, bass.ds(i, 1)], ALU.is_equal, ALU.mult).then_inc(hot_ready, 1)

            by_twos(dve, NC, one_hots)
            dve.wait_ge(table_done, 1)
            step(V.tensor_copy(table[:].rearrange("p a b -> p (a b)"), ps_table))
            step(V.scalar_tensor_tensor(route["token"][:, 0:NB], table[:, 1, :], float(P), table[:, 0, :], ALU.mult, ALU.add))


def scan_branch(nc, X, xnT, w, const, expert_weights):
    HALF = 512
    with phase(nc) as stack:
        m = stack.memory
        wz = m.sb("w_z", [P, HC, D])
        w3 = m.sb("w_bcd", [P, HC, 3, 32])
        wo = m.sb("w_out0", [P, HC, D])
        bz = m.sb("b_z", [P, HC])
        b3 = m.sb("b_bcd_alog", [P, 4])
        bo = m.sb("b_out0", [P, D])
        U = m.sb("u", [P, SEQ])
        V1 = m.sb("abs_u", [P, SEQ])
        V2 = m.sb("exp_u", [P, SEQ])
        Bt = m.sb("b_t", [P, SEQ])
        St = m.sb("state", [P, SEQ])
        Cs = Bt
        negA = m.sb("neg_a", [P, 1])
        YS = m.sb("y_scan", [P, NT])
        gz = [m.sb(f"gelu_z{s}", [P, HC, HALF]) for s in range(2)]
        loaded = m.sem("scan_w_loaded")
        small_loaded = m.sem("bcd_b_loaded")
        cleared, chain = m.sem("scan_cleared"), m.sem("scan_chain")
        bcd_done = m.sem("bcd_done")
        u_ready, abs_ready, act_chain, e_ready, decay_ready = (
            m.sem("u_ready"), m.sem("abs_ready"), m.sem("scan_act_chain"), m.sem("delta_ready"), m.sem("decay_ready"))
        cs_ready, y_done, y_ready = m.sem("cs_ready"), m.sem("y_done"), m.sem("y_ready")
        z_done, z_ready, o_done, o_read = m.sem("z_done"), m.sem("z_ready"), m.sem("gelu_o_done"), m.sem("gelu_o_read")
        x_biased = m.sem("x_biased")
        ps = stack.enter_context(nc.psum_tensor("ps_scan", [P, 8, 512], F32))
        block = stack.block.enter_context(nc.Block())
        GROUPS = TOK // HALF

        @block.sync
        def _(sp):
            sp.wait_ge(cleared, 2)
            for b in range(BATCH):
                sp.dma_start(b3[32 * b:32 * b + N_STATE, :], w["bcd_alog"]).then_inc(small_loaded, 16)
            for f in range(3):
                c0 = 2 * D + f * N_STATE
                sp.dma_start(w3[:, :, f, 0:N_STATE], w["in"][:, :, c0:c0 + N_STATE]).then_inc(loaded, 16)
            sp.dma_start(wz[:], w["in"][:, :, D:2 * D]).then_inc(loaded, 16)
            sp.dma_start(wo[:], w["out"]).then_inc(loaded, 16)
            sp.dma_start(bz[:], w["b_z"]).then_inc(loaded, 16)
            sp.dma_start(bo[:], w["b_out"].to_broadcast([P, D])).then_inc(loaded, 16)
            for (dst, src), sem in zip(expert_weights["loads"], expert_weights["loaded"]):
                sp.dma_start(dst[:], src).then_inc(sem, 16)

        @block.gpsimd
        def _(pool):
            nc.gpsimd.memset(b3[:], 0.0).then_inc(cleared, 1)
            nc.gpsimd.memset(w3[:], 0.0).then_inc(cleared, 1)
            pool.wait_ge(loaded, 7 * 16)
            with pool.Fori(0, NT) as i:
                nc.gpsimd.tensor_tensor(X[:, i, :], X[:, i, :], bo[:], ALU.add).then_inc(x_biased, 1)

        @block.tensor
        def _(pe):
            pe.wait_ge(loaded, 7 * 16)
            for f in range(3):
                for h in range(2):
                    for b in range(BATCH):
                        t0 = b * SEQ + h * HALF
                        for c in range(HC):
                            last = nc.tensor.matmul(ps[32 * b:32 * b + 32, 2 * f + h, :], w3[:, c, f, :],
                                                    xnT[:, c, t0:t0 + HALF], start=(c == 0), stop=(c == HC - 1))
                last.then_inc(bcd_done, 1)
            pe.wait_ge(cs_ready, 1)
            for j in range(SEQ // P):
                last = nc.tensor.matmul(ps[:, 4, 4 * j:4 * j + 4], Cs[:, j * P:(j + 1) * P], const["batch_of"],
                                        start=True, stop=True)
            last.then_inc(y_done, 1)
            pe.wait_ge(y_ready, 1)
            pe.sem_inc(z_done, 2)
            pe.sem_inc(o_done, 2)

            def project(g, s, turn):
                pe.wait_ge(z_ready, reusable(g))
                for c in range(HC):
                    for k in range(HC):
                        last = nc.tensor.matmul(ps[:, 2 * s + c, :], wz[:, k, c * P:(c + 1) * P],
                                                xnT[:, k, bass.ts(g, HALF)], start=(k == 0), stop=(k == HC - 1))
                last.then_inc(z_done, 1)

            def out(g, s, turn):
                pe.wait_ge(z_ready, made(g))
                pe.wait_ge(o_read, reusable(g))
                for t in range(4):
                    for c in range(HC):
                        last = nc.tensor.matmul(ps[:, 4 + 2 * s + t // 2, (t % 2) * D:(t % 2) * D + D],
                                                gz[s][:, c, t * P:(t + 1) * P], wo[:, c, :],
                                                start=(c == 0), stop=(c == HC - 1))
                last.then_inc(o_done, 1)

            software_pipelined(pe, GROUPS, project, out)

        @block.scalar
        def _(act):
            link = Chain(act, act_chain)
            act.wait_ge(small_loaded, 4 * 16)
            link(nc.scalar.activation(negA[:], b3[:, 3:4], ACT.Exp))
            link(nc.scalar.mul(negA[:], negA[:], -1.0))
            act.wait_ge(u_ready, 1)
            link(nc.scalar.activation(V1[:], U[:], ACT.Abs))
            link(nc.scalar.activation(V2[:], V1[:], ACT.Exp, scale=-1.0))
            nc.scalar.activation(V1[:], V2[:], ACT.Ln, bias=1.0).then_inc(abs_ready, 1)
            act.wait_ge(e_ready, 1)
            nc.scalar.activation(V2[:], U[:], ACT.Exp, scale=negA[:]).then_inc(decay_ready, 1)
            act.sem_inc(z_ready, 2)

            def gelu(g, s, turn):
                act.wait_ge(z_done, made(g))
                act.wait_ge(o_done, reusable(g))
                for c in range(HC):
                    last = nc.scalar.activation(gz[s][:, c, :], ps[:, 2 * s + c, :], ACT.Gelu, bias=bz[:, c:c + 1])
                last.then_inc(z_ready, 1)

            by_twos(act, GROUPS, gelu)

        @block.vector
        def _(dve):
            V = nc.vector
            step = Chain(dve, chain)
            dve.wait_ge(small_loaded, 4 * 16)
            dve.wait_ge(bcd_done, 3)
            field = lambda f: ps[:, 2 * f:2 * f + 2, :].rearrange("p a t -> p (a t)")
            V.tensor_scalar(U[:], field(2), b3[:, 2:3], None, ALU.add).then_inc(u_ready, 1)
            step(V.tensor_scalar(Bt[:], field(0), b3[:, 0:1], None, ALU.add))
            dve.wait_ge(abs_ready, 1)
            V.scalar_tensor_tensor(U[:], U[:], 0.0, V1[:], ALU.max, ALU.add).then_inc(e_ready, 1)
            dve.wait_ge(decay_ready, 1)
            step(V.tensor_tensor_scan(St[:], V2[:], Bt[:], 0.0, ALU.mult, ALU.add))
            V.scalar_tensor_tensor(Cs[:], field(1), b3[:, 1:2], St[:], ALU.add, ALU.mult).then_inc(cs_ready, 1)
            dve.wait_ge(y_done, 1)
            V.tensor_copy(YS[:].rearrange("p (b j) -> p b j", b=BATCH),
                          ps[:, 4, 0:NT].rearrange("p (j b) -> p b j", b=BATCH)).then_inc(y_ready, 1)
            dve.wait_ge(y_ready, 1)
            dve.wait_ge(x_biased, NT)
            dve.sem_inc(o_read, 2)

            def add(g, s, turn):
                dve.wait_ge(o_done, made(g))
                for t in range(4):
                    src = ps[:, 4 + 2 * s + t // 2, (t % 2) * D:(t % 2) * D + D]
                    last = V.scalar_tensor_tensor(X[:, g * 4 + t, :], src, YS[:, bass.ds(g * 4 + t, 1)],
                                                  X[:, g * 4 + t, :], ALU.mult, ALU.add)
                last.then_inc(o_read, 1)

            by_twos(dve, GROUPS, add)


def shared_expert(nc, X, xnT, w):
    N = 512
    IC = I0 // P
    GROUPS = TOK // N
    with phase(nc) as stack:
        m = stack.memory
        wg, wu = m.sb("wg_shared", [P, HC, I0]), m.sb("wu_shared", [P, HC, I0])
        wd = m.sb("wd_shared", [P, IC, D])
        sg = [m.sb(f"silu_shared{s}", [P, N]) for s in range(2)]
        hT = [m.sb(f"h_shared{s}", [P, IC, N]) for s in range(2)]
        loaded = m.sem("shared_w_loaded")
        gu_done, silu_ready, h_ready = m.sem("gu_done"), m.sem("silu_ready"), m.sem("h_ready")
        y_done, y_read = m.sem("shared_y_done"), m.sem("shared_y_read")
        ps = stack.enter_context(nc.psum_tensor("ps_shared", [P, 8, 512], F32))
        block = stack.block.enter_context(nc.Block())

        @block.sync
        def _(sp):
            for dst, src in ((wg, w["g"]), (wu, w["u"]), (wd, w["d"])):
                sp.dma_start(dst[:], src).then_inc(loaded, 16)

        @block.tensor
        def _(pe):
            pe.wait_ge(loaded, 48)
            pe.sem_inc(gu_done, 2)
            pe.sem_inc(y_done, 2)

            def up(g, s, turn):
                for i in range(IC):
                    n = g * IC + i
                    pe.wait_ge(h_ready, reusable(n))
                    for bank, wt in ((i % 2, wg), (2 + i % 2, wu)):
                        for k in range(HC):
                            last = nc.tensor.matmul(ps[:, bank, :], wt[:, k, i * P:(i + 1) * P], xnT[:, k, bass.ts(g, N)],
                                                    start=(k == 0), stop=(k == HC - 1))
                    last.then_inc(gu_done, 1)

            def down(g, s, turn):
                pe.wait_ge(h_ready, g * IC + IC + 2)
                pe.wait_ge(y_read, reusable(g))
                for t in range(4):
                    for i in range(IC):
                        last = nc.tensor.matmul(ps[:, 4 + 2 * s + t // 2, (t % 2) * D:(t % 2) * D + D],
                                                hT[s][:, i, t * P:(t + 1) * P], wd[:, i, :], start=(i == 0), stop=(i == IC - 1))
                last.then_inc(y_done, 1)

            software_pipelined(pe, GROUPS, up, down)

        @block.scalar
        def _(act):
            act.sem_inc(silu_ready, 2)

            def silu(g, s, turn):
                for i in range(IC):
                    n = g * IC + i
                    act.wait_ge(gu_done, made(n))
                    act.wait_ge(h_ready, reusable(n))
                    nc.scalar.activation(sg[i % 2][:], ps[:, i % 2, :], ACT.Silu).then_inc(silu_ready, 1)

            by_twos(act, GROUPS, silu)

        @block.vector
        def _(dve):
            V = nc.vector
            dve.sem_inc(h_ready, 2)
            dve.sem_inc(y_read, 2)

            def gated(g, s, turn):
                dve.wait_ge(y_done, reusable(g))
                for i in range(IC):
                    dve.wait_ge(silu_ready, made(g * IC + i))
                    V.tensor_tensor(hT[s][:, i, :], sg[i % 2][:], ps[:, 2 + i % 2, :], ALU.mult).then_inc(h_ready, 1)

            def add(g, s, turn):
                dve.wait_ge(y_done, made(g))
                for t in range(4):
                    src = ps[:, 4 + 2 * s + t // 2, (t % 2) * D:(t % 2) * D + D]
                    last = V.tensor_tensor(X[:, g * 4 + t, :], src, X[:, g * 4 + t, :], ALU.add)
                last.then_inc(y_read, 1)

            software_pipelined(dve, GROUPS, gated, add)


def routed_experts(nc, w, route, xn_dram, y_dram, const):
    IC = I0 // P
    with phase(nc) as stack:
        m = stack.memory
        wg, wu, wd, w_loaded = w["wg"], w["wu"], w["wd"], w["loaded"]
        ids = [m.sb(f"row_tokens{s}", [P, 1], I32) for s in range(2)]
        xg = [m.sb(f"rows{s}", [P, D]) for s in range(2)]
        xt = [m.sb(f"rows_t{s}", [P, HC, P]) for s in range(2)]
        sg = [m.sb(f"silu{s}", [P, I0]) for s in range(2)]
        h = [m.sb(f"hidden{s}", [P, I0]) for s in range(2)]
        ht = [m.sb(f"hidden_t{s}", [P, IC, P]) for s in range(2)]
        yr = [m.sb(f"y_rows{s}", [P, D]) for s in range(2)]
        ids_ready, gathers, gathered = m.sem("ids_ready"), m.sem("gathers"), m.sems("gathered", 2)
        xt_done, xt_ready, g_done, u_done = m.sem("rt_xt_done"), m.sem("rt_xt_ready"), m.sem("rt_g_done"), m.sem("rt_u_done")
        silu_ready, h_ready, ht_done, ht_ready = m.sem("rt_silu"), m.sem("rt_h"), m.sem("rt_ht_done"), m.sem("rt_ht_ready")
        y_done, y_ready, y_stored = m.sem("rt_y_done"), m.sem("rt_y_ready"), m.sems("rt_y_stored", 2)
        ps = stack.enter_context(nc.psum_tensor("ps_routed", [P, 8, 512], F32))
        ps_xt = ps[:, 6, 0:D].rearrange("p (c t) -> p c t", c=HC)
        ps_y = ps[:, 7, 0:D]
        ps_ht = [ps[:, 4 + s, :].rearrange("p (c t) -> p c t", c=IC) for s in range(2)]
        block = stack.block.enter_context(nc.Block())

        @block.sync
        def _(sp):
            for s in range(2):
                sp.sem_inc(y_stored[s], 16)

            def store(i, s, turn):
                sp.wait_ge(y_ready, made(i))
                sp.dma_start(y_dram[bass.ts(i, P), :], yr[s][:]).then_inc(y_stored[s], 16)

            by_twos(sp, BLOCKS0, store)
            for s in range(2):
                sp.wait_ge(y_stored[s], stored(BLOCKS0 // 2 - 1))

        @block.gpsimd
        def _(pool):
            def gather(i, s, turn):
                pool.wait_ge(xt_done, reusable(i))
                nc.gpsimd.tensor_copy(ids[s][:], route["token"][:, bass.ds(i, 1)]).then_inc(ids_ready, 1)
                pool.wait_ge(ids_ready, i + 1)
                pool.sem_inc(gathers, 1)
                nc.gpsimd.indirect_dma_start(xg[s][:], None, xn_dram, bass.IndirectOffsetOnAxis(ap=ids[s][:, 0:1], axis=0)
                                             ).then_inc(gathered[s], 16)

            by_twos(pool, BLOCKS0, gather)

        @block.tensor
        def _(pe):
            pe.sem_inc(xt_done, 2)
            pe.sem_inc(u_done, 2)
            pe.sem_inc(ht_done, 2)
            pe.sem_inc(y_done, 2)

            def turn_rows(i, s, turn):
                pe.wait_ge(gathered[s], turn * 16 + 16)
                pe.wait_ge(xt_ready, i + 2)
                for c in range(HC):
                    last = nc.tensor.transpose(ps_xt[:, c, :], xg[s][:, c * P:(c + 1) * P], const["ident"])
                last.then_inc(xt_done, 1)

            def turn_hidden(i, s, turn):
                pe.wait_ge(h_ready, made(i))
                pe.wait_ge(ht_ready, reusable(i))
                for c in range(IC):
                    last = nc.tensor.transpose(ps_ht[s][:, c, :], h[s][:, c * P:(c + 1) * P], const["ident"])
                last.then_inc(ht_done, 1)

            def up(i, s, turn):
                e = pe.value_load(route["expert"][0:1, bass.ds(i, 1)], min_val=0, max_val=E - 1)
                pe.wait_ge(h_ready, reusable(i))
                pe.wait_ge(xt_ready, made(i))
                for bank, wt, sem in ((s, wg, g_done), (2 + s, wu, u_done)):
                    for k in range(HC):
                        last = nc.tensor.matmul(ps[:, bank, :], xt[s][:, k, :], wt[:, bass.ds(e, 1), k, :],
                                                start=(k == 0), stop=(k == HC - 1))
                    last.then_inc(sem, 1)

            def down(i, s, turn):
                e = pe.value_load(route["expert"][0:1, bass.ds(i, 1)], min_val=0, max_val=E - 1)
                pe.wait_ge(y_ready, i + 2)
                pe.wait_ge(ht_ready, made(i))
                for c in range(IC):
                    last = nc.tensor.matmul(ps_y, ht[s][:, c, :], wd[:, bass.ds(e, 1), c, :], start=(c == 0), stop=(c == IC - 1))
                last.then_inc(y_done, 1)

            turn_rows(0, 0, 0)
            turn_rows(1, 1, 0)
            for n in range(3):
                pe.wait_ge(w_loaded[n], 16)
            up(0, 0, 0)
            with pe.Fori(0, BLOCKS0 // 2 - 1) as j:
                for i, s, turn, before in ((j * 2 + 1, 1, j, j), (j * 2 + 2, 0, j + 1, j)):
                    turn_rows(i + 1, 1 - s, j + 1)
                    turn_hidden(i - 1, 1 - s, before)
                    up(i, s, turn)
                    down(i - 1, 1 - s, before)
            turn_hidden(BLOCKS0 - 2, 0, 0)
            up(BLOCKS0 - 1, 1, 0)
            down(BLOCKS0 - 2, 0, 0)
            turn_hidden(BLOCKS0 - 1, 1, 0)
            down(BLOCKS0 - 1, 1, 0)

        @block.scalar
        def _(act):
            act.sem_inc(xt_ready, 2)
            act.sem_inc(silu_ready, 2)
            act.sem_inc(y_ready, 2)

            def copy_rows(i, s):
                act.wait_ge(xt_done, made(i))
                act.wait_ge(u_done, reusable(i))
                nc.scalar.copy(xt[s][:], ps_xt).then_inc(xt_ready, 1)

            def silu(i, s):
                act.wait_ge(g_done, i + 1)
                act.wait_ge(h_ready, reusable(i))
                nc.scalar.activation(sg[s][:], ps[:, s, :], ACT.Silu).then_inc(silu_ready, 1)

            def copy_result(i, s, turn):
                act.wait_ge(y_done, made(i))
                act.wait_ge(y_stored[s], storable(turn))
                nc.scalar.copy(yr[s][:], ps_y).then_inc(y_ready, 1)

            copy_rows(0, 0)
            copy_rows(1, 1)
            silu(0, 0)
            with act.Fori(0, BLOCKS0 // 2 - 1) as j:
                for i, s in ((j * 2 + 1, 1), (j * 2 + 2, 0)):
                    copy_rows(i + 1, 1 - s)
                    silu(i, s)
                    copy_result(i - 1, 1 - s, j)
            silu(BLOCKS0 - 1, 1)
            copy_result(BLOCKS0 - 2, 0, BLOCKS0 // 2 - 1)
            copy_result(BLOCKS0 - 1, 1, BLOCKS0 // 2 - 1)

        @block.vector
        def _(dve):
            dve.sem_inc(h_ready, 2)
            dve.sem_inc(ht_ready, 2)

            def gated(i, s, turn):
                dve.wait_ge(silu_ready, made(i))
                dve.wait_ge(u_done, made(i))
                dve.wait_ge(ht_done, reusable(i))
                nc.vector.tensor_tensor(h[s][:], sg[s][:], ps[:, 2 + s, :], ALU.mult).then_inc(h_ready, 1)

            def turned(i, s, turn):
                dve.wait_ge(ht_done, made(i))
                dve.wait_ge(y_done, reusable(i))
                nc.vector.tensor_copy(ht[s][:], ps_ht[s]).then_inc(ht_ready, 1)

            gated(0, 0, 0)
            with dve.Fori(0, BLOCKS0 // 2 - 1) as j:
                for i, s in ((j * 2 + 1, 1), (j * 2 + 2, 0)):
                    turned(i - 1, 1 - s, j)
                    gated(i, s, j)
            turned(BLOCKS0 - 2, 0, 0)
            gated(BLOCKS0 - 1, 1, 0)
            turned(BLOCKS0 - 1, 1, 0)


def combine(nc, L, X, route, y_dram, out=None):
    G = 1 if L == 0 else G1
    TG = NT // G
    with phase(nc) as stack:
        m = stack.memory
        ids = [[m.sb(f"from{L}_{k}_{s}", [P, 1], I32) for s in range(2)] for k in range(2)]
        rows = [[m.sb(f"back{L}_{k}_{s}", [P, D]) for s in range(2)] for k in range(2)]
        part = [m.sb(f"part{L}_{s}", [P, D]) for s in range(2)]
        ids_ready, gathers = m.sem(f"back_ids{L}"), m.sem(f"back_gathers{L}")
        gathered = [m.sems(f"back{L}_{k}_", 2) for k in range(2)]
        first_ready, used = m.sem(f"first_added{L}"), m.sem(f"back_used{L}")
        out_stored = m.sem(f"out_stored{L}")
        block = stack.block.enter_context(nc.Block())

        @block.gpsimd
        def _(pool):
            for g in range(G):
                def gather(i, s, turn):
                    pool.wait_ge(used, i + g * TG + 1)
                    for k in range(2):
                        col = i + (g * 2 + k) * TG
                        last = nc.gpsimd.tensor_copy(ids[k][s][:], route["dest"][:, bass.ds(col, 1)])
                    last.then_inc(ids_ready, 1)
                    pool.wait_ge(ids_ready, i + g * TG + 1)
                    pool.sem_inc(gathers, 1)
                    for k in range(2):
                        nc.gpsimd.indirect_dma_start(rows[k][s][:], None, y_dram,
                                                     bass.IndirectOffsetOnAxis(ap=ids[k][s][:, 0:1], axis=0)
                                                     ).then_inc(gathered[k][s], 16)

                by_twos(pool, TG, gather)

        @block.vector
        def _(dve):
            dve.sem_inc(used, 2)
            for g in range(G):
                def add(i, s, turn):
                    col = i + g * 2 * TG
                    t = i + g * TG
                    dve.wait_ge(gathered[0][s], turn * 16 + (16 + 16 * (g * TG // 2)))
                    nc.vector.scalar_tensor_tensor(part[s][:], rows[0][s][:], route["gate"][:, bass.ds(col, 1)], X[:, t, :],
                                                   ALU.mult, ALU.add).then_inc(first_ready, 1)
                    dve.wait_ge(gathered[1][s], turn * 16 + (16 + 16 * (g * TG // 2)))
                    dve.wait_ge(first_ready, t + 1)
                    nc.vector.scalar_tensor_tensor(X[:, t, :], rows[1][s][:], route["gate"][:, bass.ds(col + TG, 1)], part[s][:],
                                                   ALU.mult, ALU.add).then_inc(used, 1)

                by_twos(dve, TG, add)

        @block.sync
        def _(sp):
            if out is not None:
                for c in range(4):
                    n = NT // 4
                    sp.wait_ge(used, (c + 1) * n + 2)
                    sp.dma_start(out[:, c * n:(c + 1) * n, :], X[:, c * n:(c + 1) * n, :]).then_inc(out_stored, 16)
                sp.wait_ge(out_stored, 4 * 16)


def project_qk(nc, X, xnT, w, q_dram, k_dram):
    N = 512
    RT = 2 * HC
    GROUPS = TOK // N
    with phase(nc) as stack:
        m = stack.memory
        wqk = m.sb("w_qk", [P, HC, 2 * D])
        bqk = m.sb("b_qk", [P, RT])
        bo = m.sb("b_out1", [P, D])
        full = [m.sb(f"qk_full{s}", [P, RT, N]) for s in range(2)]
        rest = [m.sb(f"qk_rest{s}", [P, RT, N]) for s in range(2)]
        part = [m.sb(f"qk_part{s}", [P, 3, RT, N], BF16) for s in range(2)]
        loaded = m.sem("qk_w_loaded")
        qk_done, full_ready, high_ready, rest_ready, mid_ready, low_ready = (
            m.sem("qk_done"), m.sem("qk_full_ready"), m.sem("qk_high_ready"), m.sem("qk_rest_ready"),
            m.sem("qk_mid_ready"), m.sem("qk_low_ready"))
        qk_stored = m.sems("qk_stored", 2)
        ps = stack.enter_context(nc.psum_tensor("ps_qk", [P, 8, 512], F32))
        block = stack.block.enter_context(nc.Block())
        HPT = HEADS // HC
        COPIES = [(q_dram, 0, part_no, row) for row, part_no in enumerate(Q_PARTS)] + \
                 [(k_dram, HC, part_no, part_no) for part_no in range(3)]
        PER_STORE = 16 * len(COPIES) * HC

        @block.sync
        def _(sp):
            sp.dma_start(wqk[:], w["qk"]).then_inc(loaded, 16)
            sp.dma_start(bqk[:], w["b_qk"]).then_inc(loaded, 16)
            sp.dma_start(bo[:], w["b_out"].to_broadcast([P, D])).then_inc(loaded, 16)
            for s in range(2):
                sp.sem_inc(qk_stored[s], PER_STORE)

            def store(g, s, turn):
                sp.wait_ge(low_ready, made(g))
                for dram, tile, part_no, row in COPIES:
                    for c in range(HC):
                        dst = dram[bass.ds(turn * HEADS + c * HPT, HPT), row, :, s * N:(s + 1) * N]
                        src = part[s][:, part_no, tile + c, :]
                        sp.dma_start(dst, src).then_inc(qk_stored[s], 16)

            by_twos(sp, GROUPS, store)
            for s in range(2):
                sp.wait_ge(qk_stored[s], PER_STORE * (GROUPS // 2 + 1))

        @block.tensor
        def _(pe):
            pe.wait_ge(loaded, 48)

            def project(g, s, turn):
                pe.wait_ge(full_ready, reusable(g))
                for r in range(RT):
                    for k in range(HC):
                        last = nc.tensor.matmul(ps[:, s * RT + r, :], wqk[:, k, r * P:(r + 1) * P], xnT[:, k, bass.ts(g, N)],
                                                start=(k == 0), stop=(k == HC - 1))
                last.then_inc(qk_done, 1)

            by_twos(pe, GROUPS, project)

        @block.vector
        def _(dve):
            dve.wait_ge(loaded, 48)
            dve.sem_inc(full_ready, 2)

            def fill(g, s, turn):
                dve.wait_ge(qk_done, g + 1)
                dve.wait_ge(low_ready, reusable(g))
                for r in range(RT):
                    last = nc.vector.tensor_scalar(full[s][:, r, :], ps[:, s * RT + r, :], bqk[:, r:r + 1],
                                                   0.25 if r < HC else 1.0, ALU.add, ALU.mult)
                last.then_inc(full_ready, 1)

            by_twos(dve, GROUPS, fill)

        @block.scalar
        def _(act):
            def parts(g, s, turn):
                act.wait_ge(full_ready, made(g))
                act.wait_ge(qk_stored[s], (turn + 1) * PER_STORE)
                nc.scalar.copy(part[s][:, 0, :, :], full[s][:]).then_inc(high_ready, 1)
                act.wait_ge(rest_ready, g + 1)
                nc.scalar.copy(part[s][:, 1, :, :], rest[s][:]).then_inc(mid_ready, 1)

            by_twos(act, GROUPS, parts)

        @block.gpsimd
        def _(pool):
            pool.sem_inc(low_ready, 2)
            pool.wait_ge(loaded, 48)

            def rests(g, s, turn):
                pool.wait_ge(high_ready, g + 1)
                nc.gpsimd.tensor_tensor(rest[s][:], full[s][:], part[s][:, 0, :, :], ALU.subtract).then_inc(rest_ready, 1)
                pool.wait_ge(mid_ready, g + 1)
                nc.gpsimd.tensor_tensor(part[s][:, 2, :, :], rest[s][:], part[s][:, 1, :, :], ALU.subtract).then_inc(low_ready, 1)
                for t in range(4):
                    nc.gpsimd.tensor_tensor(X[:, g * 4 + t, :], X[:, g * 4 + t, :], bo[:], ALU.add)

            by_twos(pool, GROUPS, rests)


Q_PARTS = (0, 0, 0, 1, 1, 2)
K_PARTS = (0, 1, 2, 0, 1, 0)
PART_ROWS = HD * len(Q_PARTS)
BIAS_ROWS, MAX_ROWS = 12, 2
SCORE_ROWS = PART_ROWS + BIAS_ROWS
STACK = SCORE_ROWS + MAX_ROWS
QT = SEQ // P
PAIRS = BATCH * HEADS // 2
AHEAD = (3, 3, 2, 3, 3, 2, 0, 0)


def attention(nc, v, q_dram, k_dram, o_dram, s_dram, w, const):
    RING = 3
    with phase(nc) as stack:
        m = stack.memory
        qs = [[m.sb(f"q_stack{s}_{h}", [STACK, SEQ], BF16) for h in range(2)] for s in range(RING)]
        ks = [[[m.sb(f"k_stack{s}_{h}_{side}", [STACK, SEQ], BF16) for side in range(2)] for h in range(2)] for s in range(RING)]
        vs = [m.sb(f"v_stage{s}", [P, 2, QT, 2 * HD]) for s in range(RING)]
        prob = [m.sb(f"prob{n}", [P, 4, 512]) for n in range(2)]
        top = [m.sb(f"top{h}", [P, QT]) for h in range(2)]
        neg = [m.sb(f"neg_top{h}", [P, 2, QT], BF16) for h in range(2)]
        negT = [m.sb(f"neg_top_t{h}", [2 * QT, P], BF16) for h in range(2)]
        osb = [m.sb(f"o_stage{s}", [P, 512]) for s in range(RING)]
        fix_t = m.sb("fix_by_key", [P, HEADS, 3, P], BF16)
        fix = m.sb("fix_by_query", [P, HEADS, P], BF16)
        identb = m.sb("ident_bf", [P, P], BF16)
        tables_loaded = m.sem("attn_tables_loaded")
        stack_loaded = m.sems("stack_loaded", RING)
        ones_ready, v_ready = m.sem("ones_ready"), m.sem("v_staged")
        s1_done, s1_read = m.sem("s1_done"), m.sem("s1_read")
        high_ready, neg_ready = m.sem("top_high_ready"), m.sem("neg_ready")
        turned, turned_read = m.sem("neg_turned"), m.sem("neg_turned_read")
        max_loaded = [m.sems(f"max_loaded{s}_", 2) for s in range(RING)]
        s2_done, exp_ready, pv_done = m.sem("s2_done"), m.sem("exp_ready"), m.sem("pv_done")
        o_read, o_stored = m.sem("o_read"), m.sems("o_stored", RING)
        ps = stack.enter_context(nc.psum_tensor("ps_attn", [P, 8, 512], F32))
        ps_turn = ps[0:2 * QT, 7, 0:P // 2].bitcast(BF16)
        block = stack.block.enter_context(nc.Block())
        CONST_DMAS = 3
        LOADS = 16 * 2 * (1 + 2 * 3 + CONST_DMAS)

        def over_pairs(engine, body, peeled=False):
            if peeled:
                for p in range(RING):
                    body(p, p, 0, True)
            with engine.Fori(1 if peeled else 0, PAIRS // RING) as j:
                for s in range(RING):
                    body(j * RING + s, s, j, True)
            for p in range(PAIRS // RING * RING, PAIRS):
                body(p, p % RING, p // RING, p < PAIRS - 1)

        @block.sync
        def _(sp):
            for dst, src in ((fix_t[:].rearrange("p h a q -> p (h a q)"), w["fix_by_key"]),
                             (fix[:].rearrange("p h q -> p (h q)"), w["fix_by_query"]), (identb[:], w["ident_bf"])):
                sp.dma_start(dst, src).then_inc(tables_loaded, 16)

            def load(p, s):
                for h in range(2):
                    bh = p * 2 + h
                    head = (p % (HEADS // 2)) * 2 + h
                    row = lambda dram, a, b: dram[bass.ds(bh, 1), a:b].rearrange("o a d t -> (o a d) t")
                    sp.dma_start(qs[s][h][0:PART_ROWS, :], row(q_dram, 0, 6)).then_inc(stack_loaded[s], 16)
                    sp.dma_start(qs[s][h][PART_ROWS:SCORE_ROWS, :],
                                 w["q_bias"][bass.ds(head, 1)].rearrange("o r t -> (o r) t")).then_inc(stack_loaded[s], 16)
                    for side in range(2):
                        at = 0
                        for n in (3, 2, 1):
                            sp.dma_start(ks[s][h][side][at:at + n * HD, :], row(k_dram, 0, n)).then_inc(stack_loaded[s], 16)
                            at += n * HD
                        sp.dma_start(ks[s][h][side][PART_ROWS:STACK, :],
                                     w["k_bias"][bass.ds(head, 1), side].rearrange("o r t -> (o r) t")).then_inc(stack_loaded[s], 16)

            def maxima(p, s, h):
                sp.wait_ge(turned_read, p * 2 + h + 1)
                for n in range(2):
                    sp.dma_start(qs[s][h][SCORE_ROWS + n:SCORE_ROWS + n + 1, :],
                                 negT[h][n * QT:(n + 1) * QT, :]).then_inc(max_loaded[s][h], 16)

            def store(p, s):
                sp.wait_ge(o_read, p + 2)
                for h in range(2):
                    for half in range(2):
                        at = 32 * (2 * h + half)
                        for dram, first in ((o_dram, 0), (s_dram, HD)):
                            sp.dma_start(dram[bass.ds(p * 2 * HD + h * HD, HD), half * 512:(half + 1) * 512],
                                         osb[s][at + first:at + first + HD, :]).then_inc(o_stored[s], 16)

            for p in range(RING):
                load(p, p)
                sp.sem_inc(o_stored[p], 16 * 8)
            for h in range(2):
                maxima(0, 0, h)

            def body(p, s, turn, more):
                if more:
                    for h in range(2):
                        maxima(p + 1, (s + 1) % RING, h)

            with sp.Fori(0, (PAIRS - RING) // RING) as j:
                for s in range(RING):
                    p = j * RING + s
                    body(p, s, j, True)
                    sp.wait_ge(pv_done, p * QT + QT + 2)
                    load(p + RING, s)
                    store(p, s)
            for p in range((PAIRS - RING) // RING * RING, PAIRS):
                body(p, p % RING, 0, p < PAIRS - 1)
                if p + RING < PAIRS:
                    sp.wait_ge(pv_done, p * QT + QT + 2)
                    load(p + RING, p % RING)
                store(p, p % RING)
            for s in range(RING):
                sp.wait_ge(o_stored[s], 16 * 8 * (1 + len(range(s, PAIRS, RING))))

        @block.gpsimd
        def _(pool):
            for s in range(RING):
                nc.gpsimd.memset(vs[s][:], 1.0).then_inc(ones_ready, 1)
            pool.wait_ge(ones_ready, RING)

            def stage(p, s):
                for h in range(2):
                    col = (p % (HEADS // 2)) * (2 * HD) + h * HD
                    last = nc.gpsimd.tensor_copy(vs[s][:, h, :, 0:HD], v[:, bass.ds((p // (HEADS // 2)) * QT, QT), bass.ds(col, HD)])
                last.then_inc(v_ready, 1)

            stage(0, 0)

            def body(p, s, turn, more):
                if more:
                    if not isinstance(p, int) or p > 0:
                        pool.wait_ge(pv_done, p * QT - QT + 2)
                    stage(p + 1, (s + 1) % RING)

            over_pairs(pool, body, peeled=True)

        def first_ranges(qb):
            out = []
            for bank in range(2):
                lo, hi, cut = bank * 512, bank * 512 + 512, P * (qb + 1)
                if lo < min(cut, hi):
                    out.append((0, lo, min(cut, hi), bank == qb // 4))
                if max(cut, lo) < hi:
                    out.append((1, max(cut, lo), hi, False))
            return out

        @block.tensor
        def _(pe):
            T = nc.tensor
            pe.wait_ge(tables_loaded, 48)
            pe.sem_inc(pv_done, 2)

            def first(p, s, u):
                h, qb = u // QT, u % QT
                at = 2 * (u % 2)
                n = p * 2 * QT + u
                pe.wait_ge(s1_read, reusable(n))
                opened = set()
                for side, a, b, diagonal in first_ranges(qb):
                    bank = at + a // 512
                    last = T.matmul(ps[:, bank, a % 512:a % 512 + b - a], qs[s][h][0:SCORE_ROWS, qb * P:(qb + 1) * P],
                                    ks[s][h][side][0:SCORE_ROWS, a:b], start=bank not in opened, stop=True, skip_group_check=True)
                    opened.add(bank)
                    if diagonal:
                        head = (p % (HEADS // 2)) * 2 + h
                        last = T.matmul(ps[:, bank, qb % 4 * P:qb % 4 * P + P], identb[:], fix[:, bass.ds(head, 1), :],
                                        start=False, stop=True, skip_group_check=True)
                last.then_inc(s1_done, 1)

            def turn_maxima(p, h):
                pe.wait_ge(neg_ready, p * 2 + h + 1)
                if not isinstance(p, int) or p + h > 0:
                    pe.wait_ge(turned_read, p * 2 + h)
                T.transpose(ps_turn, neg[h][:].rearrange("p a q -> p (a q)"), identb[:]).then_inc(turned, 1)

            def second(p, s, kb, h, half):
                u = (kb * 2 + h) * 2 + half
                bank = 4 + u % 2
                n = p * 4 * QT + u
                pe.wait_ge(exp_ready, reusable(n))
                lo, hi, cut = half * 512, half * 512 + 512, kb * P
                keys = slice(kb * P, (kb + 1) * P)
                opened = False
                if max(cut, lo) < hi:
                    a = max(cut, lo)
                    last = T.matmul(ps[:, bank, a - lo:512], ks[s][h][0][0:STACK, keys], qs[s][h][0:STACK, a:hi],
                                    start=True, stop=True, skip_group_check=True)
                    opened = True
                if lo <= cut < hi:
                    head = (p % (HEADS // 2)) * 2 + h
                    for part in range(1 if h == 0 else 3):
                        last = T.matmul(ps[:, bank, cut - lo:cut - lo + P], identb[:], fix_t[:, bass.ds(head, 1), part, :],
                                        start=False, stop=True, skip_group_check=True)
                if lo < min(cut, hi):
                    b = min(cut, hi)
                    last = T.matmul(ps[:, bank, 0:b - lo], ks[s][h][1][0:STACK, keys], qs[s][h][0:STACK, lo:b],
                                    start=not opened, stop=True, skip_group_check=True)
                last.then_inc(s2_done, 1)

            def values(p, s, kb):
                n = p * QT + kb
                pe.wait_ge(exp_ready, n * 4 + 4 + 2)
                if kb == 0:
                    pe.wait_ge(v_ready, p + 1)
                    pe.wait_ge(o_read, p + 1)
                for h in range(2):
                    for half in range(2):
                        c = 2 * h + half
                        last = T.matmul(ps[32 * c:32 * c + 32, 6, :], vs[s][:, h, kb, :], prob[kb % 2][:, c, :],
                                        start=(kb == 0), stop=(kb == QT - 1))
                last.then_inc(pv_done, 1)

            def both(p, s, turn, more):
                nxt, u = (s + 1) % RING, 0
                if more:
                    pe.wait_ge(stack_loaded[nxt], ((turn + 1) if nxt == 0 else turn) * LOADS + LOADS)
                for h in range(2):
                    pe.wait_ge(max_loaded[s][h], turn * 32 + 32)
                for kb in range(QT):
                    queue = [lambda h=h, half=half: second(p, s, kb, h, half) for h in range(2) for half in range(2)]
                    tiles = AHEAD[kb] if more else 0
                    for i in range(4):
                        queue[i]()
                        if i < tiles:
                            first(p + 1, nxt, u)
                            u += 1
                            if u == QT + 3:
                                turn_maxima(p + 1, 0)
                    if kb == QT - 2 and more:
                        turn_maxima(p + 1, 1)
                    if kb > 0:
                        values(p, s, kb - 1)
                values(p, s, QT - 1)

            pe.wait_ge(stack_loaded[0], LOADS)
            for u in range(2 * QT):
                first(0, 0, u)
            for h in range(2):
                turn_maxima(0, h)
            over_pairs(pe, both)

        @block.scalar
        def _(act):
            act.sem_inc(exp_ready, 2)

            def body(p, s, turn, more):
                for kb in range(QT):
                    for c in range(4):
                        n = p * 4 * QT + kb * 4 + c
                        act.wait_ge(s2_done, n + 1)
                        if c == 0:
                            act.wait_ge(pv_done, reusable(p * QT + kb))
                        nc.scalar.activation(prob[kb % 2][:, c, :], ps[:, 4 + c % 2, :], ACT.Exp).then_inc(exp_ready, 1)

            over_pairs(act, body)

        @block.vector
        def _(dve):
            V = nc.vector
            dve.sem_inc(s1_read, 2)
            dve.sem_inc(o_read, 1)

            def maximum(p, u):
                n = p * 2 * QT + u
                h = u // QT
                dve.wait_ge(s1_done, n + 1)
                V.reduce_max(top[h][:, u % QT:u % QT + 1], ps[:, 2 * (u % 2):2 * (u % 2) + 2, :].rearrange("p a q -> p (a q)"),
                             AX.X).then_inc(s1_read, 1)

            def negate(p, h):
                dve.wait_ge(s1_read, p * 2 * QT + (h + 1) * QT + 2)
                V.tensor_scalar(neg[h][:, 0, :], top[h][:], -1.0, None, ALU.mult).then_inc(high_ready, 1)
                dve.wait_ge(high_ready, p * 2 + h + 1)
                V.scalar_tensor_tensor(neg[h][:, 1, :], top[h][:], -1.0, neg[h][:, 0, :], ALU.mult, ALU.subtract).then_inc(neg_ready, 1)

            def keep_turned(p, h):
                dve.wait_ge(turned, p * 2 + h + 1)
                V.tensor_copy(negT[h][:], ps_turn).then_inc(turned_read, 1)

            for u in range(2 * QT):
                maximum(0, u)
                if u % QT == QT - 1:
                    negate(0, u // QT)
            for h in range(2):
                keep_turned(0, h)

            def body(p, s, turn, more):
                if more:
                    for u in range(2 * QT):
                        maximum(p + 1, u)
                        if u == QT - 1:
                            negate(p + 1, 0)
                        if u == QT + 3:
                            dve.wait_ge(max_loaded[s][0], turn * 32 + 32)
                            keep_turned(p + 1, 0)
                    negate(p + 1, 1)
                    dve.wait_ge(max_loaded[s][1], turn * 32 + 32)
                    keep_turned(p + 1, 1)
                dve.wait_ge(pv_done, p * QT + QT + 2)
                dve.wait_ge(o_stored[s], turn * 128 + 128)
                V.tensor_copy(osb[s][:], ps[:, 6, :]).then_inc(o_read, 1)

            over_pairs(dve, body)


def project_out(nc, X, o_dram, s_dram, w):
    N = 512
    GROUPS = TOK // N
    with phase(nc) as stack:
        m = stack.memory
        wo = m.sb("w_out1", [P, HC, D])
        raw = [m.sb(f"o_raw{s}", [P, HC, N]) for s in range(2)]
        sums = [m.sb(f"o_sums{s}", [P, HC, N]) for s in range(2)]
        inv = [m.sb(f"o_inverse{s}", [P, HC, N]) for s in range(2)]
        o = [m.sb(f"o_t{s}", [P, HC, N]) for s in range(2)]
        w_loaded, o_loaded = m.sem("w_out1_loaded"), m.sems("o_loaded", 2)
        inv_ready, o_ready, y_done, y_read = m.sem("inv_ready"), m.sem("o_ready"), m.sem("out1_done"), m.sem("out1_read")
        ps = stack.enter_context(nc.psum_tensor("ps_out1", [P, 8, 512], F32))
        block = stack.block.enter_context(nc.Block())

        @block.sync
        def _(sp):
            sp.dma_start(wo[:], w).then_inc(w_loaded, 16)

            def load(g, s, turn):
                sp.wait_ge(o_ready, reusable(g))
                for dst, dram in ((raw, o_dram), (sums, s_dram)):
                    src = dram[bass.ds(turn * D, D), s * N:(s + 1) * N]
                    sp.dma_start(dst[s][:], src.rearrange("(c p) t -> p c t", p=P)).then_inc(o_loaded[s], 16)

            by_twos(sp, GROUPS, load)

        @block.vector
        def _(dve):
            V = nc.vector
            dve.sem_inc(o_ready, 2)
            dve.sem_inc(y_read, 2)

            def divide(g, s, turn):
                dve.wait_ge(o_loaded[s], turn * 32 + 32)
                V.reciprocal(inv[s][:], sums[s][:]).then_inc(inv_ready, 1)
                dve.wait_ge(inv_ready, g + 1)
                dve.wait_ge(y_done, reusable(g))
                V.tensor_tensor(o[s][:], raw[s][:], inv[s][:], ALU.mult).then_inc(o_ready, 1)

            def add(g, s, turn):
                dve.wait_ge(y_done, made(g))
                for t in range(4):
                    src = ps[:, 2 * s + t // 2, (t % 2) * D:(t % 2) * D + D]
                    last = V.tensor_tensor(X[:, g * 4 + t, :], src, X[:, g * 4 + t, :], ALU.add)
                last.then_inc(y_read, 1)

            software_pipelined(dve, GROUPS, divide, add)

        @block.tensor
        def _(pe):
            pe.wait_ge(w_loaded, 16)
            pe.sem_inc(y_done, 2)

            def out(g, s, turn):
                pe.wait_ge(o_ready, made(g))
                pe.wait_ge(y_read, reusable(g))
                for t in range(4):
                    for c in range(HC):
                        last = nc.tensor.matmul(ps[:, 2 * s + t // 2, (t % 2) * D:(t % 2) * D + D],
                                                o[s][:, c, t * P:(t + 1) * P], wo[:, c, :], start=(c == 0), stop=(c == HC - 1))
                last.then_inc(y_done, 1)

            by_twos(pe, GROUPS, out)


def capacity_experts(nc, w, route, xn_dram, y_dram, const):
    FC = F1 // P
    PB = 2 * SLOTS1 // P
    CH = [(a, min(a + P, SLOTS1)) for a in range(0, SLOTS1, P)]
    with phase(nc) as stack:
        m = stack.memory
        wi = [m.sb(f"wi{s}", [P, HC, F1]) for s in range(2)]
        wo = [m.sb(f"wo{s}", [P, FC, D]) for s in range(2)]
        ids = m.sb("slot_tokens", [P, PB], I32)
        xg = [m.sb(f"slot_rows{n}", [P, D]) for n in range(PB)]
        xt = m.sb("slot_rows_t", [P, HC, 2 * SLOTS1])
        h = [m.sb(f"relu{s}", [P, FC, SLOTS1]) for s in range(2)]
        yr = [m.sb(f"slot_y{s}", [P, len(CH), D]) for s in range(2)]
        w_loaded = m.sems("moe1_w_loaded", 2)
        ids_ready, gathers, gathered = m.sem("slot_ids"), m.sem("slot_gathers"), m.sems("slots_gathered", PB)
        xt_done, xt_ready = m.sem("slot_xt_done"), m.sem("slot_xt_ready")
        h_done, y_done, y_ready = m.sem("m1_h_done"), m.sem("m1_y_done"), m.sem("m1_y_ready")
        h_even, h_odd = m.sem("m1_h_even"), m.sem("m1_h_odd")
        y_stored = m.sems("m1_y_stored", 2)
        ps = stack.enter_context(nc.psum_tensor("ps_moe1", [P, 8, 512], F32))
        block = stack.block.enter_context(nc.Block())
        ps_xt = [ps[:, n, 0:D].rearrange("p (c t) -> p c t", c=HC) for n in range(2)]

        @block.gpsimd
        def _(pool):
            def gather(j):
                pool.wait_ge(xt_done, j * PB + 1)
                nc.gpsimd.tensor_copy(ids[:], route["token"][:, bass.ts(j, PB)]).then_inc(ids_ready, 1)
                pool.wait_ge(ids_ready, j + 1)
                pool.sem_inc(gathers, 1)
                for n in range(PB):
                    nc.gpsimd.indirect_dma_start(xg[n][:], None, xn_dram, bass.IndirectOffsetOnAxis(ap=ids[:, n:n + 1], axis=0)
                                                 ).then_inc(gathered[n], 16)

            with pool.Fori(0, E // 2) as j:
                gather(j)

        @block.tensor
        def _(pe):
            pe.sem_inc(xt_done, 1)
            pe.sem_inc(h_done, 2)
            pe.sem_inc(y_done, 2)

            def up(e, s, turn):
                if s == 0:
                    for n in range(PB):
                        pe.wait_ge(gathered[n], turn * 16 + 16)
                        pe.wait_ge(xt_ready, turn * PB + n + 1)
                        for c in range(HC):
                            last = nc.tensor.transpose(ps_xt[n % 2][:, c, :], xg[n][:, c * P:(c + 1) * P], const["ident"])
                        last.then_inc(xt_done, 1)
                pe.wait_ge(xt_ready, turn * PB + PB + 2)
                pe.wait_ge(w_loaded[s], turn * 32 + 32)
                for f in range(FC):
                    pe.wait_ge(h_even if f % 2 == 0 else h_odd, e * (FC // 2) + f // 2 + 1)
                    for k in range(HC):
                        last = nc.tensor.matmul(ps[:, 2 + f % 2, 0:SLOTS1], wi[s][:, k, f * P:(f + 1) * P],
                                                xt[:, k, s * SLOTS1:(s + 1) * SLOTS1], start=(k == 0), stop=(k == HC - 1))
                    last.then_inc(h_done, 1)

            def down(e, s, turn):
                pe.wait_ge(h_even, e * (FC // 2) + FC // 2 + 1)
                pe.wait_ge(h_odd, e * (FC // 2) + FC // 2 + 1)
                pe.wait_ge(y_ready, reusable(e))
                for n, (a, b) in enumerate(CH):
                    for f in range(FC):
                        last = nc.tensor.matmul(ps[0:b - a, 4 + 2 * s + n // 2, n % 2 * D:n % 2 * D + D], h[s][:, f, a:b], wo[s][:, f, :],
                                                start=(f == 0), stop=(f == FC - 1))
                last.then_inc(y_done, 1)

            software_pipelined(pe, E, up, down)

        @block.scalar
        def _(act):
            act.sem_inc(xt_ready, 2)
            act.sem_inc(h_even, 1)

            def relu(e, s, turn):
                if s == 0:
                    act.wait_ge(h_done, turn * 2 * FC + 2)
                    for n in range(PB):
                        act.wait_ge(xt_done, turn * PB + n + 2)
                        nc.scalar.copy(xt[:, :, n * P:(n + 1) * P], ps_xt[n % 2]).then_inc(xt_ready, 1)
                act.wait_ge(y_done, reusable(e))
                for f in range(0, FC, 2):
                    act.wait_ge(h_done, made(e * FC + f))
                    nc.scalar.activation(h[s][:, f, :], ps[:, 2, 0:SLOTS1], ACT.Relu).then_inc(h_even, 1)

            by_twos(act, E, relu)

        @block.vector
        def _(dve):
            dve.sem_inc(h_odd, 1)
            dve.sem_inc(y_ready, 2)

            def relu(e, s, turn):
                dve.wait_ge(y_done, reusable(e))
                for f in range(1, FC, 2):
                    dve.wait_ge(h_done, made(e * FC + f))
                    nc.vector.tensor_scalar(h[s][:, f, :], ps[:, 3, 0:SLOTS1], 0.0, None, ALU.max).then_inc(h_odd, 1)

            def rows(e, s, turn):
                dve.wait_ge(y_done, made(e))
                dve.wait_ge(y_stored[s], turn * 48 + 48)
                for n, (a, b) in enumerate(CH):
                    last = nc.vector.tensor_copy(yr[s][0:b - a, n, :], ps[0:b - a, 4 + 2 * s + n // 2, n % 2 * D:n % 2 * D + D])
                last.then_inc(y_ready, 1)

            software_pipelined(dve, E, relu, rows)

        @block.sync
        def _(sp):
            for s in range(2):
                sp.sem_inc(y_stored[s], 48)

            def load(e, s, turn):
                sp.wait_ge(y_done, reusable(e))
                sp.dma_start(wi[s][:], w["i"][:, bass.ds(e, 1), :, :].rearrange("p o c n -> p (o c) n")).then_inc(w_loaded[s], 16)
                sp.dma_start(wo[s][:], w["o"][:, bass.ds(e, 1), :, :].rearrange("p o c n -> p (o c) n")).then_inc(w_loaded[s], 16)

            def store(e, s, turn):
                sp.wait_ge(y_ready, made(e))
                for n, (a, b) in enumerate(CH):
                    sp.dma_start(y_dram[bass.ds(e * SLOTS1 + a, b - a), :], yr[s][0:b - a, n, :]).then_inc(y_stored[s], 16)

            software_pipelined(sp, E, load, store)
            for s in range(2):
                sp.wait_ge(y_stored[s], 48 * (E // 2 + 1))


def program(nc, a, out):
    with ExitStack() as stack:
        m = Memory(nc, stack)
        X = m.sb("x", [P, NT, D])
        const = load_constants(nc, m, a)
        route = {
            "gate": m.sb("gate", [P, 2 * NT]),
            "dest": m.sb("dest", [P, 2 * NT], I32),
            "token": m.sb("token", [P, BLOCKS0], I32),
            "expert": m.sb("expert", [P, BLOCKS0], I32),
        }
        xn_dram = nc.dram_tensor("xn_rows_dram", (TOK, D), F32, kind="Internal").ap()
        y_dram = nc.dram_tensor("y_rows_dram", (BLOCKS0 * P, D), F32, kind="Internal").ap()
        tiles = lambda ap: ap.rearrange("(i p) d -> p i d", p=P)
        chunks = lambda ap: ap.rearrange("(c p) n -> p c n", p=P)
        by_expert = lambda ap: ap.rearrange("e (c p) n -> p e c n", p=P)
        with ExitStack() as experts:
            me = Memory(nc, experts)
            ew = {"wg": me.sb("wg", [P, E, HC, I0]), "wu": me.sb("wu", [P, E, HC, I0]), "wd": me.sb("wd", [P, E, I0 // P, D]),
                  "loaded": m.sems("expert_w_loaded", 3)}
            ew["loads"] = [(ew[n], by_expert(a[n])) for n in ("wg", "wu", "wd")]
            with ExitStack() as first:
                xnT = Memory(nc, first).sb("xn_t", [P, HC, TOK])
                norm_and_route(nc, 0, tiles(a["x"]), X, xnT, xn_dram, chunks(a["wr0"]), const["rb0"], const, route)
                scan_branch(nc, X, xnT, {"in": chunks(a["w_in"]), "out": chunks(a["w_out0"]), "b_z": a["b_z"],
                                         "bcd_alog": a["bcd_alog"], "b_out": a["b_out0"]}, const, ew)
                shared_expert(nc, X, xnT, {"g": chunks(a["wg_s"]), "u": chunks(a["wu_s"]), "d": chunks(a["wd_s"])})
            routed_experts(nc, ew, route, xn_dram, y_dram, const)
        combine(nc, 0, X, route, y_dram)
        q_dram = nc.dram_tensor("q_dram", (BATCH * HEADS, len(Q_PARTS), HD, SEQ), BF16, kind="Internal").ap()
        k_dram = nc.dram_tensor("k_dram", (BATCH * HEADS, 3, HD, SEQ), BF16, kind="Internal").ap()
        o_dram = nc.dram_tensor("o_dram", (BATCH * D, SEQ), F32, kind="Internal").ap()
        s_dram = nc.dram_tensor("s_dram", (BATCH * D, SEQ), F32, kind="Internal").ap()
        with ExitStack() as second:
            v = Memory(nc, second).sb("v", [P, NT, D])
            with ExitStack() as inner:
                mi = Memory(nc, inner)
                xnT = mi.sb("xn_t1", [P, HC, TOK])
                wv, bv = mi.sb("w_v", [P, HC, D]), mi.sb("b_v", [P, D])
                wv_loaded = m.sem("wv_loaded")
                with nc.Block() as block:
                    @block.sync
                    def _(sp):
                        sp.dma_start(wv[:], chunks(a["w_qkv"])[:, :, 2 * D:3 * D]).then_inc(wv_loaded, 16)
                        sp.dma_start(bv[:], a["b_v"].to_broadcast([P, D])).then_inc(wv_loaded, 16)
                        sp.wait_ge(wv_loaded, 32)
                norm_and_route(nc, 1, None, X, xnT, xn_dram, chunks(a["wr1"]), None, const, route,
                               {"w": wv, "b": bv, "v": v})
                project_qk(nc, X, xnT, {"qk": chunks(a["w_qkv"])[:, :, 0:2 * D], "b_qk": a["b_qk"], "b_out": a["b_out1"]},
                           q_dram, k_dram)
            attention(nc, v, q_dram, k_dram, o_dram, s_dram, a, const)
        project_out(nc, X, o_dram, s_dram, chunks(a["w_out1"]))
        capacity_experts(nc, {"i": by_expert(a["wi"]), "o": by_expert(a["wo"])}, route, xn_dram, y_dram, const)
        combine(nc, 1, X, route, y_dram, tiles(out))


def load_constants(nc, m, a):
    const = {}
    names = ("ident", "expert_no", "go_on0", "go_on1", "rows_before", "one8", "count_up", "part_no", "tile_no0",
             "tile_no1", "slot_base", "batch_of")
    loaded = m.sem("consts_loaded")
    tri, ones, rb = m.sb("tri", [P, P], BF16), m.sb("ones", [P, P], BF16), m.sb("rb", [P, E])
    const["tri"], const["ones"], const["rb0"] = tri[:], ones[:], rb[:]
    for n in names:
        const[n] = m.sb(n, list(a[n].shape))[:]
    with nc.Block() as block:
        @block.sync
        def _(sp):
            for n in names + ("tri", "ones"):
                sp.dma_start(const[n], a[n]).then_inc(loaded, 16)
            sp.dma_start(rb[:], a["rb"].to_broadcast([P, E])).then_inc(loaded, 16)
            sp.wait_ge(loaded, 16 * (len(names) + 3))
    for n, shape in (("expert_no", [P, NT, E]),):
        const[n] = const[n].rearrange("p (t e) -> p t e", e=E)
    return const


def constant_arrays():
    import numpy as np
    f, bf = np.float32, mybir.dt.np(BF16)
    rows = lambda v: np.ascontiguousarray(np.broadcast_to(np.asarray(v, f).reshape(1, -1), (P, np.asarray(v).size)))
    p = np.arange(P)
    c = {
        "ident": np.eye(P, dtype=f),
        "tri": (p[:, None] < p[None, :]).astype(bf),
        "ones": np.ones((P, P), bf),
        "expert_no": rows(np.tile(np.arange(E), NT)),
        "rows_before": rows(P * np.arange(NT)),
        "one8": rows(np.ones(E)),
        "count_up": rows(np.arange(P)),
        "part_no": p.astype(f).reshape(P, 1),
        "batch_of": (p[:, None] // 32 == np.arange(BATCH)[None, :]).astype(f),
        "slot_base": rows(np.broadcast_to((np.arange(E)[None, :, None] * SLOTS1 + np.arange(G1)[:, None, None] * CAP),
                                          (G1, E, 2 * NT // G1)).reshape(-1)),
    }
    for L, g in ((0, 1), (1, G1)):
        tg = NT // g
        go = np.ones((g * E, 2 * tg))
        go[:, 0] = 0
        c[f"go_on{L}"] = rows(go.reshape(-1))
        c[f"tile_no{L}"] = rows(np.broadcast_to(np.arange(NT).reshape(g, 1, tg), (g, 2, tg)).reshape(-1))
    slope = np.asarray([(2 ** -0.5) ** i for i in range(HEADS)], f)
    cut = lambda v: (lambda h: (h, *(lambda r: (r.astype(bf), (r - r.astype(bf).astype(f)).astype(bf)))((v - h.astype(f)).astype(f))))(v.astype(bf))
    parts = np.stack([x.astype(f) for x in cut(slope)], 1)
    pos = np.arange(SEQ)
    coarse, fine = (pos // P * P).astype(f), (pos % P).astype(f)
    each = np.repeat(parts, 2, 1)
    both = np.tile(np.stack([coarse, fine]), (3, 1))
    q = np.concatenate([np.broadcast_to(both, (HEADS, 6, SEQ)), np.broadcast_to(each[:, :, None], (HEADS, 6, SEQ))], 1)
    k = np.concatenate([np.broadcast_to(-each[:, :, None], (HEADS, 6, SEQ)), np.broadcast_to(both, (HEADS, 6, SEQ))], 1)
    ones = np.ones((HEADS, 2, SEQ), f)
    c["q_bias"] = q.astype(bf)
    c["k_bias"] = np.stack([np.concatenate([k, ones], 1), np.concatenate([-k, ones], 1)], 1).astype(bf)
    ahead = -2 * np.maximum(p[:, None] - p[None, :], 0).astype(f)
    fix = np.stack([x.astype(f) for x in cut(slope[:, None, None] * ahead)], 1)
    c["fix_by_key"] = np.ascontiguousarray(fix.transpose(2, 0, 1, 3)).reshape(P, -1).astype(bf)
    c["fix_by_query"] = np.ascontiguousarray(fix[:, 0].transpose(2, 0, 1)).reshape(P, -1).astype(bf)
    c["ident_bf"] = np.eye(P).astype(bf)
    return c


def kernel(**inputs):
    import numpy as np
    import concourse.bacc as bacc
    from concourse.bass_utils import run_bass_kernel_spmd as run

    t = {k: np.asarray(v) for k, v in inputs.items()}
    flat = lambda v: np.ascontiguousarray(v)
    turned = lambda v: np.ascontiguousarray(np.swapaxes(v, -1, -2))
    b_in = t["L0_attn_b_in"]
    arrays = {
        "x": t["L0_attn_x"].reshape(TOK, D),
        "w_in": t["L0_attn_W_in"],
        "w_out0": t["L0_attn_W_out"],
        "b_z": flat(b_in[D:2 * D].reshape(HC, P).T),
        "bcd_alog": flat(np.concatenate([b_in[2 * D:].reshape(3, N_STATE), t["L0_attn_A_log"].reshape(1, N_STATE)]).T),
        "b_out0": t["L0_attn_b_out"].reshape(1, D),
        "wg_s": turned(t["L0_ffn_Wg_s"]), "wu_s": turned(t["L0_ffn_Wu_s"]), "wd_s": turned(t["L0_ffn_Wd_s"]),
        "wg": turned(t["L0_ffn_Wg"]), "wu": turned(t["L0_ffn_Wu"]), "wd": turned(t["L0_ffn_Wd"]),
        "wr0": turned(t["L0_ffn_Wr"]),
        "rb": t["L0_ffn_rb"].reshape(1, E),
        "w_qkv": t["L1_attn_Wqkv"],
        "b_qk": flat(t["L1_attn_bqkv"][:2 * D].reshape(2 * HC, P).T),
        "b_v": t["L1_attn_bqkv"][2 * D:].reshape(1, D),
        "w_out1": t["L1_attn_Wout"],
        "b_out1": t["L1_attn_bout"].reshape(1, D),
        "wr1": t["L1_ffn_w_router"],
        "wi": t["L1_ffn_wi"],
        "wo": t["L1_ffn_wo"],
    }
    arrays.update(constant_arrays())
    nc = bacc.Bacc("TRN2", target_bir_lowering=False, num_devices=1)
    a = {k: nc.dram_tensor("in_" + k, v.shape, mybir.dt.from_np(v.dtype), kind="ExternalInput").ap() for k, v in arrays.items()}
    out = nc.dram_tensor("out", (TOK, D), F32, kind="ExternalOutput").ap()
    program(nc, a, out)
    result = run(nc, [{"in_" + k: v for k, v in arrays.items()}], core_ids=[0])
    return result.results[0]["out"].reshape(BATCH, SEQ, D)
```

```python
import concourse.bass as bass
from concourse import mybir
from concourse.alu_op_type import AluOpType as ALU
from contextlib import ExitStack

F32 = mybir.dt.float32
BF16 = mybir.dt.bfloat16
I32 = mybir.dt.int32
ACT = mybir.ActivationFunctionType
AX = mybir.AxisListType

P = 128
BATCH, SEQ, D = 4, 1024, 256
TOK = BATCH * SEQ
NT = TOK // P
HC = D // P
N_STATE = 16
E = 8
I0 = 512
F1 = 1024
BLOCKS0 = 2 * NT + E
G1, CAP = 2, 160
SLOTS1 = G1 * CAP
BLOCKS1 = E * SLOTS1 // P
HEADS, HD = 16, 16
EPS = 1e-5


class Chain:

    def __init__(self, engine, sem):
        self.engine, self.sem, self.n = engine, sem, 0

    def __call__(self, instruction):
        self.n += 1
        instruction.then_inc(self.sem, 1)
        self.engine.wait_ge(self.sem, self.n)


class Memory:

    def __init__(self, nc, stack):
        self.nc, self.stack, self.semaphores = nc, stack, []

    def sb(self, name, shape, dt=F32):
        return self.stack.enter_context(self.nc.sbuf_tensor(name, shape, dt))

    def sem(self, name):
        self.semaphores.append(self.stack.enter_context(self.nc.semaphore(name)))
        return self.semaphores[-1]

    def sems(self, name, n):
        return [self.sem(f"{name}{i}") for i in range(n)]


def phase(nc):
    return _Phase(nc)


class _Phase(ExitStack):
    def __init__(self, nc):
        super().__init__()
        self.nc, self.memory, self.block = nc, Memory(nc, self), ExitStack()

    def __exit__(self, *error):
        self.block.close()
        if error[0] is None:
            with self.nc.Block() as block:
                @block.sync
                def _(sp):
                    for s in self.memory.semaphores:
                        sp.sem_clear(s)
        return super().__exit__(*error)


def pipelined(engine, count, produce, consume, ahead=1, unroll=2):
    for i in range(ahead):
        produce(i, i % unroll, i // unroll)
    with engine.Fori(0, count // unroll - 1) as j:
        for n in range(unroll):
            produce(j * unroll + (n + ahead), (n + ahead) % unroll, j + (n + ahead) // unroll)
            consume(j * unroll + n, n, j)
    for i in range(count - unroll, count):
        if i + ahead < count:
            produce(i + ahead, (i + ahead) % unroll, (i + ahead) // unroll)
        consume(i, i % unroll, i // unroll)


def software_pipelined(engine, count, produce, consume):
    pipelined(engine, count, produce, consume)


def by_twos(engine, count, step):
    with engine.Fori(0, count // 2) as j:
        step(j * 2, 0, j)
        step(j * 2 + 1, 1, j)


def made(i):
    return i + 3


def reusable(i):
    return i + 1


def stored(turn):
    return turn * 16 + 32


def storable(turn):
    return turn * 16 + 16


def spread(ap, axis, shape):
    return ap.unsqueeze(axis).to_broadcast(shape)


def norm_and_route(nc, L, x_src, X, xnT, xn_dram, wr_src, bias, const, route, v_out=None):
    G = 1 if L == 0 else G1
    TG = NT // G
    NC = 2 * NT
    NCE = E * NC
    NB = BLOCKS0 if L == 0 else BLOCKS1
    with phase(nc) as stack:
        m = stack.memory
        st = m.sb(f"stats{L}", [P, NT, 6])
        sd = m.sb(f"mean_diff{L}", [P, NT])
        mean = m.sb(f"mean{L}", [P, NT])
        var = m.sb(f"var{L}", [P, NT])
        root = m.sb(f"root{L}", [P, NT])
        quot = m.sb(f"quot{L}", [P, NT])
        rstd = m.sb(f"rstd{L}", [P, NT])
        XN = 4
        xn = [m.sb(f"xn_stage{L}_{s}", [P, D]) for s in range(XN)]
        xt = [m.sb(f"xt_stage{L}_{s}", [P, HC, P]) for s in range(2)]
        wr = m.sb(f"w_router{L}", [P, HC, E])
        LG = m.sb(f"logits{L}", [P, NT, E])
        PR = m.sb(f"scores{L}", [P, NT, E])
        A1 = m.sb(f"work_a{L}", [P, NT, E])
        A2 = m.sb(f"work_b{L}", [P, NT, E])
        pick = m.sb(f"pick{L}", [P, NT])
        OH = m.sb(f"onehot{L}", [P, G, E, 2, TG])
        OHb = m.sb(f"onehot_bf{L}", [P, NCE], BF16)
        T = m.sb(f"totals{L}", [P, NCE])
        S = m.sb(f"totals_up_to{L}", [P, NCE])
        R = m.sb(f"rank{L}", [P, NCE])
        over = m.sb(f"count_over{L}", [P, E, NT])
        nblk = m.sb(f"expert_blocks{L}", [P, E])
        ends = m.sb(f"expert_end{L}", [P, E])
        base = m.sb(f"expert_base{L}", [P, E])
        after = m.sb(f"block_after{L}", [P, BLOCKS0, E])
        blk_e = m.sb(f"block_expert_f{L}", [P, BLOCKS0])
        dest = m.sb(f"dest{L}", [P, NC])
        keep = m.sb(f"keep{L}", [P, NC])
        row_i = m.sb(f"row_i{L}", [P, NC], I32)
        lo_i = m.sb(f"row_in_block_i{L}", [P, NC], I32)
        hi_i = m.sb(f"row_block_i{L}", [P, NC], I32)
        lo = m.sb(f"row_in_block{L}", [P, NC])
        hi = m.sb(f"row_block{L}", [P, NC])
        W = 8
        hot_row = [m.sb(f"hot_row{L}_{s}", [P, W, P], BF16) for s in range(2)]
        hot_block = [m.sb(f"hot_block{L}_{s}", [P, W, NB], BF16) for s in range(2)]
        placed = [m.sb(f"hot_block_no{L}_{s}", [P, W, 2, NB], BF16) for s in range(2)]
        zeros = m.sb(f"zeros_bf{L}", [P, 2 * NB], BF16)
        table = T[:, 0:2 * NB].rearrange("p (a b) -> p a b", a=2)
        x_loaded = m.sems(f"x_loaded{L}_", 4)
        wr_loaded, chain = m.sem(f"wr_loaded{L}"), m.sem(f"dve_chain{L}")
        stats_made = m.sem(f"stats_made{L}")
        var_ready, root_ready = m.sem(f"var_ready{L}"), m.sem(f"root_ready{L}")
        xn_ready, xn_stored = m.sem(f"xn_ready{L}"), m.sems(f"xn_stored{L}_", XN)
        xt_done, xt_ready, xt_copied = m.sem(f"xt_done{L}"), m.sem(f"xt_ready{L}"), m.sem(f"xt_copied{L}")
        lg_done, lg_read = m.sem(f"lg_done{L}"), m.sem(f"lg_read{L}")
        exp_wanted, exp_ready = m.sem(f"exp_wanted{L}"), m.sem(f"exp_ready{L}")
        oh_ready, rank_done, blocks_hot = m.sem(f"oh_ready{L}"), m.sem(f"rank_done{L}"), m.sem(f"blocks_hot{L}")
        zeros_ready, hot_ready, hot_used, table_done = (
            m.sem(f"zeros_ready{L}"), m.sem(f"hot_ready{L}"), m.sem(f"hot_used{L}"), m.sem(f"table_done{L}"))
        ps = stack.enter_context(nc.psum_tensor(f"ps_route{L}", [P, 8, 512], F32))
        ps_xt = [ps[:, s, 0:D].rearrange("p (c t) -> p c t", c=HC) for s in range(2)]
        ps_lg = [ps[:, 2 + s, 0:E] for s in range(2)]
        ps_v = [ps[:, 4 + s, 0:D] for s in range(2)]
        ps_rank, ps_total = ps[:, 6, :], ps[:, 7, :]
        ps_table = ps[:, 2, 0:2 * NB]
        block = stack.block.enter_context(nc.Block())

        @block.sync
        def _(sp):
            if x_src is not None:
                n = NT // 4
                for c in range(4):
                    sp.dma_start(X[:, c * n:(c + 1) * n, :], x_src[:, c * n:(c + 1) * n, :]).then_inc(x_loaded[c], 16)
            sp.dma_start(wr[:], wr_src).then_inc(wr_loaded, 16)
            for s in range(XN):
                sp.sem_inc(xn_stored[s], 16)

            def store(i, s, turn):
                sp.wait_ge(xn_ready, i + 1)
                sp.dma_start(xn_dram[bass.ts(i, P), :], xn[s][:]).then_inc(xn_stored[s], 16)

            with sp.Fori(0, NT // XN) as j:
                for s in range(XN):
                    store(j * XN + s, s, j)
            for s in range(XN):
                sp.wait_ge(xn_stored[s], stored(NT // XN - 1))

        @block.tensor
        def _(pe):
            pe.wait_ge(wr_loaded, 16)
            pe.sem_inc(xt_done, 2)
            pe.sem_inc(lg_done, 2)

            def transpose(i, n, turn):
                s = n % 2
                pe.wait_ge(xn_ready, i + 1)
                pe.wait_ge(xt_ready, reusable(i))
                for c in range(HC):
                    last = nc.tensor.transpose(ps_xt[s][:, c, :], xn[n][:, c * P:(c + 1) * P], const["ident"])
                last.then_inc(xt_done, 1)

            def logits(i, n, turn):
                s = n % 2
                pe.wait_ge(xt_ready, made(i))
                pe.wait_ge(lg_read, reusable(i))
                if v_out is not None:
                    for c in range(HC):
                        nc.tensor.matmul(ps_v[s], xt[s][:, c, :], v_out["w"][:, c, :], start=(c == 0), stop=(c == HC - 1))
                for c in range(HC):
                    last = nc.tensor.matmul(ps_lg[s], xt[s][:, c, :], wr[:, c, :], start=(c == 0), stop=(c == HC - 1))
                last.then_inc(lg_done, 1)

            pipelined(pe, NT, transpose, logits, ahead=1, unroll=XN)
            pe.wait_ge(oh_ready, 1)
            nc.tensor.matmul(ps_rank, const["tri"], OHb[:], start=True, stop=True)
            nc.tensor.matmul(ps_total, const["ones"], OHb[:], start=True, stop=True).then_inc(rank_done, 1)
            pe.wait_ge(zeros_ready, 1)
            pe.wait_ge(lg_read, NT + 2)
            nc.tensor.matmul(ps_table, const["ones"], zeros[:], start=True, stop=False)
            pe.sem_inc(hot_used, 2)

            def place(i, s, turn):
                pe.wait_ge(hot_ready, i + 1)
                for w in range(W):
                    last = nc.tensor.matmul(ps_table, hot_row[s][:, w, :], placed[s][:, w, :, :].rearrange("p a b -> p (a b)"),
                                            start=False, stop=False)
                last.then_inc(hot_used, 1)

            by_twos(pe, NC // W, place)
            nc.tensor.matmul(ps_table, const["ones"], zeros[:], start=False, stop=True).then_inc(table_done, 1)

        @block.scalar
        def _(act):
            act.wait_ge(var_ready, 1)
            nc.scalar.activation(root[:], var[:], ACT.Sqrt).then_inc(root_ready, 1)
            act.sem_inc(xt_ready, 2)

            def copy(i, s, turn):
                act.wait_ge(xt_done, made(i))
                act.wait_ge(lg_done, reusable(i))
                act.wait_ge(xt_copied, reusable(i))
                nc.scalar.copy(xt[s][:], ps_xt[s]).then_inc(xt_ready, 1)

            by_twos(act, NT, copy)
            act.wait_ge(exp_wanted, 1)
            nc.scalar.activation(A2[:], LG[:] if L == 0 else A1[:], ACT.Exp, scale=(-1.0 if L == 0 else 1.0)).then_inc(exp_ready, 1)

        @block.gpsimd
        def _(pool):
            pool.sem_inc(xt_copied, 2)

            def copy(i, s, turn):
                pool.wait_ge(xt_ready, made(i))
                nc.gpsimd.tensor_copy(xnT[:, :, bass.ts(i, P)], xt[s][:]).then_inc(xt_copied, 1)

            by_twos(pool, NT, copy)

        @block.vector
        def _(dve):
            V = nc.vector
            step = Chain(dve, chain)
            V.memset(zeros[:], 0.0).then_inc(zeros_ready, 1)
            for c in range(4):
                if x_src is not None:
                    dve.wait_ge(x_loaded[c], 16)
                with dve.Fori(0, 2) as j:
                    for n in range(NT // 8):
                        t = j * (NT // 8) + (c * (NT // 4) + n)
                        last = V.bn_stats(st[:, t, :], X[:, t, :])
                    last.then_inc(stats_made, 1)
            dve.wait_ge(stats_made, 8)
            step(V.tensor_tensor(sd[:], st[:, :, 1], st[:, :, 4], ALU.subtract))
            step(V.tensor_tensor(mean[:], st[:, :, 1], st[:, :, 4], ALU.add))
            step(V.tensor_scalar(mean[:], mean[:], 0.5, None, ALU.mult))
            step(V.tensor_tensor(sd[:], sd[:], sd[:], ALU.mult))
            step(V.tensor_tensor(var[:], st[:, :, 2], st[:, :, 5], ALU.add))
            step(V.tensor_scalar(var[:], var[:], 1.0 / D, EPS, ALU.mult, ALU.add))
            V.scalar_tensor_tensor(var[:], sd[:], 0.25, var[:], ALU.mult, ALU.add).then_inc(var_ready, 1)
            dve.wait_ge(var_ready, 1)
            dve.wait_ge(root_ready, 1)
            step(V.reciprocal(quot[:], root[:]))
            step(V.tensor_tensor(quot[:], quot[:], var[:], ALU.mult))
            step(V.tensor_tensor(root[:], root[:], quot[:], ALU.add))
            step(V.tensor_scalar(root[:], root[:], 0.5, None, ALU.mult))
            step(V.reciprocal(rstd[:], root[:]))
            dve.sem_inc(lg_read, 2)

            def normalise(i, n, turn):
                if not isinstance(i, int) or i >= XN:
                    dve.wait_ge(xt_done, i - XN + 3)
                dve.wait_ge(xn_stored[n], storable(turn))
                V.tensor_scalar(xn[n][:], X[:, i, :], mean[:, bass.ds(i, 1)], rstd[:, bass.ds(i, 1)],
                                ALU.subtract, ALU.mult).then_inc(xn_ready, 1)

            def keep_logits(i, n, turn):
                s = n % 2
                dve.wait_ge(lg_done, made(i))
                if v_out is not None:
                    V.tensor_tensor(v_out["v"][:, i, :], ps_v[s], v_out["b"][:], ALU.add)
                if bias is not None:
                    V.tensor_tensor(LG[:, i, :], ps_lg[s], bias, ALU.add).then_inc(lg_read, 1)
                else:
                    V.tensor_copy(LG[:, i, :], ps_lg[s]).then_inc(lg_read, 1)

            pipelined(dve, NT, normalise, keep_logits, ahead=2, unroll=XN)
            dve.wait_ge(lg_read, NT + 2)
            full = [P, NT, E]
            if L == 0:
                V.memset(pick[:], 0.0).then_inc(exp_wanted, 1)
                dve.wait_ge(exp_ready, 1)
                step(V.tensor_scalar(A1[:], A2[:], 1.0, None, ALU.add))
                step(V.reciprocal(PR[:], A1[:]))
            else:
                step(V.reduce_max(pick[:], LG[:], AX.X))
                V.tensor_tensor(A1[:], LG[:], spread(pick[:], 2, full), ALU.subtract).then_inc(exp_wanted, 1)
                dve.wait_ge(exp_ready, 1)
                step(V.reduce_sum(pick[:], A2[:], AX.X))
                step(V.reciprocal(pick[:], pick[:]))
                step(V.tensor_tensor(PR[:], A2[:], spread(pick[:], 2, full), ALU.mult))
            gate = route["gate"][:].rearrange("p (g k t) -> p g k t", g=G, k=2)
            for k in range(2):
                src = PR if k == 0 else A1
                step(V.reduce_max(pick[:], src[:], AX.X))
                step(V.tensor_copy(gate[:, :, k, :], pick[:].rearrange("p (g t) -> p g t", g=G)))
                step(V.tensor_tensor(A2[:], src[:], spread(pick[:], 2, full), ALU.is_equal))
                step(V.scalar_tensor_tensor(A2[:], A2[:], -64.0, const["expert_no"], ALU.mult, ALU.add))
                step(V.tensor_reduce(pick[:], A2[:], AX.X, ALU.min))
                step(V.tensor_tensor(A2[:], A2[:], spread(pick[:], 2, full), ALU.is_equal))
                for g in range(G):
                    step(V.tensor_copy(OH[:, g, :, k, :], A2[:, g * TG:(g + 1) * TG, :].rearrange("p t e -> p e t")))
                if k == 0:
                    step(V.scalar_tensor_tensor(A1[:], A2[:], -4.0, PR[:], ALU.mult, ALU.add))
            oh = OH[:].rearrange("p g e k t -> p (g e k t)")
            V.tensor_copy(OHb[:], oh).then_inc(oh_ready, 1)
            dve.wait_ge(rank_done, 1)
            step(V.tensor_copy(T[:], ps_total))
            step(V.tensor_tensor_scan(S[:], const[f"go_on{L}"], T[:], 0.0, ALU.mult, ALU.add))
            step(V.tensor_tensor(R[:], S[:], T[:], ALU.subtract))
            step(V.tensor_tensor(R[:], R[:], ps_rank, ALU.add))
            if L == 0:
                counts = S[:].rearrange("p (e c) -> p e c", e=E)[:, :, NC - 1]
                step(V.tensor_tensor(over[:], spread(counts, 2, [P, E, NT]), spread(const["rows_before"], 1, [P, E, NT]), ALU.is_gt))
                step(V.reduce_sum(nblk[:], over[:], AX.X))
                step(V.tensor_tensor_scan(ends[:], const["one8"], nblk[:], 0.0, ALU.mult, ALU.add))
                step(V.tensor_tensor(base[:], ends[:], nblk[:], ALU.subtract))
                step(V.tensor_scalar(base[:], base[:], float(P), None, ALU.mult))
                view = R[:].rearrange("p (e c) -> p e c", e=E)
                step(V.tensor_tensor(view, view, spread(base[:], 2, [P, E, NC]), ALU.add))
                sh = [P, BLOCKS0, E]
                step(V.tensor_tensor(after[:], spread(const["count_up"][:, 0:BLOCKS0], 2, sh), spread(ends[:], 1, sh), ALU.is_ge))
                step(V.reduce_sum(blk_e[:], after[:], AX.X))
                step(V.tensor_scalar(route["expert"][:], blk_e[:], float(E - 1), None, ALU.min))
            else:
                step(V.tensor_tensor(T[:], oh, R[:], ALU.mult))
                for g in range(G):
                    step(V.reduce_sum(keep[:, g * 2 * TG:(g + 1) * 2 * TG],
                                      T[:, g * E * 2 * TG:(g + 1) * E * 2 * TG].rearrange("p (e c) -> p c e", e=E), AX.X))
                step(V.tensor_scalar(keep[:], keep[:], float(CAP), None, ALU.is_lt))
                step(V.tensor_tensor(R[:], R[:], const["slot_base"], ALU.add))
            step(V.tensor_tensor(T[:], oh, R[:], ALU.mult))
            for g in range(G):
                step(V.reduce_sum(dest[:, g * 2 * TG:(g + 1) * 2 * TG],
                                  T[:, g * E * 2 * TG:(g + 1) * E * 2 * TG].rearrange("p (e c) -> p c e", e=E), AX.X))
            if L == 1:
                step(V.tensor_tensor(dest[:], dest[:], keep[:], ALU.mult))
                step(V.tensor_tensor(route["gate"][:], route["gate"][:], keep[:], ALU.mult))
            step(V.tensor_copy(route["dest"][:], dest[:]))
            if L == 1:
                step(V.tensor_scalar(keep[:], keep[:], -8192.0, 8192.0, ALU.mult, ALU.add))
                step(V.tensor_tensor(dest[:], dest[:], keep[:], ALU.add))
            step(V.tensor_copy(row_i[:], dest[:]))
            step(V.tensor_scalar(lo_i[:], row_i[:], P - 1, None, ALU.bitwise_and))
            step(V.tensor_scalar(hi_i[:], row_i[:], 7, None, ALU.logical_shift_right))
            step(V.tensor_copy(lo[:], lo_i[:]))
            step(V.tensor_copy(hi[:], hi_i[:]))

            count_rows = spread(const["count_up"], 1, [P, W, P])
            count_blocks = spread(const["count_up"][:, 0:NB], 1, [P, W, NB])

            def one_hots(i, s, turn):
                dve.wait_ge(hot_used, reusable(i))
                cols = bass.ds(i * W, W)
                V.tensor_tensor(hot_row[s][:], count_rows, spread(lo[:, cols], 2, [P, W, P]), ALU.is_equal)
                V.tensor_tensor(hot_block[s][:], count_blocks, spread(hi[:, cols], 2, [P, W, NB]), ALU.is_equal).then_inc(blocks_hot, 1)
                dve.wait_ge(blocks_hot, i + 1)
                V.tensor_scalar(placed[s][:, :, 0, :], hot_block[s][:], const["part_no"], None, ALU.mult)
                V.tensor_tensor(placed[s][:, :, 1, :], hot_block[s][:], spread(const[f"tile_no{L}"][:, cols], 2, [P, W, NB]),
                                ALU.mult).then_inc(hot_ready, 1)

            by_twos(dve, NC // W, one_hots)
            dve.wait_ge(table_done, 1)
            step(V.tensor_copy(T[:, 0:2 * NB], ps_table))
            step(V.scalar_tensor_tensor(route["token"][:, 0:NB], table[:, 1, :], float(P), table[:, 0, :], ALU.mult, ALU.add))


def scan_branch(nc, X, xnT, w, const, expert_weights):
    HALF = 512
    with phase(nc) as stack:
        m = stack.memory
        wz = m.sb("w_z", [P, HC, D])
        w3 = m.sb("w_bcd", [P, HC, 3, 32])
        wo = m.sb("w_out0", [P, HC, D])
        bz = m.sb("b_z", [P, HC])
        b3 = m.sb("b_bcd_alog", [P, 4])
        bo = m.sb("b_out0", [P, D])
        U = m.sb("u", [P, SEQ])
        V1 = m.sb("abs_u", [P, SEQ])
        V2 = m.sb("exp_u", [P, SEQ])
        Bt = m.sb("b_t", [P, SEQ])
        St = m.sb("state", [P, SEQ])
        Cs = Bt
        negA = m.sb("neg_a", [P, 1])
        YS = m.sb("y_scan", [P, NT])
        gz = [m.sb(f"gelu_z{s}", [P, HC, HALF]) for s in range(2)]
        loaded = m.sem("scan_w_loaded")
        small_loaded = m.sem("bcd_b_loaded")
        cleared, chain = m.sem("scan_cleared"), m.sem("scan_chain")
        bcd_done = m.sem("bcd_done")
        u_ready, abs_ready, act_chain, e_ready, decay_ready = (
            m.sem("u_ready"), m.sem("abs_ready"), m.sem("scan_act_chain"), m.sem("delta_ready"), m.sem("decay_ready"))
        cs_ready, y_done, y_ready = m.sem("cs_ready"), m.sem("y_done"), m.sem("y_ready")
        z_done, z_ready, o_done, o_read = m.sem("z_done"), m.sem("z_ready"), m.sem("gelu_o_done"), m.sem("gelu_o_read")
        x_biased = m.sem("x_biased")
        ps = stack.enter_context(nc.psum_tensor("ps_scan", [P, 8, 512], F32))
        block = stack.block.enter_context(nc.Block())
        GROUPS = TOK // HALF

        @block.sync
        def _(sp):
            sp.wait_ge(cleared, 2)
            for b in range(BATCH):
                sp.dma_start(b3[32 * b:32 * b + N_STATE, :], w["bcd_alog"]).then_inc(small_loaded, 16)
            for f in range(3):
                c0 = 2 * D + f * N_STATE
                sp.dma_start(w3[:, :, f, 0:N_STATE], w["in"][:, :, c0:c0 + N_STATE]).then_inc(loaded, 16)
            sp.dma_start(wz[:], w["in"][:, :, D:2 * D]).then_inc(loaded, 16)
            sp.dma_start(wo[:], w["out"]).then_inc(loaded, 16)
            sp.dma_start(bz[:], w["b_z"]).then_inc(loaded, 16)
            sp.dma_start(bo[:], w["b_out"].to_broadcast([P, D])).then_inc(loaded, 16)
            for (dst, src), sem in zip(expert_weights["loads"], expert_weights["loaded"]):
                sp.dma_start(dst[:], src).then_inc(sem, 16)

        @block.gpsimd
        def _(pool):
            nc.gpsimd.memset(b3[:], 0.0).then_inc(cleared, 1)
            nc.gpsimd.memset(w3[:], 0.0).then_inc(cleared, 1)
            pool.wait_ge(loaded, 7 * 16)
            with pool.Fori(0, NT) as i:
                nc.gpsimd.tensor_tensor(X[:, i, :], X[:, i, :], bo[:], ALU.add).then_inc(x_biased, 1)

        @block.tensor
        def _(pe):
            pe.wait_ge(loaded, 7 * 16)
            for f in range(3):
                for h in range(2):
                    for b in range(BATCH):
                        t0 = b * SEQ + h * HALF
                        for c in range(HC):
                            last = nc.tensor.matmul(ps[32 * b:32 * b + 32, 2 * f + h, :], w3[:, c, f, :],
                                                    xnT[:, c, t0:t0 + HALF], start=(c == 0), stop=(c == HC - 1))
                last.then_inc(bcd_done, 1)
            pe.wait_ge(cs_ready, 1)
            for j in range(SEQ // P):
                last = nc.tensor.matmul(ps[:, 4, 4 * j:4 * j + 4], Cs[:, j * P:(j + 1) * P], const["batch_of"],
                                        start=True, stop=True)
            last.then_inc(y_done, 1)
            pe.wait_ge(y_ready, 1)
            pe.sem_inc(z_done, 2)
            pe.sem_inc(o_done, 2)

            def project(g, s, turn):
                pe.wait_ge(z_ready, reusable(g))
                for c in range(HC):
                    for k in range(HC):
                        last = nc.tensor.matmul(ps[:, 2 * s + c, :], wz[:, k, c * P:(c + 1) * P],
                                                xnT[:, k, bass.ts(g, HALF)], start=(k == 0), stop=(k == HC - 1))
                last.then_inc(z_done, 1)

            def out(g, s, turn):
                pe.wait_ge(z_ready, made(g))
                pe.wait_ge(o_read, reusable(g))
                for t in range(4):
                    for c in range(HC):
                        last = nc.tensor.matmul(ps[:, 4 + 2 * s + t // 2, (t % 2) * D:(t % 2) * D + D],
                                                gz[s][:, c, t * P:(t + 1) * P], wo[:, c, :],
                                                start=(c == 0), stop=(c == HC - 1))
                last.then_inc(o_done, 1)

            software_pipelined(pe, GROUPS, project, out)

        @block.scalar
        def _(act):
            link = Chain(act, act_chain)
            act.wait_ge(small_loaded, 4 * 16)
            link(nc.scalar.activation(negA[:], b3[:, 3:4], ACT.Exp))
            link(nc.scalar.mul(negA[:], negA[:], -1.0))
            act.wait_ge(u_ready, 1)
            link(nc.scalar.activation(V1[:], U[:], ACT.Abs))
            link(nc.scalar.activation(V2[:], V1[:], ACT.Exp, scale=-1.0))
            nc.scalar.activation(V1[:], V2[:], ACT.Ln, bias=1.0).then_inc(abs_ready, 1)
            act.wait_ge(e_ready, 1)
            nc.scalar.activation(V2[:], U[:], ACT.Exp, scale=negA[:]).then_inc(decay_ready, 1)
            act.sem_inc(z_ready, 2)

            def gelu(g, s, turn):
                act.wait_ge(z_done, made(g))
                act.wait_ge(o_done, reusable(g))
                for c in range(HC):
                    last = nc.scalar.activation(gz[s][:, c, :], ps[:, 2 * s + c, :], ACT.Gelu, bias=bz[:, c:c + 1])
                last.then_inc(z_ready, 1)

            by_twos(act, GROUPS, gelu)

        @block.vector
        def _(dve):
            V = nc.vector
            step = Chain(dve, chain)
            dve.wait_ge(small_loaded, 4 * 16)
            dve.wait_ge(bcd_done, 3)
            field = lambda f: ps[:, 2 * f:2 * f + 2, :].rearrange("p a t -> p (a t)")
            V.tensor_scalar(U[:], field(2), b3[:, 2:3], None, ALU.add).then_inc(u_ready, 1)
            step(V.tensor_scalar(Bt[:], field(0), b3[:, 0:1], None, ALU.add))
            dve.wait_ge(abs_ready, 1)
            V.scalar_tensor_tensor(U[:], U[:], 0.0, V1[:], ALU.max, ALU.add).then_inc(e_ready, 1)
            dve.wait_ge(decay_ready, 1)
            step(V.tensor_tensor_scan(St[:], V2[:], Bt[:], 0.0, ALU.mult, ALU.add))
            V.scalar_tensor_tensor(Cs[:], field(1), b3[:, 1:2], St[:], ALU.add, ALU.mult).then_inc(cs_ready, 1)
            dve.wait_ge(y_done, 1)
            V.tensor_copy(YS[:].rearrange("p (b j) -> p b j", b=BATCH),
                          ps[:, 4, 0:NT].rearrange("p (j b) -> p b j", b=BATCH)).then_inc(y_ready, 1)
            dve.wait_ge(y_ready, 1)
            dve.wait_ge(x_biased, NT)
            dve.sem_inc(o_read, 2)

            def add(g, s, turn):
                dve.wait_ge(o_done, made(g))
                for t in range(4):
                    src = ps[:, 4 + 2 * s + t // 2, (t % 2) * D:(t % 2) * D + D]
                    last = V.scalar_tensor_tensor(X[:, g * 4 + t, :], src, YS[:, bass.ds(g * 4 + t, 1)],
                                                  X[:, g * 4 + t, :], ALU.mult, ALU.add)
                last.then_inc(o_read, 1)

            by_twos(dve, GROUPS, add)


def shared_expert(nc, X, xnT, w):
    N = 512
    IC = I0 // P
    GROUPS = TOK // N
    with phase(nc) as stack:
        m = stack.memory
        wg, wu = m.sb("wg_shared", [P, HC, I0]), m.sb("wu_shared", [P, HC, I0])
        wd = m.sb("wd_shared", [P, IC, D])
        sg = [m.sb(f"silu_shared{s}", [P, N]) for s in range(2)]
        hT = [m.sb(f"h_shared{s}", [P, IC, N]) for s in range(2)]
        loaded = m.sem("shared_w_loaded")
        gu_done, silu_ready, h_ready = m.sem("gu_done"), m.sem("silu_ready"), m.sem("h_ready")
        y_done, y_read = m.sem("shared_y_done"), m.sem("shared_y_read")
        ps = stack.enter_context(nc.psum_tensor("ps_shared", [P, 8, 512], F32))
        block = stack.block.enter_context(nc.Block())

        @block.sync
        def _(sp):
            for dst, src in ((wg, w["g"]), (wu, w["u"]), (wd, w["d"])):
                sp.dma_start(dst[:], src).then_inc(loaded, 16)

        @block.tensor
        def _(pe):
            pe.wait_ge(loaded, 48)
            pe.sem_inc(gu_done, 2)
            pe.sem_inc(y_done, 2)

            def up(g, s, turn):
                for i in range(IC):
                    n = g * IC + i
                    pe.wait_ge(h_ready, reusable(n))
                    for bank, wt in ((i % 2, wg), (2 + i % 2, wu)):
                        for k in range(HC):
                            last = nc.tensor.matmul(ps[:, bank, :], wt[:, k, i * P:(i + 1) * P], xnT[:, k, bass.ts(g, N)],
                                                    start=(k == 0), stop=(k == HC - 1))
                    last.then_inc(gu_done, 1)

            def down(g, s, turn):
                pe.wait_ge(h_ready, g * IC + IC + 2)
                pe.wait_ge(y_read, reusable(g))
                for t in range(4):
                    for i in range(IC):
                        last = nc.tensor.matmul(ps[:, 4 + 2 * s + t // 2, (t % 2) * D:(t % 2) * D + D],
                                                hT[s][:, i, t * P:(t + 1) * P], wd[:, i, :], start=(i == 0), stop=(i == IC - 1))
                last.then_inc(y_done, 1)

            software_pipelined(pe, GROUPS, up, down)

        @block.scalar
        def _(act):
            act.sem_inc(silu_ready, 2)

            def silu(g, s, turn):
                for i in range(IC):
                    n = g * IC + i
                    act.wait_ge(gu_done, made(n))
                    act.wait_ge(h_ready, reusable(n))
                    nc.scalar.activation(sg[i % 2][:], ps[:, i % 2, :], ACT.Silu).then_inc(silu_ready, 1)

            by_twos(act, GROUPS, silu)

        @block.vector
        def _(dve):
            V = nc.vector
            dve.sem_inc(h_ready, 2)
            dve.sem_inc(y_read, 2)

            def gated(g, s, turn):
                dve.wait_ge(y_done, reusable(g))
                for i in range(IC):
                    dve.wait_ge(silu_ready, made(g * IC + i))
                    V.tensor_tensor(hT[s][:, i, :], sg[i % 2][:], ps[:, 2 + i % 2, :], ALU.mult).then_inc(h_ready, 1)

            def add(g, s, turn):
                dve.wait_ge(y_done, made(g))
                for t in range(4):
                    src = ps[:, 4 + 2 * s + t // 2, (t % 2) * D:(t % 2) * D + D]
                    last = V.tensor_tensor(X[:, g * 4 + t, :], src, X[:, g * 4 + t, :], ALU.add)
                last.then_inc(y_read, 1)

            software_pipelined(dve, GROUPS, gated, add)


def routed_experts(nc, w, route, xn_dram, y_dram, const):
    IC = I0 // P
    with phase(nc) as stack:
        m = stack.memory
        wg, wu, wd, w_loaded = w["wg"], w["wu"], w["wd"], w["loaded"]
        ids = [m.sb(f"row_tokens{s}", [P, 1], I32) for s in range(2)]
        xg = [m.sb(f"rows{s}", [P, D]) for s in range(2)]
        xt = [m.sb(f"rows_t{s}", [P, HC, P]) for s in range(2)]
        sg = [m.sb(f"silu{s}", [P, I0]) for s in range(2)]
        h = [m.sb(f"hidden{s}", [P, I0]) for s in range(2)]
        ht = [m.sb(f"hidden_t{s}", [P, IC, P]) for s in range(2)]
        yr = [m.sb(f"y_rows{s}", [P, D]) for s in range(2)]
        ids_ready, gathers, gathered = m.sem("ids_ready"), m.sem("gathers"), m.sems("gathered", 2)
        xt_done, xt_ready, g_done, u_done = m.sem("rt_xt_done"), m.sem("rt_xt_ready"), m.sem("rt_g_done"), m.sem("rt_u_done")
        silu_ready, h_ready, ht_done, ht_ready = m.sem("rt_silu"), m.sem("rt_h"), m.sem("rt_ht_done"), m.sem("rt_ht_ready")
        y_done, y_ready, y_stored = m.sem("rt_y_done"), m.sem("rt_y_ready"), m.sems("rt_y_stored", 2)
        ps = stack.enter_context(nc.psum_tensor("ps_routed", [P, 8, 512], F32))
        ps_xt = ps[:, 6, 0:D].rearrange("p (c t) -> p c t", c=HC)
        ps_y = ps[:, 7, 0:D]
        ps_ht = [ps[:, 4 + s, :].rearrange("p (c t) -> p c t", c=IC) for s in range(2)]
        block = stack.block.enter_context(nc.Block())

        @block.sync
        def _(sp):
            for s in range(2):
                sp.sem_inc(y_stored[s], 16)

            def store(i, s, turn):
                sp.wait_ge(y_ready, made(i))
                sp.dma_start(y_dram[bass.ts(i, P), :], yr[s][:]).then_inc(y_stored[s], 16)

            by_twos(sp, BLOCKS0, store)
            for s in range(2):
                sp.wait_ge(y_stored[s], stored(BLOCKS0 // 2 - 1))

        @block.gpsimd
        def _(pool):
            def gather(i, s, turn):
                pool.wait_ge(xt_done, reusable(i))
                nc.gpsimd.tensor_copy(ids[s][:], route["token"][:, bass.ds(i, 1)]).then_inc(ids_ready, 1)
                pool.wait_ge(ids_ready, i + 1)
                pool.sem_inc(gathers, 1)
                nc.gpsimd.indirect_dma_start(xg[s][:], None, xn_dram, bass.IndirectOffsetOnAxis(ap=ids[s][:, 0:1], axis=0)
                                             ).then_inc(gathered[s], 16)

            by_twos(pool, BLOCKS0, gather)

        @block.tensor
        def _(pe):
            pe.sem_inc(xt_done, 2)
            pe.sem_inc(u_done, 2)
            pe.sem_inc(ht_done, 2)
            pe.sem_inc(y_done, 2)

            def turn_rows(i, s, turn):
                pe.wait_ge(gathered[s], turn * 16 + 16)
                pe.wait_ge(xt_ready, i + 2)
                for c in range(HC):
                    last = nc.tensor.transpose(ps_xt[:, c, :], xg[s][:, c * P:(c + 1) * P], const["ident"])
                last.then_inc(xt_done, 1)

            def turn_hidden(i, s, turn):
                pe.wait_ge(h_ready, made(i))
                pe.wait_ge(ht_ready, reusable(i))
                for c in range(IC):
                    last = nc.tensor.transpose(ps_ht[s][:, c, :], h[s][:, c * P:(c + 1) * P], const["ident"])
                last.then_inc(ht_done, 1)

            def up(i, s, turn):
                e = pe.value_load(route["expert"][0:1, bass.ds(i, 1)], min_val=0, max_val=E - 1)
                pe.wait_ge(h_ready, reusable(i))
                pe.wait_ge(xt_ready, made(i))
                for bank, wt, sem in ((s, wg, g_done), (2 + s, wu, u_done)):
                    for k in range(HC):
                        last = nc.tensor.matmul(ps[:, bank, :], xt[s][:, k, :], wt[:, bass.ds(e, 1), k, :],
                                                start=(k == 0), stop=(k == HC - 1))
                    last.then_inc(sem, 1)

            def down(i, s, turn):
                e = pe.value_load(route["expert"][0:1, bass.ds(i, 1)], min_val=0, max_val=E - 1)
                pe.wait_ge(y_ready, i + 2)
                pe.wait_ge(ht_ready, made(i))
                for c in range(IC):
                    last = nc.tensor.matmul(ps_y, ht[s][:, c, :], wd[:, bass.ds(e, 1), c, :], start=(c == 0), stop=(c == IC - 1))
                last.then_inc(y_done, 1)

            turn_rows(0, 0, 0)
            turn_rows(1, 1, 0)
            for n in range(3):
                pe.wait_ge(w_loaded[n], 16)
            up(0, 0, 0)
            with pe.Fori(0, BLOCKS0 // 2 - 1) as j:
                for i, s, turn, before in ((j * 2 + 1, 1, j, j), (j * 2 + 2, 0, j + 1, j)):
                    turn_rows(i + 1, 1 - s, j + 1)
                    turn_hidden(i - 1, 1 - s, before)
                    up(i, s, turn)
                    down(i - 1, 1 - s, before)
            turn_hidden(BLOCKS0 - 2, 0, 0)
            up(BLOCKS0 - 1, 1, 0)
            down(BLOCKS0 - 2, 0, 0)
            turn_hidden(BLOCKS0 - 1, 1, 0)
            down(BLOCKS0 - 1, 1, 0)

        @block.scalar
        def _(act):
            act.sem_inc(xt_ready, 2)
            act.sem_inc(silu_ready, 2)
            act.sem_inc(y_ready, 2)

            def copy_rows(i, s):
                act.wait_ge(xt_done, made(i))
                act.wait_ge(u_done, reusable(i))
                nc.scalar.copy(xt[s][:], ps_xt).then_inc(xt_ready, 1)

            def silu(i, s):
                act.wait_ge(g_done, i + 1)
                act.wait_ge(h_ready, reusable(i))
                nc.scalar.activation(sg[s][:], ps[:, s, :], ACT.Silu).then_inc(silu_ready, 1)

            def copy_result(i, s, turn):
                act.wait_ge(y_done, made(i))
                act.wait_ge(y_stored[s], storable(turn))
                nc.scalar.copy(yr[s][:], ps_y).then_inc(y_ready, 1)

            copy_rows(0, 0)
            copy_rows(1, 1)
            silu(0, 0)
            with act.Fori(0, BLOCKS0 // 2 - 1) as j:
                for i, s in ((j * 2 + 1, 1), (j * 2 + 2, 0)):
                    copy_rows(i + 1, 1 - s)
                    silu(i, s)
                    copy_result(i - 1, 1 - s, j)
            silu(BLOCKS0 - 1, 1)
            copy_result(BLOCKS0 - 2, 0, BLOCKS0 // 2 - 1)
            copy_result(BLOCKS0 - 1, 1, BLOCKS0 // 2 - 1)

        @block.vector
        def _(dve):
            dve.sem_inc(h_ready, 2)
            dve.sem_inc(ht_ready, 2)

            def gated(i, s, turn):
                dve.wait_ge(silu_ready, made(i))
                dve.wait_ge(u_done, made(i))
                dve.wait_ge(ht_done, reusable(i))
                nc.vector.tensor_tensor(h[s][:], sg[s][:], ps[:, 2 + s, :], ALU.mult).then_inc(h_ready, 1)

            def turned(i, s, turn):
                dve.wait_ge(ht_done, made(i))
                dve.wait_ge(y_done, reusable(i))
                nc.vector.tensor_copy(ht[s][:], ps_ht[s]).then_inc(ht_ready, 1)

            gated(0, 0, 0)
            with dve.Fori(0, BLOCKS0 // 2 - 1) as j:
                for i, s in ((j * 2 + 1, 1), (j * 2 + 2, 0)):
                    turned(i - 1, 1 - s, j)
                    gated(i, s, j)
            turned(BLOCKS0 - 2, 0, 0)
            gated(BLOCKS0 - 1, 1, 0)
            turned(BLOCKS0 - 1, 1, 0)


def combine(nc, X, route, y_dram):
    with phase(nc) as stack:
        m = stack.memory
        ids = [[m.sb(f"from{k}_{s}", [P, 1], I32) for s in range(2)] for k in range(2)]
        rows = [[m.sb(f"back{k}_{s}", [P, D]) for s in range(2)] for k in range(2)]
        part = [m.sb(f"part{s}", [P, D]) for s in range(2)]
        ids_ready, gathers = m.sem("back_ids"), m.sem("back_gathers")
        gathered = [m.sems(f"back{k}_", 2) for k in range(2)]
        first_ready, used = m.sem("first_added"), m.sem("back_used")
        block = stack.block.enter_context(nc.Block())

        @block.gpsimd
        def _(pool):
            def gather(i, s, turn):
                pool.wait_ge(used, reusable(i))
                for k in range(2):
                    last = nc.gpsimd.tensor_copy(ids[k][s][:], route["dest"][:, bass.ds(i + k * NT, 1)])
                last.then_inc(ids_ready, 1)
                pool.wait_ge(ids_ready, i + 1)
                pool.sem_inc(gathers, 1)
                for k in range(2):
                    nc.gpsimd.indirect_dma_start(rows[k][s][:], None, y_dram,
                                                 bass.IndirectOffsetOnAxis(ap=ids[k][s][:, 0:1], axis=0)
                                                 ).then_inc(gathered[k][s], 16)

            by_twos(pool, NT, gather)

        @block.vector
        def _(dve):
            dve.sem_inc(used, 2)

            def add(i, s, turn):
                dve.wait_ge(gathered[0][s], turn * 16 + 16)
                nc.vector.scalar_tensor_tensor(part[s][:], rows[0][s][:], route["gate"][:, bass.ds(i, 1)], X[:, i, :],
                                               ALU.mult, ALU.add).then_inc(first_ready, 1)
                dve.wait_ge(gathered[1][s], turn * 16 + 16)
                dve.wait_ge(first_ready, i + 1)
                nc.vector.scalar_tensor_tensor(X[:, i, :], rows[1][s][:], route["gate"][:, bass.ds(i + NT, 1)], part[s][:],
                                               ALU.mult, ALU.add).then_inc(used, 1)

            by_twos(dve, NT, add)


def project_qk(nc, X, xnT, w, q_dram, k_dram):
    N = 512
    RT = 2 * HC
    GROUPS = TOK // N
    with phase(nc) as stack:
        m = stack.memory
        wqk = m.sb("w_qk", [P, HC, 2 * D])
        bqk = m.sb("b_qk", [P, RT])
        bo = m.sb("b_out1", [P, D])
        full = [m.sb(f"qk_full{s}", [P, RT, N]) for s in range(2)]
        rest = [m.sb(f"qk_rest{s}", [P, RT, N]) for s in range(2)]
        part = [m.sb(f"qk_part{s}", [P, 3, RT, N], BF16) for s in range(2)]
        loaded = m.sem("qk_w_loaded")
        qk_done, full_ready, high_ready, rest_ready, mid_ready, low_ready = (
            m.sem("qk_done"), m.sem("qk_full_ready"), m.sem("qk_high_ready"), m.sem("qk_rest_ready"),
            m.sem("qk_mid_ready"), m.sem("qk_low_ready"))
        qk_stored = m.sems("qk_stored", 2)
        ps = stack.enter_context(nc.psum_tensor("ps_qk", [P, 8, 512], F32))
        block = stack.block.enter_context(nc.Block())
        COPIES = [(q_dram, 0, part_no, row) for row, part_no in enumerate(Q_PARTS)] + \
                 [(k_dram, HC, part_no, row) for row, part_no in enumerate(K_PARTS)]
        PER_STORE = 16 * len(COPIES)

        @block.sync
        def _(sp):
            sp.dma_start(wqk[:], w["qk"]).then_inc(loaded, 16)
            sp.dma_start(bqk[:], w["b_qk"]).then_inc(loaded, 16)
            sp.dma_start(bo[:], w["b_out"].to_broadcast([P, D])).then_inc(loaded, 16)
            for s in range(2):
                sp.sem_inc(qk_stored[s], PER_STORE)

            def store(g, s, turn):
                sp.wait_ge(low_ready, made(g))
                for dram, tile, part_no, row in COPIES:
                    dst = dram[bass.ds(turn * HEADS, HEADS), :, row, s * N:(s + 1) * N].rearrange("(c h) d t -> (h d) c t", c=HC)
                    sp.dma_start(dst, part[s][:, part_no, tile:tile + HC, :]).then_inc(qk_stored[s], 16)

            by_twos(sp, GROUPS, store)
            for s in range(2):
                sp.wait_ge(qk_stored[s], PER_STORE * (GROUPS // 2 + 1))

        @block.tensor
        def _(pe):
            pe.wait_ge(loaded, 48)

            def project(g, s, turn):
                pe.wait_ge(full_ready, reusable(g))
                for r in range(RT):
                    for k in range(HC):
                        last = nc.tensor.matmul(ps[:, s * RT + r, :], wqk[:, k, r * P:(r + 1) * P], xnT[:, k, bass.ts(g, N)],
                                                start=(k == 0), stop=(k == HC - 1))
                last.then_inc(qk_done, 1)

            by_twos(pe, GROUPS, project)

        @block.vector
        def _(dve):
            dve.wait_ge(loaded, 48)
            dve.sem_inc(full_ready, 2)
            dve.sem_inc(low_ready, 2)

            def fill(g, s, turn):
                dve.wait_ge(qk_done, g + 1)
                dve.wait_ge(low_ready, reusable(g))
                for r in range(RT):
                    last = nc.vector.tensor_scalar(full[s][:, r, :], ps[:, s * RT + r, :], bqk[:, r:r + 1],
                                                   0.25 if r < HC else 1.0, ALU.add, ALU.mult)
                last.then_inc(full_ready, 1)

            def low(g, s, turn):
                dve.wait_ge(mid_ready, g + 1)
                nc.vector.tensor_tensor(part[s][:, 2, :, :], rest[s][:], part[s][:, 1, :, :], ALU.subtract).then_inc(low_ready, 1)
                for t in range(4):
                    nc.vector.tensor_tensor(X[:, g * 4 + t, :], X[:, g * 4 + t, :], bo[:], ALU.add)

            software_pipelined(dve, GROUPS, fill, low)

        @block.scalar
        def _(act):
            def parts(g, s, turn):
                act.wait_ge(full_ready, made(g))
                act.wait_ge(qk_stored[s], (turn + 1) * PER_STORE)
                nc.scalar.copy(part[s][:, 0, :, :], full[s][:]).then_inc(high_ready, 1)
                act.wait_ge(rest_ready, g + 1)
                nc.scalar.copy(part[s][:, 1, :, :], rest[s][:]).then_inc(mid_ready, 1)

            by_twos(act, GROUPS, parts)

        @block.gpsimd
        def _(pool):
            def rests(g, s, turn):
                pool.wait_ge(high_ready, g + 1)
                pool.wait_ge(low_ready, reusable(g))
                nc.gpsimd.tensor_tensor(rest[s][:], full[s][:], part[s][:, 0, :, :], ALU.subtract).then_inc(rest_ready, 1)

            by_twos(pool, GROUPS, rests)


Q_PARTS = (0, 0, 0, 1, 1, 2)
K_PARTS = (0, 1, 2, 0, 1, 0)
PART_ROWS = HD * len(Q_PARTS)
BIAS_ROWS, MAX_ROWS = 12, 2
SCORE_ROWS = PART_ROWS + BIAS_ROWS
STACK = SCORE_ROWS + MAX_ROWS
QT = SEQ // P
PAIRS = BATCH * HEADS // 2
assert PAIRS == NT
TG = NT // G1
AHEAD = (3, 3, 2, 3, 3, 2, 0, 0)


def attention(nc, X, v, q_dram, k_dram, o_dram, s_dram, route, y_dram, w, const):
    RING = 3
    with phase(nc) as stack:
        m = stack.memory
        qs = [[m.sb(f"q_stack{s}_{h}", [STACK, SEQ], BF16) for h in range(2)] for s in range(RING)]
        ks = [[[m.sb(f"k_stack{s}_{h}_{side}", [STACK, SEQ], BF16) for side in range(2)] for h in range(2)] for s in range(RING)]
        vs = [m.sb(f"v_stage{s}", [P, 2, QT, 2 * HD]) for s in range(RING)]
        prob = [m.sb(f"prob{n}", [P, 4, 512]) for n in range(2)]
        top = [m.sb(f"top{h}", [P, QT]) for h in range(2)]
        neg = [m.sb(f"neg_top{h}", [P, 2, QT], BF16) for h in range(2)]
        negT = [m.sb(f"neg_top_t{h}", [2 * QT, P], BF16) for h in range(2)]
        osb = [m.sb(f"o_stage{s}", [P, 512]) for s in range(RING)]
        fix_t = m.sb("fix_by_key", [P, HEADS, 3, P], BF16)
        fix = m.sb("fix_by_query", [P, HEADS, P], BF16)
        identb = m.sb("ident_bf", [P, P], BF16)
        tables_loaded = m.sem("attn_tables_loaded")
        stack_loaded = m.sems("stack_loaded", RING)
        ones_ready, v_ready = m.sem("ones_ready"), m.sem("v_staged")
        s1_done, s1_read = m.sem("s1_done"), m.sem("s1_read")
        high_ready, neg_ready = m.sem("top_high_ready"), m.sem("neg_ready")
        turned, turned_read = m.sem("neg_turned"), m.sem("neg_turned_read")
        max_loaded = [m.sems(f"max_loaded{s}_", 2) for s in range(RING)]
        s2_done, exp_ready, pv_done = m.sem("s2_done"), m.sem("exp_ready"), m.sem("pv_done")
        o_read, o_stored = m.sem("o_read"), m.sems("o_stored", RING)
        ids = [[m.sb(f"moe_from{k}_{s}", [P, 1], I32) for s in range(RING)] for k in range(2)]
        rows = [[m.sb(f"moe_rows{k}_{s}", [P, D]) for s in range(RING)] for k in range(2)]
        part = m.sb("moe_part", [P, D])
        ids_ready, gathers = m.sem("moe_ids"), m.sem("moe_gathers")
        gathered = [m.sems(f"moe_gathered{k}_", RING) for k in range(2)]
        first_added, rows_used = m.sem("moe_first_added"), m.sem("moe_rows_used")
        ps = stack.enter_context(nc.psum_tensor("ps_attn", [P, 8, 512], F32))
        ps_turn = ps[0:2 * QT, 7, 0:P // 2].bitcast(BF16)
        block = stack.block.enter_context(nc.Block())
        LOADS = 16 * 2 * (2 + 2 * 2)

        def over_pairs(engine, body, peeled=False):
            if peeled:
                for p in range(RING):
                    body(p, p, 0, True)
            with engine.Fori(1 if peeled else 0, PAIRS // RING) as j:
                for s in range(RING):
                    body(j * RING + s, s, j, True)
            for p in range(PAIRS // RING * RING, PAIRS):
                body(p, p % RING, p // RING, p < PAIRS - 1)

        @block.sync
        def _(sp):
            for dst, src in ((fix_t[:].rearrange("p h a q -> p (h a q)"), w["fix_by_key"]),
                             (fix[:].rearrange("p h q -> p (h q)"), w["fix_by_query"]), (identb[:], w["ident_bf"])):
                sp.dma_start(dst, src).then_inc(tables_loaded, 16)

            def load(p, s):
                for h in range(2):
                    bh = p * 2 + h
                    head = (p % (HEADS // 2)) * 2 + h
                    parts = lambda dram: dram[bass.ds(bh, 1)].rearrange("o d a t -> (o d a) t")
                    bias = lambda table: table.rearrange("o r t -> (o r) t")
                    sp.dma_start(qs[s][h][0:PART_ROWS, :], parts(q_dram)).then_inc(stack_loaded[s], 16)
                    sp.dma_start(qs[s][h][PART_ROWS:SCORE_ROWS, :], bias(w["q_bias"][bass.ds(head, 1)])).then_inc(stack_loaded[s], 16)
                    for side in range(2):
                        sp.dma_start(ks[s][h][side][0:PART_ROWS, :], parts(k_dram)).then_inc(stack_loaded[s], 16)
                        sp.dma_start(ks[s][h][side][PART_ROWS:STACK, :], bias(w["k_bias"][bass.ds(head, 1), side])).then_inc(stack_loaded[s], 16)

            def maxima(p, s, h):
                sp.wait_ge(turned_read, p * 2 + h + 1)
                for n in range(2):
                    sp.dma_start(qs[s][h][SCORE_ROWS + n:SCORE_ROWS + n + 1, :],
                                 negT[h][n * QT:(n + 1) * QT, :]).then_inc(max_loaded[s][h], 16)

            def store(p, s):
                sp.wait_ge(o_read, p + 2)
                for h in range(2):
                    for half in range(2):
                        at = 32 * (2 * h + half)
                        cols = slice(half * 512, (half + 1) * 512)
                        sp.dma_start(o_dram[bass.ds(p * 2 * HD + h * HD, HD), cols], osb[s][at:at + HD, :]).then_inc(o_stored[s], 16)
                        sp.dma_start(s_dram[bass.ds(p * 2 + h, 1), cols], osb[s][at + HD:at + HD + 1, :]).then_inc(o_stored[s], 16)

            for p in range(RING):
                load(p, p)
                sp.sem_inc(o_stored[p], 16 * 8)
            for h in range(2):
                maxima(0, 0, h)

            def body(p, s, turn, more):
                if more:
                    for h in range(2):
                        maxima(p + 1, (s + 1) % RING, h)

            with sp.Fori(0, (PAIRS - RING) // RING) as j:
                for s in range(RING):
                    p = j * RING + s
                    body(p, s, j, True)
                    sp.wait_ge(pv_done, p * QT + QT + 2)
                    load(p + RING, s)
                    store(p, s)
            for p in range((PAIRS - RING) // RING * RING, PAIRS):
                body(p, p % RING, 0, p < PAIRS - 1)
                if p + RING < PAIRS:
                    sp.wait_ge(pv_done, p * QT + QT + 2)
                    load(p + RING, p % RING)
                store(p, p % RING)
            for s in range(RING):
                sp.wait_ge(o_stored[s], 16 * 8 * (1 + len(range(s, PAIRS, RING))))

        @block.gpsimd
        def _(pool):
            for s in range(RING):
                nc.gpsimd.memset(vs[s][:], 1.0).then_inc(ones_ready, 1)
            pool.wait_ge(ones_ready, RING)

            def stage(p, s):
                for h in range(2):
                    col = (p % (HEADS // 2)) * (2 * HD) + h * HD
                    last = nc.gpsimd.tensor_copy(vs[s][:, h, :, 0:HD], v[:, bass.ds((p // (HEADS // 2)) * QT, QT), bass.ds(col, HD)])
                last.then_inc(v_ready, 1)

            stage(0, 0)

            def gather(t, s):
                pool.wait_ge(rows_used, t + 1)
                for k in range(2):
                    last = nc.gpsimd.tensor_copy(ids[k][s][:], route["dest"][:, bass.ds(t + t // TG * TG + k * TG, 1)])
                last.then_inc(ids_ready, 1)
                pool.wait_ge(ids_ready, t + 1)
                pool.sem_inc(gathers, 1)
                for k in range(2):
                    nc.gpsimd.indirect_dma_start(rows[k][s][:], None, y_dram,
                                                 bass.IndirectOffsetOnAxis(ap=ids[k][s][:, 0:1], axis=0)
                                                 ).then_inc(gathered[k][s], 16)

            def body(p, s, turn, more):
                gather(p, s)
                if more:
                    if not isinstance(p, int) or p > 0:
                        pool.wait_ge(pv_done, p * QT - QT + 2)
                    stage(p + 1, (s + 1) % RING)

            over_pairs(pool, body, peeled=True)

        def first_ranges(qb):
            out = []
            for bank in range(2):
                lo, hi, cut = bank * 512, bank * 512 + 512, P * (qb + 1)
                if lo < min(cut, hi):
                    out.append((0, lo, min(cut, hi), bank == qb // 4))
                if max(cut, lo) < hi:
                    out.append((1, max(cut, lo), hi, False))
            return out

        @block.tensor
        def _(pe):
            T = nc.tensor
            pe.wait_ge(tables_loaded, 48)
            pe.sem_inc(pv_done, 2)

            def first(p, s, u):
                h, qb = u // QT, u % QT
                at = 2 * (u % 2)
                n = p * 2 * QT + u
                pe.wait_ge(s1_read, reusable(n))
                opened = set()
                for side, a, b, diagonal in first_ranges(qb):
                    bank = at + a // 512
                    last = T.matmul(ps[:, bank, a % 512:a % 512 + b - a], qs[s][h][0:SCORE_ROWS, qb * P:(qb + 1) * P],
                                    ks[s][h][side][0:SCORE_ROWS, a:b], start=bank not in opened, stop=True, skip_group_check=True)
                    opened.add(bank)
                    if diagonal:
                        head = (p % (HEADS // 2)) * 2 + h
                        last = T.matmul(ps[:, bank, qb % 4 * P:qb % 4 * P + P], identb[:], fix[:, bass.ds(head, 1), :],
                                        start=False, stop=True, skip_group_check=True)
                last.then_inc(s1_done, 1)

            def turn_maxima(p, h):
                pe.wait_ge(neg_ready, p * 2 + h + 1)
                if not isinstance(p, int) or p + h > 0:
                    pe.wait_ge(turned_read, p * 2 + h)
                T.transpose(ps_turn, neg[h][:].rearrange("p a q -> p (a q)"), identb[:]).then_inc(turned, 1)

            def second(p, s, kb, h, half):
                u = (kb * 2 + h) * 2 + half
                bank = 4 + u % 2
                n = p * 4 * QT + u
                pe.wait_ge(exp_ready, reusable(n))
                lo, hi, cut = half * 512, half * 512 + 512, kb * P
                keys = slice(kb * P, (kb + 1) * P)
                opened = False
                if max(cut, lo) < hi:
                    a = max(cut, lo)
                    last = T.matmul(ps[:, bank, a - lo:512], ks[s][h][0][0:STACK, keys], qs[s][h][0:STACK, a:hi],
                                    start=True, stop=True, skip_group_check=True)
                    opened = True
                if lo <= cut < hi:
                    head = (p % (HEADS // 2)) * 2 + h
                    for part in range(1 if h == 0 else 3):
                        last = T.matmul(ps[:, bank, cut - lo:cut - lo + P], identb[:], fix_t[:, bass.ds(head, 1), part, :],
                                        start=False, stop=True, skip_group_check=True)
                if lo < min(cut, hi):
                    b = min(cut, hi)
                    last = T.matmul(ps[:, bank, 0:b - lo], ks[s][h][1][0:STACK, keys], qs[s][h][0:STACK, lo:b],
                                    start=not opened, stop=True, skip_group_check=True)
                last.then_inc(s2_done, 1)

            def values(p, s, kb):
                n = p * QT + kb
                pe.wait_ge(exp_ready, n * 4 + 4 + 2)
                if kb == 0:
                    pe.wait_ge(v_ready, p + 1)
                    pe.wait_ge(o_read, p + 1)
                for h in range(2):
                    for half in range(2):
                        c = 2 * h + half
                        last = T.matmul(ps[32 * c:32 * c + 32, 6, :], vs[s][:, h, kb, :], prob[kb % 2][:, c, :],
                                        start=(kb == 0), stop=(kb == QT - 1))
                last.then_inc(pv_done, 1)

            def both(p, s, turn, more):
                nxt, u = (s + 1) % RING, 0
                if more:
                    pe.wait_ge(stack_loaded[nxt], ((turn + 1) if nxt == 0 else turn) * LOADS + LOADS)
                for h in range(2):
                    pe.wait_ge(max_loaded[s][h], turn * 32 + 32)
                for kb in range(QT):
                    queue = [lambda h=h, half=half: second(p, s, kb, h, half) for h in range(2) for half in range(2)]
                    tiles = AHEAD[kb] if more else 0
                    for i in range(4):
                        queue[i]()
                        if i < tiles:
                            first(p + 1, nxt, u)
                            u += 1
                            if u == QT + 3:
                                turn_maxima(p + 1, 0)
                    if kb == QT - 2 and more:
                        turn_maxima(p + 1, 1)
                    if kb > 0:
                        values(p, s, kb - 1)
                values(p, s, QT - 1)

            pe.wait_ge(stack_loaded[0], LOADS)
            for u in range(2 * QT):
                first(0, 0, u)
            for h in range(2):
                turn_maxima(0, h)
            over_pairs(pe, both)

        @block.scalar
        def _(act):
            act.sem_inc(exp_ready, 2)

            def body(p, s, turn, more):
                for kb in range(QT):
                    for c in range(4):
                        n = p * 4 * QT + kb * 4 + c
                        act.wait_ge(s2_done, n + 1)
                        if c == 0:
                            act.wait_ge(pv_done, reusable(p * QT + kb))
                        nc.scalar.activation(prob[kb % 2][:, c, :], ps[:, 4 + c % 2, :], ACT.Exp).then_inc(exp_ready, 1)

            over_pairs(act, body)

        @block.vector
        def _(dve):
            V = nc.vector
            dve.sem_inc(s1_read, 2)
            dve.sem_inc(o_read, 1)
            dve.sem_inc(rows_used, RING)

            def add_expert_rows(t, s, turn):
                col = t + t // TG * TG
                dve.wait_ge(rows_used, t + RING)
                dve.wait_ge(gathered[0][s], turn * 16 + 16)
                V.scalar_tensor_tensor(part[:], rows[0][s][:], route["gate"][:, bass.ds(col, 1)], X[:, bass.ds(t, 1), :],
                                       ALU.mult, ALU.add).then_inc(first_added, 1)
                dve.wait_ge(gathered[1][s], turn * 16 + 16)
                dve.wait_ge(first_added, t + 1)
                V.scalar_tensor_tensor(X[:, bass.ds(t, 1), :], rows[1][s][:], route["gate"][:, bass.ds(col + TG, 1)], part[:],
                                       ALU.mult, ALU.add).then_inc(rows_used, 1)

            def maximum(p, u):
                n = p * 2 * QT + u
                h = u // QT
                dve.wait_ge(s1_done, n + 1)
                V.reduce_max(top[h][:, u % QT:u % QT + 1], ps[:, 2 * (u % 2):2 * (u % 2) + 2, :].rearrange("p a q -> p (a q)"),
                             AX.X).then_inc(s1_read, 1)

            def negate(p, h):
                dve.wait_ge(s1_read, p * 2 * QT + (h + 1) * QT + 2)
                V.tensor_scalar(neg[h][:, 0, :], top[h][:], -1.0, None, ALU.mult).then_inc(high_ready, 1)
                dve.wait_ge(high_ready, p * 2 + h + 1)
                V.scalar_tensor_tensor(neg[h][:, 1, :], top[h][:], -1.0, neg[h][:, 0, :], ALU.mult, ALU.subtract).then_inc(neg_ready, 1)

            def keep_turned(p, h):
                dve.wait_ge(turned, p * 2 + h + 1)
                V.tensor_copy(negT[h][:], ps_turn).then_inc(turned_read, 1)

            for u in range(2 * QT):
                maximum(0, u)
                if u % QT == QT - 1:
                    negate(0, u // QT)
            for h in range(2):
                keep_turned(0, h)

            def body(p, s, turn, more):
                if more:
                    for u in range(2 * QT):
                        maximum(p + 1, u)
                        if u == QT - 1:
                            negate(p + 1, 0)
                        if u == QT + 3:
                            dve.wait_ge(max_loaded[s][0], turn * 32 + 32)
                            keep_turned(p + 1, 0)
                    negate(p + 1, 1)
                    dve.wait_ge(max_loaded[s][1], turn * 32 + 32)
                    keep_turned(p + 1, 1)
                add_expert_rows(p, s, turn)
                dve.wait_ge(pv_done, p * QT + QT + 2)
                dve.wait_ge(o_stored[s], turn * 128 + 128)
                V.tensor_copy(osb[s][:], ps[:, 6, :]).then_inc(o_read, 1)

            over_pairs(dve, body)


def project_out(nc, X, o_dram, s_dram, r_dram, w, out):
    N = 512
    GROUPS = TOK // N
    HPT = HEADS // HC
    with phase(nc) as stack:
        m = stack.memory
        wo = m.sb("w_out1", [P, HC, D])
        sums = m.sb("o_sums", [P, N])
        inverse = m.sb("o_inverse", [P, N])
        raw = [m.sb(f"o_raw{s}", [P, HC, N]) for s in range(2)]
        inv = [m.sb(f"o_inverse_rows{s}", [P, HC, N]) for s in range(2)]
        o = [m.sb(f"o_t{s}", [P, HC, N]) for s in range(2)]
        w_loaded, sums_loaded, inverse_ready, inverse_stored = (
            m.sem("w_out1_loaded"), m.sem("sums_loaded"), m.sem("inverse_ready"), m.sem("inverse_stored"))
        o_loaded, inv_loaded = m.sems("o_loaded", 2), m.sems("inv_loaded", 2)
        o_ready, y_done, y_read, out_stored = m.sem("o_ready"), m.sem("out1_done"), m.sem("out1_read"), m.sem("out_stored")
        ps = stack.enter_context(nc.psum_tensor("ps_out1", [P, 8, 512], F32))
        block = stack.block.enter_context(nc.Block())

        @block.sync
        def _(sp):
            halves = lambda dram: dram.rearrange("h (a t) -> (h a) t", t=N)
            sp.dma_start(sums[:], halves(s_dram)).then_inc(sums_loaded, 16)
            sp.dma_start(wo[:], w).then_inc(w_loaded, 16)
            sp.wait_ge(inverse_ready, 1)
            sp.dma_start(halves(r_dram), inverse[:]).then_inc(inverse_stored, 16)
            sp.wait_ge(inverse_stored, 16)

            def load(g, s, turn):
                sp.wait_ge(o_ready, reusable(g))
                cols = slice(s * N, (s + 1) * N)
                sp.dma_start(raw[s][:], o_dram[bass.ds(turn * D, D), cols].rearrange("(c p) t -> p c t", p=P)).then_inc(o_loaded[s], 16)
                for c in range(HC):
                    src = r_dram[bass.ds(turn * HEADS + c * HPT, HPT), cols].unsqueeze(1).to_broadcast([HPT, HD, N])
                    sp.dma_start(inv[s][:, c, :], src).then_inc(inv_loaded[s], 16)

            def store(g, s, turn):
                sp.wait_ge(y_read, made(g))
                sp.dma_start(out[:, bass.ts(g, 4), :], X[:, bass.ts(g, 4), :]).then_inc(out_stored, 16)

            pipelined(sp, GROUPS, load, store, ahead=2)
            sp.wait_ge(out_stored, GROUPS * 16)

        @block.vector
        def _(dve):
            V = nc.vector
            dve.sem_inc(o_ready, 2)
            dve.sem_inc(y_read, 2)
            dve.wait_ge(sums_loaded, 16)
            V.reciprocal(inverse[:], sums[:]).then_inc(inverse_ready, 1)

            def divide(g, s, turn):
                dve.wait_ge(o_loaded[s], turn * 16 + 16)
                dve.wait_ge(inv_loaded[s], turn * 32 + 32)
                dve.wait_ge(y_done, reusable(g))
                V.tensor_tensor(o[s][:], raw[s][:], inv[s][:], ALU.mult).then_inc(o_ready, 1)

            def add(g, s, turn):
                dve.wait_ge(y_done, made(g))
                for t in range(4):
                    src = ps[:, 2 * s + t // 2, (t % 2) * D:(t % 2) * D + D]
                    last = V.tensor_tensor(X[:, g * 4 + t, :], src, X[:, g * 4 + t, :], ALU.add)
                last.then_inc(y_read, 1)

            software_pipelined(dve, GROUPS, divide, add)

        @block.tensor
        def _(pe):
            pe.wait_ge(w_loaded, 16)
            pe.sem_inc(y_done, 2)

            def out_rows(g, s, turn):
                pe.wait_ge(o_ready, made(g))
                pe.wait_ge(y_read, reusable(g))
                for t in range(4):
                    for c in range(HC):
                        last = nc.tensor.matmul(ps[:, 2 * s + t // 2, (t % 2) * D:(t % 2) * D + D],
                                                o[s][:, c, t * P:(t + 1) * P], wo[:, c, :], start=(c == 0), stop=(c == HC - 1))
                last.then_inc(y_done, 1)

            by_twos(pe, GROUPS, out_rows)


def capacity_experts(nc, w, route, xn_dram, y_dram, const):
    FC = F1 // P
    PB = 2 * SLOTS1 // P
    CH = [(a, min(a + P, SLOTS1)) for a in range(0, SLOTS1, P)]
    with phase(nc) as stack:
        m = stack.memory
        wi = [m.sb(f"wi{s}", [P, HC, F1]) for s in range(2)]
        wo = [m.sb(f"wo{s}", [P, FC, D]) for s in range(2)]
        ids = m.sb("slot_tokens", [P, PB], I32)
        xg = [m.sb(f"slot_rows{n}", [P, D]) for n in range(PB)]
        xt = m.sb("slot_rows_t", [P, HC, 2 * SLOTS1])
        h = [m.sb(f"relu{s}", [P, FC, SLOTS1]) for s in range(2)]
        yr = [m.sb(f"slot_y{s}", [P, len(CH), D]) for s in range(2)]
        w_loaded = m.sems("moe1_w_loaded", 2)
        ids_ready, gathers, gathered = m.sem("slot_ids"), m.sem("slot_gathers"), m.sems("slots_gathered", PB)
        xt_done, xt_ready = m.sem("slot_xt_done"), m.sem("slot_xt_ready")
        h_done, y_done, y_ready = m.sem("m1_h_done"), m.sem("m1_y_done"), m.sem("m1_y_ready")
        h_even, h_odd = m.sem("m1_h_even"), m.sem("m1_h_odd")
        y_stored = m.sems("m1_y_stored", 2)
        ps = stack.enter_context(nc.psum_tensor("ps_moe1", [P, 8, 512], F32))
        block = stack.block.enter_context(nc.Block())
        ps_xt = [ps[:, n, 0:D].rearrange("p (c t) -> p c t", c=HC) for n in range(2)]

        @block.gpsimd
        def _(pool):
            def gather(j):
                pool.wait_ge(xt_done, j * PB + 1)
                nc.gpsimd.tensor_copy(ids[:], route["token"][:, bass.ts(j, PB)]).then_inc(ids_ready, 1)
                pool.wait_ge(ids_ready, j + 1)
                pool.sem_inc(gathers, 1)
                for n in range(PB):
                    nc.gpsimd.indirect_dma_start(xg[n][:], None, xn_dram, bass.IndirectOffsetOnAxis(ap=ids[:, n:n + 1], axis=0)
                                                 ).then_inc(gathered[n], 16)

            with pool.Fori(0, E // 2) as j:
                gather(j)

        @block.tensor
        def _(pe):
            pe.sem_inc(xt_done, 1)
            pe.sem_inc(h_done, 2)
            pe.sem_inc(y_done, 2)

            def up(e, s, turn):
                if s == 0:
                    for n in range(PB):
                        pe.wait_ge(gathered[n], turn * 16 + 16)
                        pe.wait_ge(xt_ready, turn * PB + n + 1)
                        for c in range(HC):
                            last = nc.tensor.transpose(ps_xt[n % 2][:, c, :], xg[n][:, c * P:(c + 1) * P], const["ident"])
                        last.then_inc(xt_done, 1)
                pe.wait_ge(xt_ready, turn * PB + PB + 2)
                pe.wait_ge(w_loaded[s], turn * 32 + 32)
                for f in range(FC):
                    pe.wait_ge(h_even if f % 2 == 0 else h_odd, e * (FC // 2) + f // 2 + 1)
                    for k in range(HC):
                        last = nc.tensor.matmul(ps[:, 2 + f % 2, 0:SLOTS1], wi[s][:, k, f * P:(f + 1) * P],
                                                xt[:, k, s * SLOTS1:(s + 1) * SLOTS1], start=(k == 0), stop=(k == HC - 1))
                    last.then_inc(h_done, 1)

            def down(e, s, turn):
                pe.wait_ge(h_even, e * (FC // 2) + FC // 2 + 1)
                pe.wait_ge(h_odd, e * (FC // 2) + FC // 2 + 1)
                pe.wait_ge(y_ready, reusable(e))
                for n, (a, b) in enumerate(CH):
                    for f in range(FC):
                        last = nc.tensor.matmul(ps[0:b - a, 4 + 2 * s + n // 2, n % 2 * D:n % 2 * D + D], h[s][:, f, a:b], wo[s][:, f, :],
                                                start=(f == 0), stop=(f == FC - 1))
                last.then_inc(y_done, 1)

            software_pipelined(pe, E, up, down)

        @block.scalar
        def _(act):
            act.sem_inc(xt_ready, 2)
            act.sem_inc(h_even, 1)

            def relu(e, s, turn):
                if s == 0:
                    act.wait_ge(h_done, turn * 2 * FC + 2)
                    for n in range(PB):
                        act.wait_ge(xt_done, turn * PB + n + 2)
                        nc.scalar.copy(xt[:, :, n * P:(n + 1) * P], ps_xt[n % 2]).then_inc(xt_ready, 1)
                act.wait_ge(y_done, reusable(e))
                for f in range(0, FC, 2):
                    act.wait_ge(h_done, made(e * FC + f))
                    nc.scalar.activation(h[s][:, f, :], ps[:, 2, 0:SLOTS1], ACT.Relu).then_inc(h_even, 1)

            by_twos(act, E, relu)

        @block.vector
        def _(dve):
            dve.sem_inc(h_odd, 1)
            dve.sem_inc(y_ready, 2)

            def relu(e, s, turn):
                dve.wait_ge(y_done, reusable(e))
                for f in range(1, FC, 2):
                    dve.wait_ge(h_done, made(e * FC + f))
                    nc.vector.tensor_scalar(h[s][:, f, :], ps[:, 3, 0:SLOTS1], 0.0, None, ALU.max).then_inc(h_odd, 1)

            def rows(e, s, turn):
                dve.wait_ge(y_done, made(e))
                dve.wait_ge(y_stored[s], turn * 48 + 48)
                for n, (a, b) in enumerate(CH):
                    last = nc.vector.tensor_copy(yr[s][0:b - a, n, :], ps[0:b - a, 4 + 2 * s + n // 2, n % 2 * D:n % 2 * D + D])
                last.then_inc(y_ready, 1)

            software_pipelined(dve, E, relu, rows)

        @block.sync
        def _(sp):
            for s in range(2):
                sp.sem_inc(y_stored[s], 48)

            def load(e, s, turn):
                sp.wait_ge(y_done, reusable(e))
                sp.dma_start(wi[s][:], w["i"][:, bass.ds(e, 1), :, :].rearrange("p o c n -> p (o c) n")).then_inc(w_loaded[s], 16)
                sp.dma_start(wo[s][:], w["o"][:, bass.ds(e, 1), :, :].rearrange("p o c n -> p (o c) n")).then_inc(w_loaded[s], 16)

            def store(e, s, turn):
                sp.wait_ge(y_ready, made(e))
                for n, (a, b) in enumerate(CH):
                    sp.dma_start(y_dram[bass.ds(e * SLOTS1 + a, b - a), :], yr[s][0:b - a, n, :]).then_inc(y_stored[s], 16)

            software_pipelined(sp, E, load, store)
            for s in range(2):
                sp.wait_ge(y_stored[s], 48 * (E // 2 + 1))


def program(nc, a, out):
    with ExitStack() as stack:
        m = Memory(nc, stack)
        X = m.sb("x", [P, NT, D])
        const = load_constants(nc, m, a)
        route = {
            "gate": m.sb("gate", [P, 2 * NT]),
            "dest": m.sb("dest", [P, 2 * NT], I32),
            "token": m.sb("token", [P, BLOCKS0], I32),
            "expert": m.sb("expert", [P, BLOCKS0], I32),
        }
        xn_dram = nc.dram_tensor("xn_rows_dram", (TOK, D), F32, kind="Internal").ap()
        y_dram = nc.dram_tensor("y_rows_dram", (BLOCKS0 * P, D), F32, kind="Internal").ap()
        tiles = lambda ap: ap.rearrange("(i p) d -> p i d", p=P)
        chunks = lambda ap: ap.rearrange("(c p) n -> p c n", p=P)
        by_expert = lambda ap: ap.rearrange("e (c p) n -> p e c n", p=P)
        with ExitStack() as experts:
            me = Memory(nc, experts)
            ew = {"wg": me.sb("wg", [P, E, HC, I0]), "wu": me.sb("wu", [P, E, HC, I0]), "wd": me.sb("wd", [P, E, I0 // P, D]),
                  "loaded": m.sems("expert_w_loaded", 3)}
            ew["loads"] = [(ew[n], by_expert(a[n])) for n in ("wg", "wu", "wd")]
            with ExitStack() as first:
                xnT = Memory(nc, first).sb("xn_t", [P, HC, TOK])
                norm_and_route(nc, 0, tiles(a["x"]), X, xnT, xn_dram, chunks(a["wr0"]), const["rb0"], const, route)
                scan_branch(nc, X, xnT, {"in": chunks(a["w_in"]), "out": chunks(a["w_out0"]), "b_z": a["b_z"],
                                         "bcd_alog": a["bcd_alog"], "b_out": a["b_out0"]}, const, ew)
                shared_expert(nc, X, xnT, {"g": chunks(a["wg_s"]), "u": chunks(a["wu_s"]), "d": chunks(a["wd_s"])})
            routed_experts(nc, ew, route, xn_dram, y_dram, const)
        combine(nc, X, route, y_dram)
        q_dram = nc.dram_tensor("q_dram", (BATCH * HEADS, HD, len(Q_PARTS), SEQ), BF16, kind="Internal").ap()
        k_dram = nc.dram_tensor("k_dram", (BATCH * HEADS, HD, len(K_PARTS), SEQ), BF16, kind="Internal").ap()
        o_dram = nc.dram_tensor("o_dram", (BATCH * D, SEQ), F32, kind="Internal").ap()
        s_dram = nc.dram_tensor("s_dram", (BATCH * HEADS, SEQ), F32, kind="Internal").ap()
        r_dram = nc.dram_tensor("r_dram", (BATCH * HEADS, SEQ), F32, kind="Internal").ap()
        with ExitStack() as second:
            v = Memory(nc, second).sb("v", [P, NT, D])
            with ExitStack() as inner:
                mi = Memory(nc, inner)
                xnT = mi.sb("xn_t1", [P, HC, TOK])
                wv, bv = mi.sb("w_v", [P, HC, D]), mi.sb("b_v", [P, D])
                wv_loaded = m.sem("wv_loaded")
                with nc.Block() as block:
                    @block.sync
                    def _(sp):
                        sp.dma_start(wv[:], chunks(a["w_qkv"])[:, :, 2 * D:3 * D]).then_inc(wv_loaded, 16)
                        sp.dma_start(bv[:], a["b_v"].to_broadcast([P, D])).then_inc(wv_loaded, 16)
                        sp.wait_ge(wv_loaded, 32)
                norm_and_route(nc, 1, None, X, xnT, xn_dram, chunks(a["wr1"]), None, const, route,
                               {"w": wv, "b": bv, "v": v})
                project_qk(nc, X, xnT, {"qk": chunks(a["w_qkv"])[:, :, 0:2 * D], "b_qk": a["b_qk"], "b_out": a["b_out1"]},
                           q_dram, k_dram)
            capacity_experts(nc, {"i": by_expert(a["wi"]), "o": by_expert(a["wo"])}, route, xn_dram, y_dram, const)
            attention(nc, X, v, q_dram, k_dram, o_dram, s_dram, route, y_dram, a, const)
        project_out(nc, X, o_dram, s_dram, r_dram, chunks(a["w_out1"]), tiles(out))


def load_constants(nc, m, a):
    const = {}
    names = ("ident", "expert_no", "go_on0", "go_on1", "rows_before", "one8", "count_up", "part_no", "tile_no0",
             "tile_no1", "slot_base", "batch_of")
    loaded = m.sem("consts_loaded")
    tri, ones, rb = m.sb("tri", [P, P], BF16), m.sb("ones", [P, P], BF16), m.sb("rb", [P, E])
    const["tri"], const["ones"], const["rb0"] = tri[:], ones[:], rb[:]
    for n in names:
        const[n] = m.sb(n, list(a[n].shape))[:]
    with nc.Block() as block:
        @block.sync
        def _(sp):
            for n in names + ("tri", "ones"):
                sp.dma_start(const[n], a[n]).then_inc(loaded, 16)
            sp.dma_start(rb[:], a["rb"].to_broadcast([P, E])).then_inc(loaded, 16)
            sp.wait_ge(loaded, 16 * (len(names) + 3))
    for n, shape in (("expert_no", [P, NT, E]),):
        const[n] = const[n].rearrange("p (t e) -> p t e", e=E)
    return const


def constant_arrays():
    import numpy as np
    f, bf = np.float32, mybir.dt.np(BF16)
    rows = lambda v: np.ascontiguousarray(np.broadcast_to(np.asarray(v, f).reshape(1, -1), (P, np.asarray(v).size)))
    p = np.arange(P)
    c = {
        "ident": np.eye(P, dtype=f),
        "tri": (p[:, None] < p[None, :]).astype(bf),
        "ones": np.ones((P, P), bf),
        "expert_no": rows(np.tile(np.arange(E), NT)),
        "rows_before": rows(P * np.arange(NT)),
        "one8": rows(np.ones(E)),
        "count_up": rows(np.arange(P)),
        "part_no": p.astype(f).reshape(P, 1),
        "batch_of": (p[:, None] // 32 == np.arange(BATCH)[None, :]).astype(f),
        "slot_base": rows(np.broadcast_to((np.arange(E)[None, :, None] * SLOTS1 + np.arange(G1)[:, None, None] * CAP),
                                          (G1, E, 2 * NT // G1)).reshape(-1)),
    }
    for L, g in ((0, 1), (1, G1)):
        tg = NT // g
        go = np.ones((g * E, 2 * tg))
        go[:, 0] = 0
        c[f"go_on{L}"] = rows(go.reshape(-1))
        c[f"tile_no{L}"] = rows(np.broadcast_to(np.arange(NT).reshape(g, 1, tg), (g, 2, tg)).reshape(-1))
    slope = np.asarray([(2 ** -0.5) ** i for i in range(HEADS)], f)
    cut = lambda v: (lambda h: (h, *(lambda r: (r.astype(bf), (r - r.astype(bf).astype(f)).astype(bf)))((v - h.astype(f)).astype(f))))(v.astype(bf))
    parts = np.stack([x.astype(f) for x in cut(slope)], 1)
    pos = np.arange(SEQ)
    coarse, fine = (pos // P * P).astype(f), (pos % P).astype(f)
    each = np.repeat(parts, 2, 1)
    both = np.tile(np.stack([coarse, fine]), (3, 1))
    q = np.concatenate([np.broadcast_to(both, (HEADS, 6, SEQ)), np.broadcast_to(each[:, :, None], (HEADS, 6, SEQ))], 1)
    k = np.concatenate([np.broadcast_to(-each[:, :, None], (HEADS, 6, SEQ)), np.broadcast_to(both, (HEADS, 6, SEQ))], 1)
    ones = np.ones((HEADS, 2, SEQ), f)
    c["q_bias"] = q.astype(bf)
    c["k_bias"] = np.stack([np.concatenate([k, ones], 1), np.concatenate([-k, ones], 1)], 1).astype(bf)
    ahead = -2 * np.maximum(p[:, None] - p[None, :], 0).astype(f)
    fix = np.stack([x.astype(f) for x in cut(slope[:, None, None] * ahead)], 1)
    c["fix_by_key"] = np.ascontiguousarray(fix.transpose(2, 0, 1, 3)).reshape(P, -1).astype(bf)
    c["fix_by_query"] = np.ascontiguousarray(fix[:, 0].transpose(2, 0, 1)).reshape(P, -1).astype(bf)
    c["ident_bf"] = np.eye(P).astype(bf)
    return c


def kernel(**inputs):
    import numpy as np
    import concourse.bacc as bacc
    from concourse.bass_utils import run_bass_kernel_spmd as run

    t = {k: np.asarray(v) for k, v in inputs.items()}
    flat = lambda v: np.ascontiguousarray(v)
    turned = lambda v: np.ascontiguousarray(np.swapaxes(v, -1, -2))
    b_in = t["L0_attn_b_in"]
    arrays = {
        "x": t["L0_attn_x"].reshape(TOK, D),
        "w_in": t["L0_attn_W_in"],
        "w_out0": t["L0_attn_W_out"],
        "b_z": flat(b_in[D:2 * D].reshape(HC, P).T),
        "bcd_alog": flat(np.concatenate([b_in[2 * D:].reshape(3, N_STATE), t["L0_attn_A_log"].reshape(1, N_STATE)]).T),
        "b_out0": t["L0_attn_b_out"].reshape(1, D),
        "wg_s": turned(t["L0_ffn_Wg_s"]), "wu_s": turned(t["L0_ffn_Wu_s"]), "wd_s": turned(t["L0_ffn_Wd_s"]),
        "wg": turned(t["L0_ffn_Wg"]), "wu": turned(t["L0_ffn_Wu"]), "wd": turned(t["L0_ffn_Wd"]),
        "wr0": turned(t["L0_ffn_Wr"]),
        "rb": t["L0_ffn_rb"].reshape(1, E),
        "w_qkv": t["L1_attn_Wqkv"],
        "b_qk": flat(t["L1_attn_bqkv"][:2 * D].reshape(2 * HC, P).T),
        "b_v": t["L1_attn_bqkv"][2 * D:].reshape(1, D),
        "w_out1": t["L1_attn_Wout"],
        "b_out1": t["L1_attn_bout"].reshape(1, D),
        "wr1": t["L1_ffn_w_router"],
        "wi": t["L1_ffn_wi"],
        "wo": t["L1_ffn_wo"],
    }
    arrays.update(constant_arrays())
    nc = bacc.Bacc("TRN2", target_bir_lowering=False, num_devices=1)
    a = {k: nc.dram_tensor("in_" + k, v.shape, mybir.dt.from_np(v.dtype), kind="ExternalInput").ap() for k, v in arrays.items()}
    out = nc.dram_tensor("out", (TOK, D), F32, kind="ExternalOutput").ap()
    program(nc, a, out)
    result = run(nc, [{"in_" + k: v for k, v in arrays.items()}], core_ids=[0])
    return result.results[0]["out"].reshape(BATCH, SEQ, D)
```

```python
import concourse.bass as bass
from concourse import mybir
from concourse.alu_op_type import AluOpType as ALU
from contextlib import ExitStack

F32 = mybir.dt.float32
BF16 = mybir.dt.bfloat16
F22 = mybir.dt.float32r
I32 = mybir.dt.int32
ACT = mybir.ActivationFunctionType
AX = mybir.AxisListType

P = 128
BATCH, SEQ, D = 4, 1024, 256
TOK = BATCH * SEQ
NT = TOK // P
HC = D // P
N_STATE = 16
E = 8
I0 = 512
F1 = 1024
BLOCKS0 = 2 * NT + E
G1, CAP = 2, 160
SLOTS1 = G1 * CAP
BLOCKS1 = E * SLOTS1 // P
HEADS, HD = 16, 16
EPS = 1e-5


class Chain:

    def __init__(self, engine, sem):
        self.engine, self.sem, self.n = engine, sem, 0

    def __call__(self, instruction):
        self.n += 1
        instruction.then_inc(self.sem, 1)
        self.engine.wait_ge(self.sem, self.n)


class Memory:

    def __init__(self, nc, stack):
        self.nc, self.stack, self.semaphores = nc, stack, []

    def sb(self, name, shape, dt=F32):
        return self.stack.enter_context(self.nc.sbuf_tensor(name, shape, dt))

    def sem(self, name):
        self.semaphores.append(self.stack.enter_context(self.nc.semaphore(name)))
        return self.semaphores[-1]

    def sems(self, name, n):
        return [self.sem(f"{name}{i}") for i in range(n)]


class Phase(ExitStack):

    def __init__(self, nc, signals):
        super().__init__()
        self.memory, self.block = Memory(nc, self), ExitStack()
        self.memory.sem = signals.sem
        self.memory.gather_sems = signals.gather_sems

    def __exit__(self, *error):
        self.block.close()
        return super().__exit__(*error)


def phase(nc, signals):
    return Phase(nc, signals)


class Signals(ExitStack):

    def __init__(self, nc, whole, clear=True):
        super().__init__()
        self.nc, self.memory, self.clear, self.gather_sems = nc, Memory(nc, self), clear, whole.sems

    def sem(self, name):
        return self.memory.sem(name)

    def __exit__(self, *error):
        if error[0] is None and self.clear:
            with self.nc.Block() as block:
                @block.sync
                def _(sp):
                    for s in self.memory.semaphores:
                        sp.sem_clear(s)
        return super().__exit__(*error)


def pipelined(engine, count, produce, consume, ahead=1, unroll=2, first=0):
    for i in range(first, first + ahead):
        produce(i, i % unroll, i // unroll)
    with engine.Fori(0, count // unroll - 1) as j:
        for n in range(unroll):
            k = first + n + ahead
            produce(j * unroll + k, k % unroll, j + k // unroll)
            consume(j * unroll + (first + n), n, j + first // unroll)
    for i in range(first + count - unroll, first + count):
        if i + ahead < first + count:
            produce(i + ahead, (i + ahead) % unroll, (i + ahead) // unroll)
        consume(i, i % unroll, i // unroll)


def software_pipelined(engine, count, produce, consume):
    pipelined(engine, count, produce, consume)


def by_twos(engine, count, step, first=0):
    with engine.Fori(0, count // 2) as j:
        step(j * 2 + first, 0, j + first // 2)
        step(j * 2 + (first + 1), 1, j + first // 2)


def made(i):
    return i + 3


def reusable(i):
    return i + 1


def stored(turn):
    return turn * 16 + 32


def storable(turn):
    return turn * 16 + 16


PRODUCTS = (("high", "high"), ("high", "low"), ("low", "high"))


def spread(ap, axis, shape):
    return ap.unsqueeze(axis).to_broadcast(shape)


def norm_and_route(nc, signals, L, x_src, X, st, xnT, xn_dram, wr_src, bias, const, route, v_out=None, tables=None):
    G = 1 if L == 0 else G1
    TG = NT // G
    NC = 2 * NT
    NCE = E * NC
    NB = BLOCKS0 if L == 0 else BLOCKS1
    with phase(nc, signals) as stack:
        m = stack.memory
        sd = m.sb(f"mean_diff{L}", [P, NT])
        mean = m.sb(f"mean{L}", [P, NT])
        var = m.sb(f"var{L}", [P, NT])
        root = m.sb(f"root{L}", [P, NT])
        quot = m.sb(f"quot{L}", [P, NT])
        rstd = m.sb(f"rstd{L}", [P, NT])
        CHUNKS = 4 if L == 0 else 1
        CT = NT // CHUNKS
        XN = 4
        xn = [m.sb(f"xn_stage{L}_{s}", [P, D]) for s in range(XN)]
        xt = [m.sb(f"xt_stage{L}_{s}", [P, HC, P]) for s in range(2)]
        wr = m.sb(f"w_router{L}", [P, HC, E])
        LG = m.sb(f"logits{L}", [P, NT, E])
        PR = m.sb(f"scores{L}", [P, NT, E])
        A1 = m.sb(f"work_a{L}", [P, NT, E])
        A2 = m.sb(f"work_b{L}", [P, NT, E])
        pick = m.sb(f"pick{L}", [P, NT])
        OH = m.sb(f"onehot{L}", [P, G, E, 2, TG])
        OHb = m.sb(f"onehot_bf{L}", [P, NCE], BF16)
        T = m.sb(f"totals{L}", [P, NCE])
        S = m.sb(f"totals_up_to{L}", [P, NCE])
        R = m.sb(f"rank{L}", [P, NCE])
        over = m.sb(f"count_over{L}", [P, E, NT])
        nblk = m.sb(f"expert_blocks{L}", [P, E])
        ends = m.sb(f"expert_end{L}", [P, E])
        base = m.sb(f"expert_base{L}", [P, E])
        after = m.sb(f"block_after{L}", [P, BLOCKS0, E])
        blk_e = m.sb(f"block_expert_f{L}", [P, BLOCKS0])
        dest = m.sb(f"dest{L}", [P, NC])
        keep = m.sb(f"keep{L}", [P, NC])
        row_i = m.sb(f"row_i{L}", [P, NC], I32)
        lo_i = m.sb(f"row_in_block_i{L}", [P, NC], I32)
        hi_i = m.sb(f"row_block_i{L}", [P, NC], I32)
        lo = m.sb(f"row_in_block{L}", [P, NC])
        hi = m.sb(f"row_block{L}", [P, NC])
        W = 8
        hot_row = [m.sb(f"hot_row{L}_{s}", [P, W, P], BF16) for s in range(2)]
        hot_block = [m.sb(f"hot_block{L}_{s}", [P, W, NB], BF16) for s in range(2)]
        placed = [m.sb(f"hot_block_no{L}_{s}", [P, W, 2, NB], BF16) for s in range(2)]
        zeros = m.sb(f"zeros_bf{L}", [P, 2 * NB], BF16)
        table = T[:, 0:2 * NB].rearrange("p (a b) -> p a b", a=2)
        x_loaded = m.sems(f"x_loaded{L}_", CHUNKS)
        if L == 0:
            first_tables, rest_tables = m.sem("first_tables_loaded"), m.sem("rest_tables_loaded")
        if v_out is not None:
            wv_loaded = m.sem("wv_loaded")
        wr_loaded, chain = m.sem(f"wr_loaded{L}"), m.sem(f"dve_chain{L}")
        stats_made = m.sem(f"stats_made{L}")
        var_ready, root_ready = m.sem(f"var_ready{L}"), m.sem(f"root_ready{L}")
        xn_ready, xn_stored = m.sem(f"xn_ready{L}"), m.sems(f"xn_stored{L}_", XN)
        xt_done, xt_ready, xt_kept = m.sem(f"xt_done{L}"), m.sem(f"xt_ready{L}"), m.sem(f"xt_kept{L}")
        lg_done, lg_read = m.sem(f"lg_done{L}"), m.sem(f"lg_read{L}")
        exp_wanted, exp_ready = m.sem(f"exp_wanted{L}"), m.sem(f"exp_ready{L}")
        oh_ready, rank_done, blocks_hot = m.sem(f"oh_ready{L}"), m.sem(f"rank_done{L}"), m.sem(f"blocks_hot{L}")
        zeros_ready, hot_ready, hot_used, table_done = (
            m.sem(f"zeros_ready{L}"), m.sem(f"hot_ready{L}"), m.sem(f"hot_used{L}"), m.sem(f"table_done{L}"))
        ps = stack.enter_context(nc.psum_tensor(f"ps_route{L}", [P, 8, 512], F32))
        ps_xt = [ps[:, s, 0:D].rearrange("p (c t) -> p c t", c=HC) for s in range(2)]
        ps_lg = [ps[:, 2 + s, 0:E] for s in range(2)]
        ps_v = [ps[:, 4 + s, 0:D] for s in range(2)]
        ps_rank, ps_total = ps[:, 6, :], ps[:, 7, :]
        ps_table = ps[:, 2, 0:2 * NB]
        block = stack.block.enter_context(nc.Block())

        @block.sync
        def _(sp):
            def load_x(c):
                part = slice(c * CT, (c + 1) * CT)
                sp.dma_start(X[:, part, :], x_src[:, part, :]).then_inc(x_loaded[c], 16)

            if L == 0:
                load_x(0)
                for dst, src in tables["first"]:
                    sp.dma_start(dst, src).then_inc(first_tables, 16)
            sp.dma_start(wr[:], wr_src).then_inc(wr_loaded, 16)
            if v_out is not None:
                for dst, src in v_out["loads"]:
                    sp.dma_start(dst, src).then_inc(wv_loaded, 16)
            if L == 0:
                for c in range(1, CHUNKS):
                    load_x(c)
                for dst, src in tables["rest"]:
                    sp.dma_start(dst, src).then_inc(rest_tables, 16)
            for s in range(XN):
                sp.sem_inc(xn_stored[s], 16)

            def store(i, s, turn):
                sp.wait_ge(xn_ready, i + 1)
                sp.dma_start(xn_dram[bass.ts(i, P), :], xn[s][:]).then_inc(xn_stored[s], 16)

            with sp.Fori(0, NT // XN) as j:
                for s in range(XN):
                    store(j * XN + s, s, j)
            for s in range(XN):
                sp.wait_ge(xn_stored[s], stored(NT // XN - 1))

        @block.tensor
        def _(pe):
            pe.wait_ge(wr_loaded, 16)
            if v_out is not None:
                pe.wait_ge(wv_loaded, 32)
            if L == 0:
                pe.wait_ge(first_tables, 16 * len(tables["first"]))
            pe.sem_inc(xt_done, 2)
            pe.sem_inc(lg_done, 2)

            def transpose(i, n, turn):
                s = n % 2
                pe.wait_ge(xn_ready, i + 1)
                pe.wait_ge(xt_kept, reusable(i))
                for c in range(HC):
                    last = nc.tensor.transpose(ps_xt[s][:, c, :], xn[n][:, c * P:(c + 1) * P], const["ident"])
                last.then_inc(xt_done, 1)

            def logits(i, n, turn):
                s = n % 2
                pe.wait_ge(xt_ready, made(i))
                pe.wait_ge(lg_read, reusable(i))
                if v_out is not None:
                    for c in range(HC):
                        nc.tensor.matmul(ps_v[s], xt[s][:, c, :], v_out["w"][:, c, :], start=(c == 0), stop=(c == HC - 1))
                for c in range(HC):
                    last = nc.tensor.matmul(ps_lg[s], xt[s][:, c, :], wr[:, c, :], start=(c == 0), stop=(c == HC - 1))
                last.then_inc(lg_done, 1)

            for c in range(CHUNKS):
                pipelined(pe, CT, transpose, logits, unroll=XN, first=c * CT)
            if L == 0:
                pe.wait_ge(rest_tables, 16 * len(tables["rest"]))
            pe.wait_ge(oh_ready, 1)
            nc.tensor.matmul(ps_rank, const["tri"], OHb[:], start=True, stop=True)
            nc.tensor.matmul(ps_total, const["ones"], OHb[:], start=True, stop=True).then_inc(rank_done, 1)
            pe.wait_ge(zeros_ready, 1)
            pe.wait_ge(lg_read, NT + 2)
            nc.tensor.matmul(ps_table, const["ones"], zeros[:], start=True, stop=False)
            pe.sem_inc(hot_used, 2)

            def place(i, s, turn):
                pe.wait_ge(hot_ready, i + 1)
                for w in range(W):
                    last = nc.tensor.matmul(ps_table, hot_row[s][:, w, :], placed[s][:, w, :, :].rearrange("p a b -> p (a b)"),
                                            start=False, stop=False)
                last.then_inc(hot_used, 1)

            by_twos(pe, NC // W, place)
            nc.tensor.matmul(ps_table, const["ones"], zeros[:], start=False, stop=True).then_inc(table_done, 1)

        @block.scalar
        def _(act):
            act.sem_inc(xt_ready, 2)
            act.sem_inc(xt_kept, 2)

            def copy(i, s, turn):
                act.wait_ge(xt_done, made(i))
                act.wait_ge(lg_done, reusable(i))
                nc.scalar.copy(xt[s][:], ps_xt[s]).then_inc(xt_ready, 1)
                nc.scalar.copy(xnT[:, :, bass.ts(i, P)], ps_xt[s]).then_inc(xt_kept, 1)

            for c in range(CHUNKS):
                cols = slice(c * CT, (c + 1) * CT)
                act.wait_ge(var_ready, c + 1)
                nc.scalar.activation(root[:, cols], var[:, cols], ACT.Sqrt).then_inc(root_ready, 1)
                by_twos(act, CT, copy, first=c * CT)
            act.wait_ge(exp_wanted, 1)
            nc.scalar.activation(A2[:], LG[:] if L == 0 else A1[:], ACT.Exp, scale=(-1.0 if L == 0 else 1.0)).then_inc(exp_ready, 1)

        @block.vector
        def _(dve):
            V = nc.vector
            step = Chain(dve, chain)
            V.memset(zeros[:], 0.0).then_inc(zeros_ready, 1)

            def statistics(c):
                dve.wait_ge(x_loaded[c], 16)
                with dve.Fori(0, 2) as j:
                    for n in range(CT // 2):
                        t = j * (CT // 2) + (c * CT + n)
                        last = V.bn_stats(st[:, t, :], X[:, t, :])
                    last.then_inc(stats_made, 1)

            def mean_and_rstd(c):
                if x_src is not None:
                    dve.wait_ge(stats_made, c * 2 + 2)
                cols = slice(c * CT, (c + 1) * CT)
                mean_c, sd_c, var_c, root_c, quot_c = mean[:, cols], sd[:, cols], var[:, cols], root[:, cols], quot[:, cols]
                V.tensor_tensor(sd_c, st[:, cols, 1], st[:, cols, 4], ALU.subtract)
                V.tensor_tensor(var_c, st[:, cols, 2], st[:, cols, 5], ALU.add)
                step(V.tensor_tensor(mean_c, st[:, cols, 1], st[:, cols, 4], ALU.add))
                V.tensor_scalar(mean_c, mean_c, 0.5, None, ALU.mult)
                V.tensor_scalar(var_c, var_c, 1.0 / D, EPS, ALU.mult, ALU.add)
                step(V.tensor_tensor(sd_c, sd_c, sd_c, ALU.mult))
                V.scalar_tensor_tensor(var_c, sd_c, 0.25, var_c, ALU.mult, ALU.add).then_inc(var_ready, 1)
                dve.wait_ge(var_ready, c + 1)
                dve.wait_ge(root_ready, c + 1)
                step(V.reciprocal(quot_c, root_c))
                step(V.tensor_tensor(quot_c, quot_c, var_c, ALU.mult))
                step(V.tensor_tensor(root_c, root_c, quot_c, ALU.add))
                step(V.tensor_scalar(root_c, root_c, 0.5, None, ALU.mult))
                step(V.reciprocal(rstd[:, cols], root_c))

            dve.sem_inc(lg_read, 2)
            if L == 0:
                dve.wait_ge(first_tables, 16 * len(tables["first"]))
            if v_out is not None:
                dve.wait_ge(wv_loaded, 32)

            def normalise(i, n, turn):
                if not isinstance(i, int) or i >= XN:
                    dve.wait_ge(xt_done, i - XN + 3)
                dve.wait_ge(xn_stored[n], storable(turn))
                V.tensor_scalar(xn[n][:], X[:, i, :], mean[:, bass.ds(i, 1)], rstd[:, bass.ds(i, 1)],
                                ALU.subtract, ALU.mult).then_inc(xn_ready, 1)

            def keep_logits(i, n, turn):
                s = n % 2
                dve.wait_ge(lg_done, made(i))
                if v_out is not None:
                    V.tensor_tensor(v_out["v"][:, i, :], ps_v[s], v_out["b"][:], ALU.add)
                if bias is not None:
                    V.tensor_tensor(LG[:, i, :], ps_lg[s], bias, ALU.add).then_inc(lg_read, 1)
                else:
                    V.tensor_copy(LG[:, i, :], ps_lg[s]).then_inc(lg_read, 1)

            if x_src is not None:
                statistics(0)
            for c in range(CHUNKS):
                mean_and_rstd(c)
                if c + 1 < CHUNKS:
                    statistics(c + 1)
                pipelined(dve, CT, normalise, keep_logits, ahead=2, unroll=XN, first=c * CT)
            dve.wait_ge(lg_read, NT + 2)
            if L == 0:
                dve.wait_ge(rest_tables, 16 * len(tables["rest"]))
            full = [P, NT, E]
            if L == 0:
                V.memset(pick[:], 0.0).then_inc(exp_wanted, 1)
                dve.wait_ge(exp_ready, 1)
                step(V.tensor_scalar(A1[:], A2[:], 1.0, None, ALU.add))
                step(V.reciprocal(PR[:], A1[:]))
            else:
                step(V.reduce_max(pick[:], LG[:], AX.X))
                V.tensor_tensor(A1[:], LG[:], spread(pick[:], 2, full), ALU.subtract).then_inc(exp_wanted, 1)
                dve.wait_ge(exp_ready, 1)
                step(V.reduce_sum(pick[:], A2[:], AX.X))
                step(V.reciprocal(pick[:], pick[:]))
                step(V.tensor_tensor(PR[:], A2[:], spread(pick[:], 2, full), ALU.mult))
            gate = route["gate"][:].rearrange("p (g k t) -> p g k t", g=G, k=2)
            for k in range(2):
                src = PR if k == 0 else A1
                step(V.reduce_max(pick[:], src[:], AX.X))
                step(V.tensor_copy(gate[:, :, k, :], pick[:].rearrange("p (g t) -> p g t", g=G)))
                step(V.tensor_tensor(A2[:], src[:], spread(pick[:], 2, full), ALU.is_equal))
                step(V.scalar_tensor_tensor(A2[:], A2[:], -64.0, const["expert_no"], ALU.mult, ALU.add))
                step(V.tensor_reduce(pick[:], A2[:], AX.X, ALU.min))
                step(V.tensor_tensor(A2[:], A2[:], spread(pick[:], 2, full), ALU.is_equal))
                for g in range(G):
                    step(V.tensor_copy(OH[:, g, :, k, :], A2[:, g * TG:(g + 1) * TG, :].rearrange("p t e -> p e t")))
                if k == 0:
                    step(V.scalar_tensor_tensor(A1[:], A2[:], -4.0, PR[:], ALU.mult, ALU.add))
            oh = OH[:].rearrange("p g e k t -> p (g e k t)")
            V.tensor_copy(OHb[:], oh).then_inc(oh_ready, 1)
            dve.wait_ge(rank_done, 1)
            step(V.tensor_copy(T[:], ps_total))
            step(V.tensor_tensor_scan(S[:], const[f"go_on{L}"], T[:], 0.0, ALU.mult, ALU.add))
            step(V.tensor_tensor(R[:], S[:], T[:], ALU.subtract))
            step(V.tensor_tensor(R[:], R[:], ps_rank, ALU.add))
            if L == 0:
                counts = S[:].rearrange("p (e c) -> p e c", e=E)[:, :, NC - 1]
                step(V.tensor_tensor(over[:], spread(counts, 2, [P, E, NT]), spread(const["rows_before"], 1, [P, E, NT]), ALU.is_gt))
                step(V.reduce_sum(nblk[:], over[:], AX.X))
                step(V.tensor_tensor_scan(ends[:], const["one8"], nblk[:], 0.0, ALU.mult, ALU.add))
                step(V.tensor_tensor(base[:], ends[:], nblk[:], ALU.subtract))
                step(V.tensor_scalar(base[:], base[:], float(P), None, ALU.mult))
                view = R[:].rearrange("p (e c) -> p e c", e=E)
                step(V.tensor_tensor(view, view, spread(base[:], 2, [P, E, NC]), ALU.add))
                sh = [P, BLOCKS0, E]
                step(V.tensor_tensor(after[:], spread(const["count_up"][:, 0:BLOCKS0], 2, sh), spread(ends[:], 1, sh), ALU.is_ge))
                step(V.reduce_sum(blk_e[:], after[:], AX.X))
                step(V.tensor_scalar(route["expert"][:], blk_e[:], float(E - 1), None, ALU.min))
            else:
                step(V.tensor_tensor(T[:], oh, R[:], ALU.mult))
                for g in range(G):
                    step(V.reduce_sum(keep[:, g * 2 * TG:(g + 1) * 2 * TG],
                                      T[:, g * E * 2 * TG:(g + 1) * E * 2 * TG].rearrange("p (e c) -> p c e", e=E), AX.X))
                step(V.tensor_scalar(keep[:], keep[:], float(CAP), None, ALU.is_lt))
                step(V.tensor_tensor(R[:], R[:], const["slot_base"], ALU.add))
            step(V.tensor_tensor(T[:], oh, R[:], ALU.mult))
            for g in range(G):
                step(V.reduce_sum(dest[:, g * 2 * TG:(g + 1) * 2 * TG],
                                  T[:, g * E * 2 * TG:(g + 1) * E * 2 * TG].rearrange("p (e c) -> p c e", e=E), AX.X))
            if L == 1:
                step(V.tensor_tensor(dest[:], dest[:], keep[:], ALU.mult))
                step(V.tensor_tensor(route["gate"][:], route["gate"][:], keep[:], ALU.mult))
            step(V.tensor_copy(route["dest"][:], dest[:]))
            if L == 1:
                step(V.tensor_scalar(keep[:], keep[:], -8192.0, 8192.0, ALU.mult, ALU.add))
                step(V.tensor_tensor(dest[:], dest[:], keep[:], ALU.add))
            step(V.tensor_copy(row_i[:], dest[:]))
            step(V.tensor_scalar(lo_i[:], row_i[:], P - 1, None, ALU.bitwise_and))
            step(V.tensor_scalar(hi_i[:], row_i[:], 7, None, ALU.logical_shift_right))
            step(V.tensor_copy(lo[:], lo_i[:]))
            step(V.tensor_copy(hi[:], hi_i[:]))

            count_rows = spread(const["count_up"], 1, [P, W, P])
            count_blocks = spread(const["count_up"][:, 0:NB], 1, [P, W, NB])

            def one_hots(i, s, turn):
                dve.wait_ge(hot_used, reusable(i))
                cols = bass.ds(i * W, W)
                V.tensor_tensor(hot_row[s][:], count_rows, spread(lo[:, cols], 2, [P, W, P]), ALU.is_equal)
                V.tensor_tensor(hot_block[s][:], count_blocks, spread(hi[:, cols], 2, [P, W, NB]), ALU.is_equal).then_inc(blocks_hot, 1)
                dve.wait_ge(blocks_hot, i + 1)
                V.tensor_scalar(placed[s][:, :, 0, :], hot_block[s][:], const["part_no"], None, ALU.mult)
                V.tensor_tensor(placed[s][:, :, 1, :], hot_block[s][:], spread(const[f"tile_no{L}"][:, cols], 2, [P, W, NB]),
                                ALU.mult).then_inc(hot_ready, 1)

            by_twos(dve, NC // W, one_hots)
            dve.wait_ge(table_done, 1)
            step(V.tensor_copy(T[:, 0:2 * NB], ps_table))
            step(V.scalar_tensor_tensor(route["token"][:, 0:NB], table[:, 1, :], float(P), table[:, 0, :], ALU.mult, ALU.add))


def scan_branch(nc, signals, X, xnT, w, const, expert_weights):
    HALF = 512
    with phase(nc, signals) as stack:
        m = stack.memory
        wz = m.sb("w_z", [P, HC, D])
        w3 = m.sb("w_bcd", [P, HC, 3, 32])
        wo = m.sb("w_out0", [P, HC, D])
        bz = m.sb("b_z", [P, HC])
        b3 = m.sb("b_bcd_alog", [P, 4])
        bo = m.sb("b_out0", [P, D])
        U = m.sb("u", [P, SEQ])
        V1 = m.sb("abs_u", [P, SEQ])
        V2 = m.sb("exp_u", [P, SEQ])
        Bt = m.sb("b_t", [P, SEQ])
        St = m.sb("state", [P, SEQ])
        Cs = Bt
        negA = m.sb("neg_a", [P, 1])
        YS = m.sb("y_scan", [P, NT])
        gz = [m.sb(f"gelu_z{s}", [P, HC, HALF]) for s in range(2)]
        loaded = m.sem("scan_w_loaded")
        small_loaded = m.sem("bcd_b_loaded")
        cleared, chain = m.sem("scan_cleared"), m.sem("scan_chain")
        bcd_done = m.sem("bcd_done")
        u_ready, abs_ready, act_chain, e_ready, decay_ready = (
            m.sem("u_ready"), m.sem("abs_ready"), m.sem("scan_act_chain"), m.sem("delta_ready"), m.sem("decay_ready"))
        cs_ready, y_done, y_ready = m.sem("cs_ready"), m.sem("y_done"), m.sem("y_ready")
        z_done, z_ready, o_done, o_read = m.sem("z_done"), m.sem("z_ready"), m.sem("gelu_o_done"), m.sem("gelu_o_read")
        x_biased = m.sem("x_biased")
        ps = stack.enter_context(nc.psum_tensor("ps_scan", [P, 8, 512], F32))
        block = stack.block.enter_context(nc.Block())
        GROUPS = TOK // HALF

        @block.sync
        def _(sp):
            sp.wait_ge(cleared, 2)
            for b in range(BATCH):
                sp.dma_start(b3[32 * b:32 * b + N_STATE, :], w["bcd_alog"]).then_inc(small_loaded, 16)
            for f in range(3):
                c0 = 2 * D + f * N_STATE
                sp.dma_start(w3[:, :, f, 0:N_STATE], w["in"][:, :, c0:c0 + N_STATE]).then_inc(loaded, 16)
            sp.dma_start(wz[:], w["in"][:, :, D:2 * D]).then_inc(loaded, 16)
            sp.dma_start(wo[:], w["out"]).then_inc(loaded, 16)
            sp.dma_start(bz[:], w["b_z"]).then_inc(loaded, 16)
            sp.dma_start(bo[:], w["b_out"].to_broadcast([P, D])).then_inc(loaded, 16)
            for (dst, src), sem in zip(expert_weights["loads"], expert_weights["loaded"]):
                sp.dma_start(dst[:], src).then_inc(sem, 16)

        @block.gpsimd
        def _(pool):
            nc.gpsimd.memset(b3[:], 0.0).then_inc(cleared, 1)
            nc.gpsimd.memset(w3[:], 0.0).then_inc(cleared, 1)
            pool.wait_ge(loaded, 7 * 16)
            with pool.Fori(0, NT) as i:
                nc.gpsimd.tensor_tensor(X[:, i, :], X[:, i, :], bo[:], ALU.add).then_inc(x_biased, 1)

        @block.tensor
        def _(pe):
            pe.wait_ge(loaded, 7 * 16)
            for f in (2, 0, 1):
                for h in range(2):
                    for b in range(BATCH):
                        t0 = b * SEQ + h * HALF
                        for c in range(HC):
                            last = nc.tensor.matmul(ps[32 * b:32 * b + 32, 2 * f + h, :], w3[:, c, f, :],
                                                    xnT[:, c, t0:t0 + HALF], start=(c == 0), stop=(c == HC - 1))
                last.then_inc(bcd_done, 1)
            pe.wait_ge(cs_ready, 1)
            for j in range(SEQ // P):
                last = nc.tensor.matmul(ps[:, 4, 4 * j:4 * j + 4], Cs[:, j * P:(j + 1) * P], const["batch_of"],
                                        start=True, stop=True)
            last.then_inc(y_done, 1)
            pe.wait_ge(y_ready, 1)
            pe.sem_inc(z_done, 2)
            pe.sem_inc(o_done, 2)

            def project(g, s, turn):
                pe.wait_ge(z_ready, reusable(g))
                for c in range(HC):
                    for k in range(HC):
                        last = nc.tensor.matmul(ps[:, 2 * s + c, :], wz[:, k, c * P:(c + 1) * P],
                                                xnT[:, k, bass.ts(g, HALF)], start=(k == 0), stop=(k == HC - 1))
                last.then_inc(z_done, 1)

            def out(g, s, turn):
                pe.wait_ge(z_ready, made(g))
                pe.wait_ge(o_read, reusable(g))
                for t in range(4):
                    for c in range(HC):
                        last = nc.tensor.matmul(ps[:, 4 + 2 * s + t // 2, (t % 2) * D:(t % 2) * D + D],
                                                gz[s][:, c, t * P:(t + 1) * P], wo[:, c, :],
                                                start=(c == 0), stop=(c == HC - 1))
                last.then_inc(o_done, 1)

            software_pipelined(pe, GROUPS, project, out)

        @block.scalar
        def _(act):
            link = Chain(act, act_chain)
            act.wait_ge(small_loaded, 4 * 16)
            link(nc.scalar.activation(negA[:], b3[:, 3:4], ACT.Exp))
            link(nc.scalar.mul(negA[:], negA[:], -1.0))
            act.wait_ge(u_ready, 1)
            link(nc.scalar.activation(V1[:], U[:], ACT.Abs))
            link(nc.scalar.activation(V2[:], V1[:], ACT.Exp, scale=-1.0))
            nc.scalar.activation(V1[:], V2[:], ACT.Ln, bias=1.0).then_inc(abs_ready, 1)
            act.wait_ge(e_ready, 1)
            nc.scalar.activation(V2[:], U[:], ACT.Exp, scale=negA[:]).then_inc(decay_ready, 1)
            act.sem_inc(z_ready, 2)

            def gelu(g, s, turn):
                act.wait_ge(z_done, made(g))
                act.wait_ge(o_done, reusable(g))
                for c in range(HC):
                    last = nc.scalar.activation(gz[s][:, c, :], ps[:, 2 * s + c, :], ACT.Gelu, bias=bz[:, c:c + 1])
                last.then_inc(z_ready, 1)

            by_twos(act, GROUPS, gelu)

        @block.vector
        def _(dve):
            V = nc.vector
            step = Chain(dve, chain)
            dve.wait_ge(small_loaded, 4 * 16)
            field = lambda f: ps[:, 2 * f:2 * f + 2, :].rearrange("p a t -> p (a t)")
            dve.wait_ge(bcd_done, 1)
            V.tensor_scalar(U[:], field(2), b3[:, 2:3], None, ALU.add).then_inc(u_ready, 1)
            dve.wait_ge(bcd_done, 2)
            step(V.tensor_scalar(Bt[:], field(0), b3[:, 0:1], None, ALU.add))
            dve.wait_ge(abs_ready, 1)
            V.scalar_tensor_tensor(U[:], U[:], 0.0, V1[:], ALU.max, ALU.add).then_inc(e_ready, 1)
            dve.wait_ge(decay_ready, 1)
            step(V.tensor_tensor_scan(St[:], V2[:], Bt[:], 0.0, ALU.mult, ALU.add))
            dve.wait_ge(bcd_done, 3)
            V.scalar_tensor_tensor(Cs[:], field(1), b3[:, 1:2], St[:], ALU.add, ALU.mult).then_inc(cs_ready, 1)
            dve.wait_ge(y_done, 1)
            V.tensor_copy(YS[:].rearrange("p (b j) -> p b j", b=BATCH),
                          ps[:, 4, 0:NT].rearrange("p (j b) -> p b j", b=BATCH)).then_inc(y_ready, 1)
            dve.wait_ge(y_ready, 1)
            dve.wait_ge(x_biased, NT)
            dve.sem_inc(o_read, 2)

            def add(g, s, turn):
                dve.wait_ge(o_done, made(g))
                for t in range(4):
                    src = ps[:, 4 + 2 * s + t // 2, (t % 2) * D:(t % 2) * D + D]
                    last = V.scalar_tensor_tensor(X[:, g * 4 + t, :], src, YS[:, bass.ds(g * 4 + t, 1)],
                                                  X[:, g * 4 + t, :], ALU.mult, ALU.add)
                last.then_inc(o_read, 1)

            by_twos(dve, GROUPS, add)


def shared_expert(nc, signals, X, xnT, w, route, y_dram, stats):
    N = 512
    IC = I0 // P
    GROUPS = TOK // N
    with phase(nc, signals) as stack:
        m = stack.memory
        cut = lambda name, shape: {part: m.sb(f"{name}_{part}", shape, F22) for part in ("high", "low")}
        raw = {"g": m.sb("wg_raw", [P, HC, I0]), "u": m.sb("wu_raw", [P, HC, I0]), "d": m.sb("wd_raw", [P, IC, D])}
        wg, wu, wd = cut("wg_shared", [P, HC, I0]), cut("wu_shared", [P, HC, I0]), cut("wd_shared", [P, IC, D])
        weights = (("g", wg), ("u", wu), ("d", wd))
        xs = [cut(f"x_shared{s}", [P, HC, N]) for s in range(2)]
        sg = [m.sb(f"silu_shared{s}", [P, N]) for s in range(2)]
        whole = [m.sb(f"h_whole{s}", [P, N]) for s in range(2)]
        hT = [cut(f"h_shared{s}", [P, IC, N]) for s in range(2)]
        GT = N // P
        back_ids = m.sb("back_ids", [P, 2, 2, GT], I32)
        back = m.sb("back_rows", [P, 2, 2, GT, D])
        ids_ready, gathers, gathered = m.sem("back_ids_ready"), m.sem("back_gathers"), m.gather_sems("back_gathered", 2)
        first_added, back_added = m.sem("back_first_added"), m.sem("back_added")
        loaded = m.sems("shared_w_loaded", 3)
        w_high, w_low, x_high, x_low = m.sem("shared_w_high"), m.sem("shared_w_low"), m.sem("shared_x_high"), m.sem("shared_x_low")
        gu_done, silu_ready, h_whole = m.sem("gu_done"), m.sem("silu_ready"), m.sem("h_whole")
        h_high, h_low = m.sem("h_high"), m.sem("h_low")
        y_done, y_read = m.sem("shared_y_done"), m.sem("shared_y_read")
        ps = stack.enter_context(nc.psum_tensor("ps_shared", [P, 8, 512], F32))
        block = stack.block.enter_context(nc.Block())

        @block.sync
        def _(sp):
            for (name, _), sem in zip(weights, loaded):
                sp.dma_start(raw[name][:], w[name]).then_inc(sem, 16)

        @block.tensor
        def _(pe):
            pe.sem_inc(gu_done, 2)
            pe.sem_inc(y_done, 2)
            pe.wait_ge(w_low, 2)

            def up(g, s, turn):
                pe.wait_ge(x_low, g + 1)
                for i in range(IC):
                    n = g * IC + i
                    pe.wait_ge(h_whole, reusable(n))
                    for bank, wt in ((i % 2, wg), (2 + i % 2, wu)):
                        for t, (a, b) in enumerate(PRODUCTS):
                            for k in range(HC):
                                last = nc.tensor.matmul(ps[:, bank, :], wt[a][:, k, i * P:(i + 1) * P], xs[s][b][:, k, :],
                                                        start=(t == 0 and k == 0), stop=(t == len(PRODUCTS) - 1 and k == HC - 1))
                    last.then_inc(gu_done, 1)

            def down(g, s, turn):
                if isinstance(g, int) and g == 0:
                    pe.wait_ge(w_low, 3)
                pe.wait_ge(h_low, g * IC + IC)
                pe.wait_ge(y_read, reusable(g))
                for t in range(4):
                    for i in range(IC):
                        for n, (a, b) in enumerate(PRODUCTS):
                            last = nc.tensor.matmul(ps[:, 4 + 2 * s + t // 2, (t % 2) * D:(t % 2) * D + D],
                                                    hT[s][a][:, i, t * P:(t + 1) * P], wd[b][:, i, :],
                                                    start=(i == 0 and n == 0), stop=(i == IC - 1 and n == len(PRODUCTS) - 1))
                last.then_inc(y_done, 1)

            software_pipelined(pe, GROUPS, up, down)

        @block.gpsimd
        def _(pool):
            def gather(g, s, turn):
                pool.wait_ge(back_added, reusable(g))
                for k in range(2):
                    last = nc.gpsimd.tensor_copy(back_ids[:, s, k, :], route["dest"][:, bass.ds(g * GT + k * NT, GT)])
                last.then_inc(ids_ready, 1)
                pool.wait_ge(ids_ready, g + 1)
                pool.sem_inc(gathers, 1)
                for t in range(GT):
                    for k in range(2):
                        nc.gpsimd.indirect_dma_start(back[:, s, k, t, :], None, y_dram,
                                                     bass.IndirectOffsetOnAxis(ap=back_ids[:, s, k, t:t + 1], axis=0)
                                                     ).then_inc(gathered[s], 16)

            by_twos(pool, GROUPS, gather)

        @block.scalar
        def _(act):
            act.sem_inc(silu_ready, 2)

            def high_rows(g, s):
                if not isinstance(g, int) or g >= 2:
                    act.wait_ge(gu_done, g * IC - (IC - 2))
                nc.scalar.copy(xs[s]["high"][:], xnT[:, :, bass.ts(g, N)]).then_inc(x_high, 1)

            def silu(g, i):
                n = g * IC + i
                act.wait_ge(gu_done, made(n))
                act.wait_ge(h_whole, reusable(n))
                nc.scalar.activation(sg[i % 2][:], ps[:, i % 2, :], ACT.Silu).then_inc(silu_ready, 1)

            def high_hidden(g, s, i):
                act.wait_ge(h_whole, made(g * IC + i))
                act.wait_ge(y_done, reusable(g))
                nc.scalar.copy(hT[s]["high"][:, i, :], whole[i % 2][:]).then_inc(h_high, 1)

            def group(g, s, more=True):
                if more:
                    high_rows(g + 1, 1 - s)
                silu(g, 0)
                for i in range(1, IC):
                    silu(g, i)
                    high_hidden(g, s, i - 1)
                high_hidden(g, s, IC - 1)

            high_rows(0, 0)
            for n, (name, parts) in enumerate(weights):
                act.wait_ge(loaded[n], 16)
                nc.scalar.copy(parts["high"][:], raw[name][:]).then_inc(w_high, 1)
            with act.Fori(0, GROUPS // 2 - 1) as j:
                for s in range(2):
                    group(j * 2 + s, s)
            group(GROUPS - 2, 0)
            group(GROUPS - 1, 1, more=False)

        @block.vector
        def _(dve):
            V = nc.vector
            dve.sem_inc(h_whole, 2)
            dve.sem_inc(y_read, 2)
            dve.sem_inc(back_added, 2)

            def low_rows(g, s):
                if not isinstance(g, int) or g >= 2:
                    dve.wait_ge(gu_done, g * IC - (IC - 2))
                dve.wait_ge(x_high, g + 1)
                V.tensor_tensor(xs[s]["low"][:], xnT[:, :, bass.ts(g, N)], xs[s]["high"][:], ALU.subtract).then_inc(x_low, 1)

            def gate(g, i):
                n = g * IC + i
                dve.wait_ge(silu_ready, made(n))
                if not isinstance(n, int) or n >= 2:
                    dve.wait_ge(h_high, n - 1)
                    dve.wait_ge(h_low, n - 1)
                V.tensor_tensor(whole[i % 2][:], sg[i % 2][:], ps[:, 2 + i % 2, :], ALU.mult).then_inc(h_whole, 1)

            def low_hidden(g, s, i):
                dve.wait_ge(h_high, g * IC + i + 1)
                dve.wait_ge(h_whole, made(g * IC + i))
                V.tensor_tensor(hT[s]["low"][:, i, :], whole[i % 2][:], hT[s]["high"][:, i, :], ALU.subtract).then_inc(h_low, 1)

            def gated(g, s, turn):
                dve.wait_ge(y_done, reusable(g))
                gate(g, 0)
                for i in range(1, IC):
                    gate(g, i)
                    low_hidden(g, s, i - 1)
                low_hidden(g, s, IC - 1)
                if not isinstance(g, int) or g + 1 < GROUPS:
                    low_rows(g + 1, 1 - s)

            def add(g, s, turn):
                dve.wait_ge(gathered[s], turn * (16 * 2 * GT) + 16 * 2 * GT)
                for k, done, count in ((0, first_added, g + 1), (1, back_added, made(g))):
                    for t in range(GT):
                        tile = g * GT + t
                        last = V.scalar_tensor_tensor(X[:, tile, :], back[:, s, k, t, :], route["gate"][:, bass.ds(tile + k * NT, 1)],
                                                      X[:, tile, :], ALU.mult, ALU.add)
                    last.then_inc(done, 1)
                    dve.wait_ge(done, count)
                dve.wait_ge(y_done, made(g))
                for t in range(4):
                    src = ps[:, 4 + 2 * s + t // 2, (t % 2) * D:(t % 2) * D + D]
                    last = V.tensor_tensor(X[:, g * 4 + t, :], src, X[:, g * 4 + t, :], ALU.add)
                last.then_inc(y_read, 1)
                dve.wait_ge(y_read, made(g))
                for t in range(4):
                    V.bn_stats(stats[:, g * 4 + t, :], X[:, g * 4 + t, :])

            low_rows(0, 0)
            for n, (name, parts) in enumerate(weights):
                dve.wait_ge(w_high, n + 1)
                V.tensor_tensor(parts["low"][:], raw[name][:], parts["high"][:], ALU.subtract).then_inc(w_low, 1)
            software_pipelined(dve, GROUPS, gated, add)


def routed_experts(nc, signals, w, route, xn_dram, y_dram, const):
    IC = I0 // P
    with phase(nc, signals) as stack:
        m = stack.memory
        wg, wu, wd, w_loaded = w["wg"], w["wu"], w["wd"], w["loaded"]
        ids = [m.sb(f"row_tokens{s}", [P, 1], I32) for s in range(2)]
        xg = [m.sb(f"rows{s}", [P, D]) for s in range(2)]
        xt = [m.sb(f"rows_t{s}", [P, HC, P]) for s in range(2)]
        sg = [m.sb(f"silu{s}", [P, I0]) for s in range(2)]
        h = [m.sb(f"hidden{s}", [P, I0]) for s in range(2)]
        ht = [m.sb(f"hidden_t{s}", [P, IC, P]) for s in range(2)]
        yr = [m.sb(f"y_rows{s}", [P, D]) for s in range(2)]
        ids_ready, gathers, gathered = m.sem("ids_ready"), m.sem("gathers"), m.gather_sems("gathered", 2)
        xt_done, xt_ready, g_done, u_done = m.sem("rt_xt_done"), m.sem("rt_xt_ready"), m.sem("rt_g_done"), m.sem("rt_u_done")
        silu_ready, h_ready, ht_done, ht_ready = m.sem("rt_silu"), m.sem("rt_h"), m.sem("rt_ht_done"), m.sem("rt_ht_ready")
        y_done, y_ready, y_stored = m.sem("rt_y_done"), m.sem("rt_y_ready"), m.sems("rt_y_stored", 2)
        ps = stack.enter_context(nc.psum_tensor("ps_routed", [P, 8, 512], F32))
        ps_xt = ps[:, 6, 0:D].rearrange("p (c t) -> p c t", c=HC)
        ps_y = ps[:, 7, 0:D]
        ps_ht = [ps[:, 4 + s, :].rearrange("p (c t) -> p c t", c=IC) for s in range(2)]
        block = stack.block.enter_context(nc.Block())

        @block.sync
        def _(sp):
            for s in range(2):
                sp.sem_inc(y_stored[s], 16)

            def store(i, s, turn):
                sp.wait_ge(y_ready, made(i))
                sp.dma_start(y_dram[bass.ts(i, P), :], yr[s][:]).then_inc(y_stored[s], 16)

            by_twos(sp, BLOCKS0, store)
            for s in range(2):
                sp.wait_ge(y_stored[s], stored(BLOCKS0 // 2 - 1))

        @block.gpsimd
        def _(pool):
            def gather(i, s, turn):
                pool.wait_ge(xt_done, reusable(i))
                nc.gpsimd.tensor_copy(ids[s][:], route["token"][:, bass.ds(i, 1)]).then_inc(ids_ready, 1)
                pool.wait_ge(ids_ready, i + 1)
                pool.sem_inc(gathers, 1)
                nc.gpsimd.indirect_dma_start(xg[s][:], None, xn_dram, bass.IndirectOffsetOnAxis(ap=ids[s][:, 0:1], axis=0)
                                             ).then_inc(gathered[s], 16)

            by_twos(pool, BLOCKS0, gather)

        @block.tensor
        def _(pe):
            pe.sem_inc(xt_done, 2)
            pe.sem_inc(u_done, 2)
            pe.sem_inc(ht_done, 2)
            pe.sem_inc(y_done, 2)

            def turn_rows(i, s, turn):
                pe.wait_ge(gathered[s], turn * 16 + 16)
                pe.wait_ge(xt_ready, i + 2)
                for c in range(HC):
                    last = nc.tensor.transpose(ps_xt[:, c, :], xg[s][:, c * P:(c + 1) * P], const["ident"])
                last.then_inc(xt_done, 1)

            def turn_hidden(i, s, turn):
                pe.wait_ge(h_ready, made(i))
                pe.wait_ge(ht_ready, reusable(i))
                for c in range(IC):
                    last = nc.tensor.transpose(ps_ht[s][:, c, :], h[s][:, c * P:(c + 1) * P], const["ident"])
                last.then_inc(ht_done, 1)

            def up(i, s, turn):
                e = pe.value_load(route["expert"][0:1, bass.ds(i, 1)], min_val=0, max_val=E - 1)
                pe.wait_ge(h_ready, reusable(i))
                pe.wait_ge(xt_ready, made(i))
                for bank, wt, sem in ((s, wg, g_done), (2 + s, wu, u_done)):
                    for k in range(HC):
                        last = nc.tensor.matmul(ps[:, bank, :], xt[s][:, k, :], wt[:, bass.ds(e, 1), k, :],
                                                start=(k == 0), stop=(k == HC - 1))
                    last.then_inc(sem, 1)

            def down(i, s, turn):
                e = pe.value_load(route["expert"][0:1, bass.ds(i, 1)], min_val=0, max_val=E - 1)
                pe.wait_ge(y_ready, i + 2)
                pe.wait_ge(ht_ready, made(i))
                for c in range(IC):
                    last = nc.tensor.matmul(ps_y, ht[s][:, c, :], wd[:, bass.ds(e, 1), c, :], start=(c == 0), stop=(c == IC - 1))
                last.then_inc(y_done, 1)

            turn_rows(0, 0, 0)
            turn_rows(1, 1, 0)
            for n in range(3):
                pe.wait_ge(w_loaded[n], 16)
            up(0, 0, 0)
            with pe.Fori(0, BLOCKS0 // 2 - 1) as j:
                for i, s, turn, before in ((j * 2 + 1, 1, j, j), (j * 2 + 2, 0, j + 1, j)):
                    turn_rows(i + 1, 1 - s, j + 1)
                    turn_hidden(i - 1, 1 - s, before)
                    up(i, s, turn)
                    down(i - 1, 1 - s, before)
            turn_hidden(BLOCKS0 - 2, 0, 0)
            up(BLOCKS0 - 1, 1, 0)
            down(BLOCKS0 - 2, 0, 0)
            turn_hidden(BLOCKS0 - 1, 1, 0)
            down(BLOCKS0 - 1, 1, 0)

        @block.scalar
        def _(act):
            act.sem_inc(xt_ready, 2)
            act.sem_inc(silu_ready, 2)
            act.sem_inc(y_ready, 2)

            def copy_rows(i, s):
                act.wait_ge(xt_done, made(i))
                act.wait_ge(u_done, reusable(i))
                nc.scalar.copy(xt[s][:], ps_xt).then_inc(xt_ready, 1)

            def silu(i, s):
                act.wait_ge(g_done, i + 1)
                act.wait_ge(h_ready, reusable(i))
                nc.scalar.activation(sg[s][:], ps[:, s, :], ACT.Silu).then_inc(silu_ready, 1)

            def copy_result(i, s, turn):
                act.wait_ge(y_done, made(i))
                act.wait_ge(y_stored[s], storable(turn))
                nc.scalar.copy(yr[s][:], ps_y).then_inc(y_ready, 1)

            copy_rows(0, 0)
            copy_rows(1, 1)
            silu(0, 0)
            with act.Fori(0, BLOCKS0 // 2 - 1) as j:
                for i, s in ((j * 2 + 1, 1), (j * 2 + 2, 0)):
                    copy_rows(i + 1, 1 - s)
                    silu(i, s)
                    copy_result(i - 1, 1 - s, j)
            silu(BLOCKS0 - 1, 1)
            copy_result(BLOCKS0 - 2, 0, BLOCKS0 // 2 - 1)
            copy_result(BLOCKS0 - 1, 1, BLOCKS0 // 2 - 1)

        @block.vector
        def _(dve):
            dve.sem_inc(h_ready, 2)
            dve.sem_inc(ht_ready, 2)

            def gated(i, s, turn):
                dve.wait_ge(silu_ready, made(i))
                dve.wait_ge(u_done, made(i))
                dve.wait_ge(ht_done, reusable(i))
                nc.vector.tensor_tensor(h[s][:], sg[s][:], ps[:, 2 + s, :], ALU.mult).then_inc(h_ready, 1)

            def turned(i, s, turn):
                dve.wait_ge(ht_done, made(i))
                dve.wait_ge(y_done, reusable(i))
                nc.vector.tensor_copy(ht[s][:], ps_ht[s]).then_inc(ht_ready, 1)

            gated(0, 0, 0)
            with dve.Fori(0, BLOCKS0 // 2 - 1) as j:
                for i, s in ((j * 2 + 1, 1), (j * 2 + 2, 0)):
                    turned(i - 1, 1 - s, j)
                    gated(i, s, j)
            turned(BLOCKS0 - 2, 0, 0)
            gated(BLOCKS0 - 1, 1, 0)
            turned(BLOCKS0 - 1, 1, 0)


def project_qk(nc, signals, X, xnT, w, q_dram, k_dram, start):
    N = 512
    RT = 2 * HC
    GROUPS = TOK // N
    with phase(nc, signals) as stack:
        m = stack.memory
        wqk = m.sb("w_qk", [P, HC, 2 * D])
        bqk = m.sb("b_qk", [P, RT])
        full = [m.sb(f"qk_full{s}", [P, RT, N]) for s in range(2)]
        rest = [m.sb(f"qk_rest{s}", [P, RT, N]) for s in range(2)]
        part = [m.sb(f"qk_part{s}", [P, 3, RT, N], BF16) for s in range(2)]
        loaded = m.sem("qk_w_loaded")
        qk_done, full_ready, high_ready, rest_ready, mid_ready, low_ready = (
            m.sem("qk_done"), m.sem("qk_full_ready"), m.sem("qk_high_ready"), m.sem("qk_rest_ready"),
            m.sem("qk_mid_ready"), m.sem("qk_low_ready"))
        qk_stored = m.sems("qk_stored", 2)
        ps = stack.enter_context(nc.psum_tensor("ps_qk", [P, 8, 512], F32))
        block = stack.block.enter_context(nc.Block())
        COPIES = [[(dram, tile, row) for dram, tile, rows in ((q_dram, 0, Q_PARTS), (k_dram, HC, K_PARTS))
                   for row in range(len(rows)) if rows[row] == part_no] for part_no in range(3)]
        PER_STORE = 16 * (len(Q_PARTS) + len(K_PARTS))

        @block.sync
        def _(sp):
            sp.dma_start(wqk[:], w["qk"]).then_inc(loaded, 16)
            sp.dma_start(bqk[:], w["b_qk"]).then_inc(loaded, 16)
            start["load"](sp, 0)
            for s in range(2):
                sp.sem_inc(qk_stored[s], PER_STORE)

            def store(g, s, turn):
                for part_no, ready, count in ((0, high_ready, g + 1), (1, mid_ready, g + 1), (2, low_ready, made(g))):
                    sp.wait_ge(ready, count)
                    for dram, tile, row in COPIES[part_no]:
                        dst = dram[bass.ds(turn * HEADS, HEADS), :, row, s * N:(s + 1) * N].rearrange("(c h) d t -> (h d) c t", c=HC)
                        sp.dma_start(dst, part[s][:, part_no, tile:tile + HC, :]).then_inc(qk_stored[s], 16)

            by_twos(sp, GROUPS, store)
            for s in range(2):
                sp.wait_ge(qk_stored[s], PER_STORE * (GROUPS // 2 + 1))

        @block.tensor
        def _(pe):
            pe.wait_ge(loaded, 32)

            def project(g, s, turn):
                pe.wait_ge(full_ready, reusable(g))
                for r in range(RT):
                    for k in range(HC):
                        last = nc.tensor.matmul(ps[:, s * RT + r, :], wqk[:, k, r * P:(r + 1) * P], xnT[:, k, bass.ts(g, N)],
                                                start=(k == 0), stop=(k == HC - 1))
                last.then_inc(qk_done, 1)

            by_twos(pe, GROUPS, project)

        @block.vector
        def _(dve):
            dve.wait_ge(loaded, 32)
            dve.sem_inc(full_ready, 2)
            dve.sem_inc(low_ready, 2)

            def fill(g, s, turn):
                dve.wait_ge(qk_done, g + 1)
                dve.wait_ge(rest_ready, reusable(g))
                for r in range(RT):
                    last = nc.vector.tensor_scalar(full[s][:, r, :], ps[:, s * RT + r, :], bqk[:, r:r + 1],
                                                   0.25 if r < HC else 1.0, ALU.add, ALU.mult)
                last.then_inc(full_ready, 1)

            def low(g, s, turn):
                dve.wait_ge(mid_ready, g + 1)
                nc.vector.tensor_tensor(part[s][:, 2, :, :], rest[s][:], part[s][:, 1, :, :], ALU.subtract).then_inc(low_ready, 1)

            software_pipelined(dve, GROUPS, fill, low)

        @block.scalar
        def _(act):
            def parts(g, s, turn):
                act.wait_ge(full_ready, made(g))
                act.wait_ge(qk_stored[s], (turn + 1) * PER_STORE)
                nc.scalar.copy(part[s][:, 0, :, :], full[s][:]).then_inc(high_ready, 1)
                act.wait_ge(rest_ready, made(g))
                nc.scalar.copy(part[s][:, 1, :, :], rest[s][:]).then_inc(mid_ready, 1)

            by_twos(act, GROUPS, parts)

        @block.gpsimd
        def _(pool):
            pool.sem_inc(rest_ready, 2)
            start["gather"](pool, 0)

            def rests(g, s, turn):
                pool.wait_ge(high_ready, g + 1)
                pool.wait_ge(low_ready, reusable(g))
                nc.gpsimd.tensor_tensor(rest[s][:], full[s][:], part[s][:, 0, :, :], ALU.subtract).then_inc(rest_ready, 1)

            by_twos(pool, GROUPS, rests)


Q_PARTS = (0, 0, 0, 1, 1, 2)
K_PARTS = (0, 1, 2, 0, 1, 0)
PART_ROWS = HD * len(Q_PARTS)
BIAS_ROWS, MAX_ROWS = 12, 2
SCORE_ROWS = PART_ROWS + BIAS_ROWS
STACK = SCORE_ROWS + MAX_ROWS
QT = SEQ // P
PAIRS = BATCH * HEADS // 2
assert PAIRS == NT
TG = NT // G1
LEAD = 4


def attention(nc, signals, X, v, q_dram, k_dram, o_dram, s_dram, route, y_dram, w, const):
    RING = 3
    with phase(nc, signals) as stack:
        m = stack.memory
        qs = [[m.sb(f"q_stack{s}_{h}", [STACK, SEQ], BF16) for h in range(2)] for s in range(RING)]
        ks = [[[m.sb(f"k_stack{s}_{h}_{side}", [STACK, SEQ], BF16) for side in range(2)] for h in range(2)] for s in range(RING)]
        vs = [m.sb(f"v_stage{s}", [P, 2, QT, 2 * HD]) for s in range(RING)]
        prob = [m.sb(f"prob{n}", [P, 4, 512]) for n in range(2)]
        top = [m.sb(f"top{h}", [P, QT]) for h in range(2)]
        neg = [m.sb(f"neg_top{h}", [P, 2, QT], BF16) for h in range(2)]
        negT = [m.sb(f"neg_top_t{h}", [2 * QT, P], BF16) for h in range(2)]
        osb = [m.sb(f"o_stage{s}", [P, 512]) for s in range(RING)]
        fix_t = m.sb("fix_by_key", [P, HEADS, 3, P], BF16)
        fix = m.sb("fix_by_query", [P, HEADS, P], BF16)
        identb = m.sb("ident_bf", [P, P], BF16)
        first_tables_loaded, tables_loaded = m.sem("attn_first_tables_loaded"), m.sem("attn_tables_loaded")
        stack_loaded = m.sems("stack_loaded", RING)
        ones_ready, v_ready = m.sem("ones_ready"), m.sem("v_staged")
        s1_done, s1_read = m.sem("s1_done"), m.sem("s1_read")
        high_ready, neg_ready = m.sem("top_high_ready"), m.sem("neg_ready")
        turned, turned_read = m.sem("neg_turned"), m.sem("neg_turned_read")
        max_loaded = [m.sems(f"max_loaded{s}_", 2) for s in range(RING)]
        s2_done, exp_ready, pv_done = m.sem("s2_done"), m.sem("exp_ready"), m.sem("pv_done")
        o_read, o_stored = m.sem("o_read"), m.sems("o_stored", RING)
        ids = [[m.sb(f"moe_from{k}_{s}", [P, 1], I32) for s in range(RING)] for k in range(2)]
        rows = [[m.sb(f"moe_rows{k}_{s}", [P, D]) for s in range(RING)] for k in range(2)]
        part = m.sb("moe_part", [P, D])
        ids_ready, gathers = m.sem("moe_ids"), m.sem("moe_gathers")
        gathered = [m.gather_sems(f"moe_gathered{k}_", RING) for k in range(2)]
        first_added, rows_used = m.sem("moe_first_added"), m.sem("moe_rows_used")
        ps = stack.enter_context(nc.psum_tensor("ps_attn", [P, 8, 512], F32))
        ps_turn = ps[0:2 * QT, 7, 0:P // 2].bitcast(BF16)
        block = stack.block.enter_context(nc.Block())
        LOADS = 16 * 2 * (2 + 2 * 2)

        def over_pairs(engine, body, peeled=False):
            if peeled:
                for p in range(RING):
                    body(p, p, 0, 2)
            with engine.Fori(1 if peeled else 0, PAIRS // RING) as j:
                for s in range(RING):
                    body(j * RING + s, s, j, 2)
            for p in range(PAIRS // RING * RING, PAIRS):
                body(p, p % RING, p // RING, PAIRS - 1 - p)

        @block.sync
        def _(sp):
            sp.dma_start(identb[:], w["ident_bf"]).then_inc(first_tables_loaded, 16)
            sp.dma_start(fix[:].rearrange("p h q -> p (h q)"), w["fix_by_query"]).then_inc(first_tables_loaded, 16)

            def load(p, s):
                for h in range(2):
                    bh = p * 2 + h
                    head = (p % (HEADS // 2)) * 2 + h
                    parts = lambda dram: dram[bass.ds(bh, 1)].rearrange("o d a t -> (o d a) t")
                    bias = lambda table: table.rearrange("o r t -> (o r) t")
                    sp.dma_start(qs[s][h][0:PART_ROWS, :], parts(q_dram)).then_inc(stack_loaded[s], 16)
                    sp.dma_start(qs[s][h][PART_ROWS:SCORE_ROWS, :], bias(w["q_bias"][bass.ds(head, 1)])).then_inc(stack_loaded[s], 16)
                    for side in range(2):
                        sp.dma_start(ks[s][h][side][0:PART_ROWS, :], parts(k_dram)).then_inc(stack_loaded[s], 16)
                        sp.dma_start(ks[s][h][side][PART_ROWS:STACK, :], bias(w["k_bias"][bass.ds(head, 1), side])).then_inc(stack_loaded[s], 16)

            def maxima(p, s, h):
                sp.wait_ge(turned_read, p * 2 + h + 1)
                for n in range(2):
                    sp.dma_start(qs[s][h][SCORE_ROWS + n:SCORE_ROWS + n + 1, :],
                                 negT[h][n * QT:(n + 1) * QT, :]).then_inc(max_loaded[s][h], 16)

            def store(p, s):
                sp.wait_ge(o_read, p + 2)
                for h in range(2):
                    for half in range(2):
                        at = 32 * (2 * h + half)
                        cols = slice(half * 512, (half + 1) * 512)
                        sp.dma_start(o_dram[bass.ds(p * 2 * HD + h * HD, HD), cols], osb[s][at:at + HD, :]).then_inc(o_stored[s], 16)
                        sp.dma_start(s_dram[bass.ds(p * 2 + h, 1), cols], osb[s][at + HD:at + HD + 1, :]).then_inc(o_stored[s], 16)

            load(0, 0)
            load(1, 1)
            sp.dma_start(fix_t[:].rearrange("p h a q -> p (h a q)"), w["fix_by_key"]).then_inc(tables_loaded, 16)
            load(2, 2)
            for s in range(RING):
                sp.sem_inc(o_stored[s], 16 * 8)
            for h in range(2):
                maxima(0, 0, h)

            def body(p, s, turn, more):
                if more:
                    for h in range(2):
                        maxima(p + 1, (s + 1) % RING, h)

            with sp.Fori(0, (PAIRS - RING) // RING) as j:
                for s in range(RING):
                    p = j * RING + s
                    body(p, s, j, True)
                    sp.wait_ge(pv_done, p * QT + QT + 2)
                    load(p + RING, s)
                    store(p, s)
            for p in range((PAIRS - RING) // RING * RING, PAIRS):
                body(p, p % RING, 0, p < PAIRS - 1)
                if p + RING < PAIRS:
                    sp.wait_ge(pv_done, p * QT + QT + 2)
                    load(p + RING, p % RING)
                store(p, p % RING)
            for s in range(RING):
                sp.wait_ge(o_stored[s], 16 * 8 * (1 + len(range(s, PAIRS, RING))))

        @block.gpsimd
        def _(pool):
            for s in range(RING):
                nc.gpsimd.memset(vs[s][:], 1.0).then_inc(ones_ready, 1)
            pool.wait_ge(ones_ready, RING)

            def stage(p, s):
                for h in range(2):
                    col = (p % (HEADS // 2)) * (2 * HD) + h * HD
                    last = nc.gpsimd.tensor_copy(vs[s][:, h, :, 0:HD], v[:, bass.ds((p // (HEADS // 2)) * QT, QT), bass.ds(col, HD)])
                last.then_inc(v_ready, 1)

            stage(0, 0)

            def gather(t, s):
                pool.wait_ge(rows_used, t + 1)
                for k in range(2):
                    last = nc.gpsimd.tensor_copy(ids[k][s][:], route["dest"][:, bass.ds(t + t // TG * TG + k * TG, 1)])
                last.then_inc(ids_ready, 1)
                pool.wait_ge(ids_ready, t + 1)
                pool.sem_inc(gathers, 1)
                for k in range(2):
                    nc.gpsimd.indirect_dma_start(rows[k][s][:], None, y_dram,
                                                 bass.IndirectOffsetOnAxis(ap=ids[k][s][:, 0:1], axis=0)
                                                 ).then_inc(gathered[k][s], 16)

            def body(p, s, turn, more):
                gather(p, s)
                if more:
                    if not isinstance(p, int) or p > 0:
                        pool.wait_ge(pv_done, p * QT - QT + 2)
                    stage(p + 1, (s + 1) % RING)

            over_pairs(pool, body, peeled=True)

        def units(more):
            return ([(1, u) for u in range(LEAD, 2 * QT)] if more >= 1 else []) + ([(2, u) for u in range(LEAD)] if more >= 2 else [])

        def first_ranges(qb):
            out = []
            for bank in range(2):
                lo, hi, cut = bank * 512, bank * 512 + 512, P * (qb + 1)
                if lo < min(cut, hi):
                    out.append((0, lo, min(cut, hi), bank == qb // 4))
                if max(cut, lo) < hi:
                    out.append((1, max(cut, lo), hi, False))
            return out

        @block.tensor
        def _(pe):
            T = nc.tensor
            pe.wait_ge(first_tables_loaded, 32)
            pe.sem_inc(pv_done, 2)

            def first(p, s, u):
                h, qb = u // QT, u % QT
                at = 2 * (u % 2)
                n = p * 2 * QT + u
                pe.wait_ge(s1_read, reusable(n))
                opened = set()
                for side, a, b, diagonal in first_ranges(qb):
                    bank = at + a // 512
                    last = T.matmul(ps[:, bank, a % 512:a % 512 + b - a], qs[s][h][0:SCORE_ROWS, qb * P:(qb + 1) * P],
                                    ks[s][h][side][0:SCORE_ROWS, a:b], start=bank not in opened, stop=True, skip_group_check=True)
                    opened.add(bank)
                    if diagonal:
                        head = (p % (HEADS // 2)) * 2 + h
                        last = T.matmul(ps[:, bank, qb % 4 * P:qb % 4 * P + P], identb[:], fix[:, bass.ds(head, 1), :],
                                        start=False, stop=True, skip_group_check=True)
                last.then_inc(s1_done, 1)

            def turn_maxima(p, h):
                pe.wait_ge(neg_ready, p * 2 + h + 1)
                if not isinstance(p, int) or p + h > 0:
                    pe.wait_ge(turned_read, p * 2 + h)
                T.transpose(ps_turn, neg[h][:].rearrange("p a q -> p (a q)"), identb[:]).then_inc(turned, 1)

            def second(p, s, kb, h, half):
                u = (kb * 2 + h) * 2 + half
                bank = 4 + u % 2
                n = p * 4 * QT + u
                pe.wait_ge(exp_ready, reusable(n))
                lo, hi, cut = half * 512, half * 512 + 512, kb * P
                keys = slice(kb * P, (kb + 1) * P)
                opened = False
                if max(cut, lo) < hi:
                    a = max(cut, lo)
                    last = T.matmul(ps[:, bank, a - lo:512], ks[s][h][0][0:STACK, keys], qs[s][h][0:STACK, a:hi],
                                    start=True, stop=True, skip_group_check=True)
                    opened = True
                if lo <= cut < hi:
                    head = (p % (HEADS // 2)) * 2 + h
                    for part in range(1 if h == 0 else 3):
                        last = T.matmul(ps[:, bank, cut - lo:cut - lo + P], identb[:], fix_t[:, bass.ds(head, 1), part, :],
                                        start=False, stop=True, skip_group_check=True)
                if lo < min(cut, hi):
                    b = min(cut, hi)
                    last = T.matmul(ps[:, bank, 0:b - lo], ks[s][h][1][0:STACK, keys], qs[s][h][0:STACK, lo:b],
                                    start=not opened, stop=True, skip_group_check=True)
                last.then_inc(s2_done, 1)

            def values(p, s, kb):
                n = p * QT + kb
                pe.wait_ge(exp_ready, n * 4 + 4 + 2)
                if kb == 0:
                    pe.wait_ge(v_ready, p + 1)
                    pe.wait_ge(o_read, p + 1)
                for h in range(2):
                    for half in range(2):
                        c = 2 * h + half
                        last = T.matmul(ps[32 * c:32 * c + 32, 6, :], vs[s][:, h, kb, :], prob[kb % 2][:, c, :],
                                        start=(kb == 0), stop=(kb == QT - 1))
                last.then_inc(pv_done, 1)

            def both(p, s, turn, more):
                ahead = units(more)
                for h in range(2):
                    pe.wait_ge(max_loaded[s][h], turn * 32 + 32)
                for kb in range(QT):
                    for n, (h, half) in enumerate(((0, 0), (0, 1), (1, 0), (1, 1))):
                        second(p, s, kb, h, half)
                        if n % 2 == 0 and kb * 2 + n // 2 < len(ahead):
                            d, u = ahead[kb * 2 + n // 2]
                            slot = (s + d) % RING
                            if u == 0:
                                pe.wait_ge(stack_loaded[slot], (turn + (s + d) // RING) * LOADS + LOADS)
                            first(p + d, slot, u)
                            if (d, u) == (1, QT + 3):
                                turn_maxima(p + 1, 0)
                    if kb == QT - 2 and more:
                        turn_maxima(p + 1, 1)
                    if kb > 0:
                        values(p, s, kb - 1)
                values(p, s, QT - 1)

            pe.wait_ge(stack_loaded[0], LOADS)
            for u in range(2 * QT):
                first(0, 0, u)
            pe.wait_ge(stack_loaded[1], LOADS)
            for h in range(2):
                turn_maxima(0, h)
            for u in range(LEAD):
                first(1, 1, u)
            pe.wait_ge(tables_loaded, 16)
            over_pairs(pe, both)

        @block.scalar
        def _(act):
            act.sem_inc(exp_ready, 2)

            def body(p, s, turn, more):
                for kb in range(QT):
                    for c in range(4):
                        n = p * 4 * QT + kb * 4 + c
                        act.wait_ge(s2_done, n + 1)
                        if c == 0:
                            act.wait_ge(pv_done, reusable(p * QT + kb))
                        nc.scalar.activation(prob[kb % 2][:, c, :], ps[:, 4 + c % 2, :], ACT.Exp).then_inc(exp_ready, 1)

            over_pairs(act, body)

        @block.vector
        def _(dve):
            V = nc.vector
            dve.sem_inc(s1_read, 2)
            dve.sem_inc(o_read, 1)
            dve.sem_inc(rows_used, RING)

            def add_expert_rows(t, s, turn):
                col = t + t // TG * TG
                dve.wait_ge(rows_used, t + RING)
                dve.wait_ge(gathered[0][s], turn * 16 + 16)
                V.scalar_tensor_tensor(part[:], rows[0][s][:], route["gate"][:, bass.ds(col, 1)], X[:, bass.ds(t, 1), :],
                                       ALU.mult, ALU.add).then_inc(first_added, 1)
                dve.wait_ge(gathered[1][s], turn * 16 + 16)
                dve.wait_ge(first_added, t + 1)
                V.scalar_tensor_tensor(X[:, bass.ds(t, 1), :], rows[1][s][:], route["gate"][:, bass.ds(col + TG, 1)], part[:],
                                       ALU.mult, ALU.add).then_inc(rows_used, 1)

            def maximum(p, u):
                n = p * 2 * QT + u
                h = u // QT
                dve.wait_ge(s1_done, n + 1)
                V.reduce_max(top[h][:, u % QT:u % QT + 1], ps[:, 2 * (u % 2):2 * (u % 2) + 2, :].rearrange("p a q -> p (a q)"),
                             AX.X).then_inc(s1_read, 1)

            def negate(p, h):
                dve.wait_ge(s1_read, p * 2 * QT + (h + 1) * QT + 2)
                V.tensor_scalar(neg[h][:, 0, :], top[h][:], -1.0, None, ALU.mult).then_inc(high_ready, 1)
                dve.wait_ge(high_ready, p * 2 + h + 1)
                V.scalar_tensor_tensor(neg[h][:, 1, :], top[h][:], -1.0, neg[h][:, 0, :], ALU.mult, ALU.subtract).then_inc(neg_ready, 1)

            def keep_turned(p, h):
                dve.wait_ge(turned, p * 2 + h + 1)
                V.tensor_copy(negT[h][:], ps_turn).then_inc(turned_read, 1)

            for u in range(2 * QT):
                maximum(0, u)
                if u % QT == QT - 1:
                    negate(0, u // QT)
            for h in range(2):
                keep_turned(0, h)
            for u in range(LEAD):
                maximum(1, u)

            def body(p, s, turn, more):
                for d, u in units(more):
                    maximum(p + d, u)
                    if (d, u) == (1, QT - 1):
                        negate(p + 1, 0)
                    if (d, u) == (1, QT + 3):
                        dve.wait_ge(max_loaded[s][0], turn * 32 + 32)
                        keep_turned(p + 1, 0)
                    if (d, u) == (1, 2 * QT - 1):
                        negate(p + 1, 1)
                    if (d, u) == ((2, 0) if more == 2 else (1, 2 * QT - 1)):
                        dve.wait_ge(max_loaded[s][1], turn * 32 + 32)
                        keep_turned(p + 1, 1)
                add_expert_rows(p, s, turn)
                dve.wait_ge(pv_done, p * QT + QT + 2)
                dve.wait_ge(o_stored[s], turn * 128 + 128)
                V.tensor_copy(osb[s][:], ps[:, 6, :]).then_inc(o_read, 1)

            over_pairs(dve, body)


def project_out(nc, signals, X, o_dram, s_dram, r_dram, w, out):
    N = 512
    GROUPS = TOK // N
    HPT = HEADS // HC
    with phase(nc, signals) as stack:
        m = stack.memory
        wo = m.sb("w_out1", [P, HC, D])
        sums = m.sb("o_sums", [P, N])
        inverse = m.sb("o_inverse", [P, N])
        raw = [m.sb(f"o_raw{s}", [P, HC, N]) for s in range(2)]
        inv = [m.sb(f"o_inverse_rows{s}", [P, HC, N]) for s in range(2)]
        o = [m.sb(f"o_t{s}", [P, HC, N]) for s in range(2)]
        w_loaded, sums_loaded, inverse_ready, inverse_stored = (
            m.sem("w_out1_loaded"), m.sem("sums_loaded"), m.sem("inverse_ready"), m.sem("inverse_stored"))
        o_loaded, inv_loaded = m.sems("o_loaded", 2), m.sems("inv_loaded", 2)
        o_ready, y_done, y_read, out_stored = m.sem("o_ready"), m.sem("out1_done"), m.sem("out1_read"), m.sem("out_stored")
        ps = stack.enter_context(nc.psum_tensor("ps_out1", [P, 8, 512], F32))
        block = stack.block.enter_context(nc.Block())

        @block.sync
        def _(sp):
            halves = lambda dram: dram.rearrange("h (a t) -> (h a) t", t=N)
            sp.dma_start(sums[:], halves(s_dram)).then_inc(sums_loaded, 16)
            sp.dma_start(wo[:], w).then_inc(w_loaded, 16)
            sp.wait_ge(inverse_ready, 1)
            sp.dma_start(halves(r_dram), inverse[:]).then_inc(inverse_stored, 16)
            sp.wait_ge(inverse_stored, 16)

            def load(g, s, turn):
                sp.wait_ge(o_ready, reusable(g))
                cols = slice(s * N, (s + 1) * N)
                sp.dma_start(raw[s][:], o_dram[bass.ds(turn * D, D), cols].rearrange("(c p) t -> p c t", p=P)).then_inc(o_loaded[s], 16)
                for c in range(HC):
                    src = r_dram[bass.ds(turn * HEADS + c * HPT, HPT), cols].unsqueeze(1).to_broadcast([HPT, HD, N])
                    sp.dma_start(inv[s][:, c, :], src).then_inc(inv_loaded[s], 16)

            def store(g, s, turn):
                sp.wait_ge(y_read, made(g))
                sp.dma_start(out[:, bass.ts(g, 4), :], X[:, bass.ts(g, 4), :]).then_inc(out_stored, 16)

            pipelined(sp, GROUPS, load, store, ahead=2)
            sp.wait_ge(out_stored, GROUPS * 16)

        @block.vector
        def _(dve):
            V = nc.vector
            dve.sem_inc(o_ready, 2)
            dve.sem_inc(y_read, 2)
            dve.wait_ge(sums_loaded, 16)
            V.reciprocal(inverse[:], sums[:]).then_inc(inverse_ready, 1)

            def divide(g, s, turn):
                dve.wait_ge(o_loaded[s], turn * 16 + 16)
                dve.wait_ge(inv_loaded[s], turn * 32 + 32)
                dve.wait_ge(y_done, reusable(g))
                V.tensor_tensor(o[s][:], raw[s][:], inv[s][:], ALU.mult).then_inc(o_ready, 1)

            def add(g, s, turn):
                dve.wait_ge(y_done, made(g))
                for t in range(4):
                    src = ps[:, 2 * s + t // 2, (t % 2) * D:(t % 2) * D + D]
                    last = V.tensor_tensor(X[:, g * 4 + t, :], src, X[:, g * 4 + t, :], ALU.add)
                last.then_inc(y_read, 1)

            software_pipelined(dve, GROUPS, divide, add)

        @block.tensor
        def _(pe):
            pe.wait_ge(w_loaded, 16)
            pe.sem_inc(y_done, 2)

            def out_rows(g, s, turn):
                pe.wait_ge(o_ready, made(g))
                pe.wait_ge(y_read, reusable(g))
                for t in range(4):
                    for c in range(HC):
                        last = nc.tensor.matmul(ps[:, 2 * s + t // 2, (t % 2) * D:(t % 2) * D + D],
                                                o[s][:, c, t * P:(t + 1) * P], wo[:, c, :], start=(c == 0), stop=(c == HC - 1))
                last.then_inc(y_done, 1)

            by_twos(pe, GROUPS, out_rows)


def capacity_start(nc, signals, m, w, route, xn_dram):
    FC = F1 // P
    PB = 2 * SLOTS1 // P
    raw_i, raw_o = m.sb("wi_raw", [P, HC, F1]), m.sb("wo_raw", [P, FC, D])
    ids = m.sb("slot_tokens", [P, PB], I32)
    xg = [m.sb(f"slot_rows{n}", [P, D]) for n in range(PB)]
    wi_loaded, wo_loaded, wi_low, wo_low = (
        signals.sem("wi_loaded"), signals.sem("wo_loaded"), signals.sem("wi_low"), signals.sem("wo_low"))
    ids_ready, gathers, gathered = signals.sem("slot_ids"), signals.sem("slot_gathers"), signals.gather_sems("slots_gathered", PB)
    xt_done = signals.sem("slot_xt_done")

    def load(sp, e):
        if not isinstance(e, int) or e > 0:
            sp.wait_ge(wi_low, e + 1)
        sp.dma_start(raw_i[:], w["i"][:, bass.ds(e, 1), :, :].rearrange("p o c n -> p (o c) n")).then_inc(wi_loaded, 16)
        if not isinstance(e, int) or e > 0:
            sp.wait_ge(wo_low, e + 1)
        sp.dma_start(raw_o[:], w["o"][:, bass.ds(e, 1), :, :].rearrange("p o c n -> p (o c) n")).then_inc(wo_loaded, 16)

    def gather(pool, j):
        if not isinstance(j, int) or j > 0:
            pool.wait_ge(xt_done, j * PB + 1)
        nc.gpsimd.tensor_copy(ids[:], route["token"][:, bass.ts(j, PB)]).then_inc(ids_ready, 1)
        pool.wait_ge(ids_ready, j + 1)
        pool.sem_inc(gathers, 1)
        for n in range(PB):
            nc.gpsimd.indirect_dma_start(xg[n][:], None, xn_dram, bass.IndirectOffsetOnAxis(ap=ids[:, n:n + 1], axis=0)
                                         ).then_inc(gathered[n], 16)

    return {"load": load, "gather": gather, "raw": (raw_i, raw_o), "rows": xg,
            "sems": (wi_loaded, wo_loaded, wi_low, wo_low, gathered, xt_done)}


def capacity_experts(nc, signals, X, start, y_dram, b_out, const):
    FC = F1 // P
    PB = 2 * SLOTS1 // P
    CH = [(0, 0), (P, 0), (SLOTS1 - P, 3 * P - SLOTS1)]
    H_BANKS = (2, 3, 6, 7)
    with phase(nc, signals) as stack:
        m = stack.memory
        cut = lambda name, shape: {part: m.sb(f"{name}_{part}", shape, F22) for part in ("high", "low")}
        (raw_i, raw_o), xg = start["raw"], start["rows"]
        wi_loaded, wo_loaded, wi_low, wo_low, gathered, xt_done = start["sems"]
        wi = [cut(f"wi{s}", [P, HC, F1]) for s in range(2)]
        wo = [cut(f"wo{s}", [P, FC, D]) for s in range(2)]
        xt = cut("slot_rows_t", [P, HC, 2 * SLOTS1])
        h = cut("relu", [P, FC, SLOTS1])
        yr = [m.sb(f"slot_y{s}", [P, len(CH), D]) for s in range(2)]
        bo, bias_loaded = m.sb("b_out1", [P, D]), m.sem("b_out1_loaded")
        wi_high, wo_high = m.sem("wi_high"), m.sem("wo_high")
        xt_high, xt_low = m.sem("slot_xt_high"), m.sem("slot_xt_low")
        h_done, h_high, h_low = m.sem("m1_h_done"), m.sem("m1_h_high"), m.sem("m1_h_low")
        y_done, y_ready, y_stored = m.sem("m1_y_done"), m.sem("m1_y_ready"), m.sems("m1_y_stored", 2)
        ps = stack.enter_context(nc.psum_tensor("ps_moe1", [P, 8, 512], F32))
        block = stack.block.enter_context(nc.Block())
        ps_xt = [ps[:, n, 0:D].rearrange("p (c t) -> p c t", c=HC) for n in range(2)]
        ps_h = lambda f: ps[:, H_BANKS[f % len(H_BANKS)], 0:SLOTS1]
        ps_y = lambda n: ps[:, 4 + n // 2, n % 2 * D:n % 2 * D + D]

        def over_pairs(engine, body):
            with engine.Fori(0, E // 2 - 1) as j:
                body(j, True)
            body(E // 2 - 1, False)

        @block.gpsimd
        def _(pool):
            NA = NT // (E // 2)

            def add_bias(j):
                for t in range(NA):
                    nc.gpsimd.tensor_tensor(X[:, j * NA + t, :], X[:, j * NA + t, :], bo[:], ALU.add)

            pool.wait_ge(bias_loaded, 16)
            add_bias(0)
            with pool.Fori(1, E // 2) as j:
                start["gather"](pool, j)
                add_bias(j)

        @block.tensor
        def _(pe):
            pe.sem_inc(xt_done, 1)
            pe.sem_inc(h_done, 2 * FC)
            pe.sem_inc(y_done, 2)

            def turn_rows(j):
                for n in range(PB):
                    pe.wait_ge(gathered[n], j * 16 + 16)
                    pe.wait_ge(xt_low, j * PB + (2 if n == 0 else n + 1))
                    for c in range(HC):
                        last = nc.tensor.transpose(ps_xt[n % 2][:, c, :], xg[n][:, c * P:(c + 1) * P], const["ident"])
                    last.then_inc(xt_done, 1)

            def up(j, s):
                e = j * 2 + s
                pe.wait_ge(xt_low, j * PB + PB + 2)
                pe.wait_ge(wi_low, e + 2)
                for f in range(FC):
                    pe.wait_ge(h_low, e * FC + f + 1)
                    for n, (a, b) in enumerate(PRODUCTS):
                        for k in range(HC):
                            last = nc.tensor.matmul(ps_h(f), wi[s][a][:, k, f * P:(f + 1) * P], xt[b][:, k, s * SLOTS1:(s + 1) * SLOTS1],
                                                    start=(n == 0 and k == 0), stop=(n == len(PRODUCTS) - 1 and k == HC - 1))
                    last.then_inc(h_done, 1)

            def down(j, s):
                e = j * 2 + s
                pe.wait_ge(wo_low, e + 2)
                pe.wait_ge(y_ready, e + 1)
                pe.wait_ge(h_low, e * FC + FC + 4)
                for c, (first, _) in enumerate(CH):
                    for f in range(FC):
                        for n, (a, b) in enumerate(PRODUCTS):
                            last = nc.tensor.matmul(ps_y(c), h[a][:, f, first:first + P], wo[s][b][:, f, :],
                                                    start=(f == 0 and n == 0), stop=(f == FC - 1 and n == len(PRODUCTS) - 1))
                last.then_inc(y_done, 1)

            def pair(j, more):
                up(j, 0)
                down(j, 0)
                up(j, 1)
                if more:
                    turn_rows(j + 1)
                down(j, 1)

            turn_rows(0)
            over_pairs(pe, pair)

        @block.scalar
        def _(act):
            def high_rows(j):
                act.wait_ge(h_done, j * 2 * FC + 2 * FC)
                for n in range(PB):
                    act.wait_ge(xt_done, j * PB + n + 2)
                    nc.scalar.copy(xt["high"][:, :, n * P:(n + 1) * P], ps_xt[n % 2]).then_inc(xt_high, 1)

            def high_weights(e, s):
                act.wait_ge(wi_loaded, e * 16 + 16)
                act.wait_ge(h_done, e * FC + FC)
                nc.scalar.copy(wi[s]["high"][:], raw_i[:]).then_inc(wi_high, 1)
                act.wait_ge(wo_loaded, e * 16 + 16)
                act.wait_ge(y_done, reusable(e))
                nc.scalar.copy(wo[s]["high"][:], raw_o[:]).then_inc(wo_high, 1)

            def relu(j, s):
                e = j * 2 + s
                act.wait_ge(y_done, e + 2)
                for f in range(FC):
                    act.wait_ge(h_done, e * FC + f + (1 + 2 * FC))
                    nc.scalar.activation(h["high"][:, f, :], ps_h(f), ACT.Relu).then_inc(h_high, 1)

            def pair(j, more):
                relu(j, 0)
                high_weights(j * 2 + 1, 1)
                relu(j, 1)
                if more:
                    high_rows(j + 1)
                    high_weights(j * 2 + 2, 0)

            high_rows(0)
            high_weights(0, 0)
            over_pairs(act, pair)

        @block.vector
        def _(dve):
            V = nc.vector
            dve.sem_inc(h_low, 4)
            dve.sem_inc(xt_low, 2)
            dve.sem_inc(wi_low, 1)
            dve.sem_inc(wo_low, 1)
            dve.sem_inc(y_ready, 1)

            def low_rows(j):
                dve.wait_ge(h_done, j * 2 * FC + 2 * FC)
                for n in range(PB):
                    dve.wait_ge(xt_high, j * PB + n + 1)
                    V.tensor_tensor(xt["low"][:, :, n * P:(n + 1) * P], ps_xt[n % 2], xt["high"][:, :, n * P:(n + 1) * P],
                                    ALU.subtract).then_inc(xt_low, 1)

            def low_weights(e, s):
                dve.wait_ge(wi_high, e + 1)
                dve.wait_ge(h_done, e * FC + FC)
                V.tensor_tensor(wi[s]["low"][:], raw_i[:], wi[s]["high"][:], ALU.subtract).then_inc(wi_low, 1)
                dve.wait_ge(wo_high, e + 1)
                dve.wait_ge(y_done, reusable(e))
                V.tensor_tensor(wo[s]["low"][:], raw_o[:], wo[s]["high"][:], ALU.subtract).then_inc(wo_low, 1)

            def low_hidden(j, s):
                e = j * 2 + s
                dve.wait_ge(y_done, e + 2)
                for f in range(FC):
                    dve.wait_ge(h_high, e * FC + f + 1)
                    V.scalar_tensor_tensor(h["low"][:, f, :], ps_h(f), 0.0, h["high"][:, f, :], ALU.max, ALU.subtract).then_inc(h_low, 1)

            def rows(j, s):
                dve.wait_ge(y_done, made(j * 2 + s))
                dve.wait_ge(y_stored[s], j * 48 + 48)
                for c in range(len(CH)):
                    last = V.tensor_copy(yr[s][:, c, :], ps_y(c))
                last.then_inc(y_ready, 1)

            def pair(j, more):
                low_hidden(j, 0)
                low_weights(j * 2 + 1, 1)
                rows(j, 0)
                low_hidden(j, 1)
                if more:
                    low_rows(j + 1)
                    low_weights(j * 2 + 2, 0)
                rows(j, 1)

            low_rows(0)
            low_weights(0, 0)
            over_pairs(dve, pair)

        @block.sync
        def _(sp):
            sp.dma_start(bo[:], b_out.to_broadcast([P, D])).then_inc(bias_loaded, 16)
            for s in range(2):
                sp.sem_inc(y_stored[s], 48)

            def store(e, s, turn):
                sp.wait_ge(y_ready, e + 2)
                for c, (first, skip) in enumerate(CH):
                    sp.dma_start(y_dram[bass.ds(e * SLOTS1 + (first + skip), P - skip), :], yr[s][skip:P, c, :]).then_inc(y_stored[s], 16)

            with sp.Fori(0, E // 2 - 1) as j:
                for s in range(2):
                    start["load"](sp, j * 2 + (s + 1))
                    store(j * 2 + s, s, j)
            start["load"](sp, E - 1)
            store(E - 2, 0, 0)
            store(E - 1, 1, 0)
            for s in range(2):
                sp.wait_ge(y_stored[s], 48 * (E // 2 + 1))


def program(nc, a, out):
    with ExitStack() as stack:
        m = Memory(nc, stack)
        X = m.sb("x", [P, NT, D])
        stats = m.sb("stats", [P, NT, 6])
        const, table_loads = constant_tables(nc, m, a)
        route = {
            "gate": m.sb("gate", [P, 2 * NT]),
            "dest": m.sb("dest", [P, 2 * NT], I32),
            "token": m.sb("token", [P, BLOCKS0], I32),
            "expert": m.sb("expert", [P, BLOCKS0], I32),
        }
        xn_dram = nc.dram_tensor("xn_rows_dram", (TOK, D), F32, kind="Internal").ap()
        y_dram = nc.dram_tensor("y_rows_dram", (BLOCKS0 * P, D), F32, kind="Internal").ap()
        tiles = lambda ap: ap.rearrange("(i p) d -> p i d", p=P)
        chunks = lambda ap: ap.rearrange("(c p) n -> p c n", p=P)
        by_expert = lambda ap: ap.rearrange("e (c p) n -> p e c n", p=P)
        with Signals(nc, m) as signals:
            with ExitStack() as first:
                xnT = Memory(nc, first).sb("xn_t", [P, HC, TOK])
                with ExitStack() as experts:
                    me = Memory(nc, experts)
                    ew = {"wg": me.sb("wg", [P, E, HC, I0]), "wu": me.sb("wu", [P, E, HC, I0]),
                          "wd": me.sb("wd", [P, E, I0 // P, D]), "loaded": m.sems("expert_w_loaded", 3)}
                    ew["loads"] = [(ew[n], by_expert(a[n])) for n in ("wg", "wu", "wd")]
                    norm_and_route(nc, signals, 0, tiles(a["x"]), X, stats, xnT, xn_dram, chunks(a["wr0"]), const["rb0"], const, route,
                                   tables=table_loads)
                    scan_branch(nc, signals, X, xnT, {"in": chunks(a["w_in"]), "out": chunks(a["w_out0"]), "b_z": a["b_z"],
                                             "bcd_alog": a["bcd_alog"], "b_out": a["b_out0"]}, const, ew)
                    routed_experts(nc, signals, ew, route, xn_dram, y_dram, const)
                shared_expert(nc, signals, X, xnT, {"g": chunks(a["wg_s"]), "u": chunks(a["wu_s"]), "d": chunks(a["wd_s"])}, route, y_dram, stats)
        q_dram = nc.dram_tensor("q_dram", (BATCH * HEADS, HD, len(Q_PARTS), SEQ), BF16, kind="Internal").ap()
        k_dram = nc.dram_tensor("k_dram", (BATCH * HEADS, HD, len(K_PARTS), SEQ), BF16, kind="Internal").ap()
        o_dram = nc.dram_tensor("o_dram", (BATCH * D, SEQ), F32, kind="Internal").ap()
        s_dram = nc.dram_tensor("s_dram", (BATCH * HEADS, SEQ), F32, kind="Internal").ap()
        r_dram = nc.dram_tensor("r_dram", (BATCH * HEADS, SEQ), F32, kind="Internal").ap()
        with Signals(nc, m, clear=False) as signals:
            with ExitStack() as second:
                mv = Memory(nc, second)
                v = mv.sb("v", [P, NT, D])
                start = capacity_start(nc, signals, mv, {"i": by_expert(a["wi"]), "o": by_expert(a["wo"])}, route, xn_dram)
                with ExitStack() as inner:
                    mi = Memory(nc, inner)
                    xnT = mi.sb("xn_t1", [P, HC, TOK])
                    wv, bv = mi.sb("w_v", [P, HC, D]), mi.sb("b_v", [P, D])
                    norm_and_route(nc, signals, 1, None, X, stats, xnT, xn_dram, chunks(a["wr1"]), None, const, route,
                                   v_out={"w": wv, "b": bv, "v": v, "loads": [(wv[:], chunks(a["w_qkv"])[:, :, 2 * D:3 * D]),
                                                                              (bv[:], a["b_v"].to_broadcast([P, D]))]})
                    project_qk(nc, signals, X, xnT, {"qk": chunks(a["w_qkv"])[:, :, 0:2 * D], "b_qk": a["b_qk"]},
                               q_dram, k_dram, start)
                capacity_experts(nc, signals, X, start, y_dram, a["b_out1"], const)
                attention(nc, signals, X, v, q_dram, k_dram, o_dram, s_dram, route, y_dram, a, const)
            project_out(nc, signals, X, o_dram, s_dram, r_dram, chunks(a["w_out1"]), tiles(out))


def constant_tables(nc, m, a):
    const = {}
    names = ("ident", "expert_no", "go_on0", "go_on1", "rows_before", "one8", "count_up", "part_no", "tile_no0",
             "tile_no1", "slot_base", "batch_of")
    tri, ones, rb = m.sb("tri", [P, P], BF16), m.sb("ones", [P, P], BF16), m.sb("rb", [P, E])
    const["tri"], const["ones"], const["rb0"] = tri[:], ones[:], rb[:]
    for n in names:
        const[n] = m.sb(n, list(a[n].shape))[:]
    loads = {"first": [(const["ident"], a["ident"]), (rb[:], a["rb"].to_broadcast([P, E]))],
             "rest": [(const[n], a[n]) for n in names[1:] + ("tri", "ones")]}
    const["expert_no"] = const["expert_no"].rearrange("p (t e) -> p t e", e=E)
    return const, loads


def constant_arrays():
    import numpy as np
    f, bf = np.float32, mybir.dt.np(BF16)
    rows = lambda v: np.ascontiguousarray(np.broadcast_to(np.asarray(v, f).reshape(1, -1), (P, np.asarray(v).size)))
    p = np.arange(P)
    c = {
        "ident": np.eye(P, dtype=f),
        "tri": (p[:, None] < p[None, :]).astype(bf),
        "ones": np.ones((P, P), bf),
        "expert_no": rows(np.tile(np.arange(E), NT)),
        "rows_before": rows(P * np.arange(NT)),
        "one8": rows(np.ones(E)),
        "count_up": rows(np.arange(P)),
        "part_no": p.astype(f).reshape(P, 1),
        "batch_of": (p[:, None] // 32 == np.arange(BATCH)[None, :]).astype(f),
        "slot_base": rows(np.broadcast_to((np.arange(E)[None, :, None] * SLOTS1 + np.arange(G1)[:, None, None] * CAP),
                                          (G1, E, 2 * NT // G1)).reshape(-1)),
    }
    for L, g in ((0, 1), (1, G1)):
        tg = NT // g
        go = np.ones((g * E, 2 * tg))
        go[:, 0] = 0
        c[f"go_on{L}"] = rows(go.reshape(-1))
        c[f"tile_no{L}"] = rows(np.broadcast_to(np.arange(NT).reshape(g, 1, tg), (g, 2, tg)).reshape(-1))
    slope = np.asarray([(2 ** -0.5) ** i for i in range(HEADS)], f)
    cut = lambda v: (lambda h: (h, *(lambda r: (r.astype(bf), (r - r.astype(bf).astype(f)).astype(bf)))((v - h.astype(f)).astype(f))))(v.astype(bf))
    parts = np.stack([x.astype(f) for x in cut(slope)], 1)
    pos = np.arange(SEQ)
    coarse, fine = (pos // P * P).astype(f), (pos % P).astype(f)
    each = np.repeat(parts, 2, 1)
    both = np.tile(np.stack([coarse, fine]), (3, 1))
    q = np.concatenate([np.broadcast_to(both, (HEADS, 6, SEQ)), np.broadcast_to(each[:, :, None], (HEADS, 6, SEQ))], 1)
    k = np.concatenate([np.broadcast_to(-each[:, :, None], (HEADS, 6, SEQ)), np.broadcast_to(both, (HEADS, 6, SEQ))], 1)
    ones = np.ones((HEADS, 2, SEQ), f)
    c["q_bias"] = q.astype(bf)
    c["k_bias"] = np.stack([np.concatenate([k, ones], 1), np.concatenate([-k, ones], 1)], 1).astype(bf)
    ahead = -2 * np.maximum(p[:, None] - p[None, :], 0).astype(f)
    fix = np.stack([x.astype(f) for x in cut(slope[:, None, None] * ahead)], 1)
    c["fix_by_key"] = np.ascontiguousarray(fix.transpose(2, 0, 1, 3)).reshape(P, -1).astype(bf)
    c["fix_by_query"] = np.ascontiguousarray(fix[:, 0].transpose(2, 0, 1)).reshape(P, -1).astype(bf)
    c["ident_bf"] = np.eye(P).astype(bf)
    return c


def kernel(**inputs):
    import numpy as np
    import concourse.bacc as bacc
    from concourse.bass_utils import run_bass_kernel_spmd as run

    t = {k: np.asarray(v) for k, v in inputs.items()}
    flat = lambda v: np.ascontiguousarray(v)
    turned = lambda v: np.ascontiguousarray(np.swapaxes(v, -1, -2))
    b_in = t["L0_attn_b_in"]
    arrays = {
        "x": t["L0_attn_x"].reshape(TOK, D),
        "w_in": t["L0_attn_W_in"],
        "w_out0": t["L0_attn_W_out"],
        "b_z": flat(b_in[D:2 * D].reshape(HC, P).T),
        "bcd_alog": flat(np.concatenate([b_in[2 * D:].reshape(3, N_STATE), t["L0_attn_A_log"].reshape(1, N_STATE)]).T),
        "b_out0": t["L0_attn_b_out"].reshape(1, D),
        "wg_s": turned(t["L0_ffn_Wg_s"]), "wu_s": turned(t["L0_ffn_Wu_s"]), "wd_s": turned(t["L0_ffn_Wd_s"]),
        "wg": turned(t["L0_ffn_Wg"]), "wu": turned(t["L0_ffn_Wu"]), "wd": turned(t["L0_ffn_Wd"]),
        "wr0": turned(t["L0_ffn_Wr"]),
        "rb": t["L0_ffn_rb"].reshape(1, E),
        "w_qkv": t["L1_attn_Wqkv"],
        "b_qk": flat(t["L1_attn_bqkv"][:2 * D].reshape(2 * HC, P).T),
        "b_v": t["L1_attn_bqkv"][2 * D:].reshape(1, D),
        "w_out1": t["L1_attn_Wout"],
        "b_out1": t["L1_attn_bout"].reshape(1, D),
        "wr1": t["L1_ffn_w_router"],
        "wi": t["L1_ffn_wi"],
        "wo": t["L1_ffn_wo"],
    }
    arrays.update(constant_arrays())
    nc = bacc.Bacc("TRN2", target_bir_lowering=False, num_devices=1)
    a = {k: nc.dram_tensor("in_" + k, v.shape, mybir.dt.from_np(v.dtype), kind="ExternalInput").ap() for k, v in arrays.items()}
    out = nc.dram_tensor("out", (TOK, D), F32, kind="ExternalOutput").ap()
    program(nc, a, out)
    result = run(nc, [{"in_" + k: v for k, v in arrays.items()}], core_ids=[0])
    return result.results[0]["out"].reshape(BATCH, SEQ, D)
```
